# Optimizing a Trainium2 kernel written in Bass

```python
import numpy as np
import jax
import jax.numpy as jnp

def _softmax(x, axis=-1):
    return jax.nn.softmax(x, axis=axis)

def _gelu(x):
    return jax.nn.gelu(x, approximate=True)

def _silu(x):
    return jax.nn.silu(x)

def _sigmoid(x):
    return jax.nn.sigmoid(x)

def _layernorm(x, axis=-1, eps=1e-05):
    m = jnp.mean(x, axis=axis, keepdims=True)
    v = jnp.var(x, axis=axis, keepdims=True)
    return (x - m) / jnp.sqrt(v + eps)

def _scatter_add(tgt, idx, src, axis=0):
    return tgt.at[idx].add(src)

def _segment_sum(src, seg, n):
    return jax.ops.segment_sum(src, seg, n)
kernel_name = 'mk_early_fusion_d2_tok_img1024_r4_7502e7'

def setup_inputs(seed: int=0):
    np.random.seed(seed)
    _w = jnp.asarray

    def _rec_inputs():
        import jax
        import jax.numpy as jnp
        _rk = jax.random.key(seed)
        x = -0.000348323 + 0.999952 * jax.random.normal(jax.random.fold_in(_rk, 1), (32, 3, 224, 224), jnp.float32)
        txt = -0.000563189 + 0.999639 * jax.random.normal(jax.random.fold_in(_rk, 2), (32, 77, 256), jnp.float32)
        return (x, txt)
    x, txt = _rec_inputs()

    def _L0_tok_setup():
        import jax, jax.numpy as jnp
        import numpy as np
        from jax import lax
        PATCH = 16
        key = jax.random.key(seed)
        k1, k2 = jax.random.split(key)
        B, C, IMG, HID = (32, 3, 96, 256)
        inputs = jax.random.normal(k1, (B, C, IMG, IMG), dtype=jnp.float32)
        flat = C * PATCH * PATCH
        W = jax.random.normal(k2, (flat, HID), dtype=jnp.float32) / np.sqrt(flat)
        return {'inputs': inputs, 'W': W}
    _L0_tok_all = _L0_tok_setup()
    _L0_tok_in = {k: v for k, v in _L0_tok_all.items() if k in ('W',)}
    del _L0_tok_all

    def _L0_attn_setup():
        import jax, jax.numpy as jnp
        import numpy as np
        B, S, HID = (2, 512, 256)
        NH, NKV, D = (16, 4, 64)
        SCALE = 1.0 / np.sqrt(D).astype(np.float32)
        SOFTCAP = 30.0
        WINDOW = 256
        NEG = -1e+30
        key = jax.random.key(seed)
        kx, kq, kk, kv, ko = jax.random.split(key, 5)
        std = 0.02
        return {'x': jax.random.normal(kx, (B, S, HID), jnp.float32), 'Wq': jax.random.normal(kq, (NH * D, HID), jnp.float32) * std, 'Wk': jax.random.normal(kk, (NKV * D, HID), jnp.float32) * std, 'Wv': jax.random.normal(kv, (NKV * D, HID), jnp.float32) * std, 'Wo': jax.random.normal(ko, (HID, NH * D), jnp.float32) * std}
    _L0_attn_all = _L0_attn_setup()
    _L0_attn_in = {k: v for k, v in _L0_attn_all.items() if k in ('Wq', 'Wk', 'Wv', 'Wo')}
    del _L0_attn_all

    def _L0_ffn_setup():
        import jax, jax.numpy as jnp
        import numpy as np
        D_MODEL, D_FF, RANK = (256, 1024, 64)
        B, S = (4, 1024)
        key = jax.random.key(seed)
        ks = jax.random.split(key, 7)
        return {'x': jax.random.normal(ks[0], (B, S, D_MODEL), dtype=jnp.float32), 'U1': jax.random.normal(ks[1], (D_MODEL, RANK), dtype=jnp.float32) * 0.02, 'V1': jax.random.normal(ks[2], (RANK, D_FF), dtype=jnp.float32) * 0.02, 'b1': jnp.zeros((D_FF,), dtype=jnp.float32), 'U2': jax.random.normal(ks[3], (D_FF, RANK), dtype=jnp.float32) * 0.02, 'V2': jax.random.normal(ks[4], (RANK, D_MODEL), dtype=jnp.float32) * 0.02, 'b2': jnp.zeros((D_MODEL,), dtype=jnp.float32)}
    _L0_ffn_all = _L0_ffn_setup()
    _L0_ffn_in = {k: v for k, v in _L0_ffn_all.items() if k in ('U1', 'V1', 'b1', 'U2', 'V2', 'b2')}
    del _L0_ffn_all

    def _L1_attn_setup():
        import math
        import jax, jax.numpy as jnp
        import numpy as np
        D_MODEL = 256
        N_HEADS = 16
        HEAD_DIM = D_MODEL // N_HEADS
        B, L = (2, 512)
        EPS = 1e-05

        def _gammas():
            return jnp.array([1.0 - 2.0 ** (-5 - math.floor(8 * i / N_HEADS)) for i in range(N_HEADS)], dtype=jnp.float32)

        def _decay_mask(seq_len):
            idx = jnp.arange(seq_len)
            diff = idx[:, None] - idx[None, :]
            g = _gammas()[:, None, None]
            pow_ = g ** jnp.maximum(diff, 0).astype(jnp.float32)
            return jnp.where(diff >= 0, pow_, 0.0)
        key = jax.random.key(seed)
        ks = jax.random.split(key, 7)
        s = 1.0 / math.sqrt(D_MODEL)
        x = jax.random.normal(ks[0], (B, L, D_MODEL), dtype=jnp.float32)
        Wq = jax.random.normal(ks[1], (N_HEADS, D_MODEL, HEAD_DIM), dtype=jnp.float32) * s
        Wk = jax.random.normal(ks[2], (N_HEADS, D_MODEL, HEAD_DIM), dtype=jnp.float32) * s
        Wv = jax.random.normal(ks[3], (N_HEADS, D_MODEL, HEAD_DIM), dtype=jnp.float32) * s
        gn_weight = jnp.ones((D_MODEL,), dtype=jnp.float32)
        gn_bias = jnp.zeros((D_MODEL,), dtype=jnp.float32)
        Wout = jax.random.normal(ks[4], (D_MODEL, D_MODEL), dtype=jnp.float32) * s
        return {'x': x, 'Wq': Wq, 'Wk': Wk, 'Wv': Wv, 'gn_weight': gn_weight, 'gn_bias': gn_bias, 'Wout': Wout}
    _L1_attn_all = _L1_attn_setup()
    _L1_attn_in = {k: v for k, v in _L1_attn_all.items() if k in ('Wq', 'Wk', 'Wv', 'gn_weight', 'gn_bias', 'Wout')}
    del _L1_attn_all

    def _L1_ffn_setup():
        import jax, jax.numpy as jnp
        import numpy as np
        B, S, D, E, H, O = (4, 512, 256, 8, 512, 256)
        key = jax.random.key(seed)
        ks = jax.random.split(key, 8)
        sd = 1.0 / np.sqrt(D)
        sh = 1.0 / np.sqrt(H)
        return {'x': jax.random.normal(ks[0], (B, S, D), dtype=jnp.float32), 'gate_w': jax.random.uniform(ks[1], (D, E), jnp.float32, -sd, sd), 'gate_b': jax.random.uniform(ks[2], (E,), jnp.float32, -sd, sd), 'expert_w': jax.random.uniform(ks[3], (E, D, H), jnp.float32, -sd, sd), 'expert_b': jax.random.uniform(ks[4], (E, H), jnp.float32, -sd, sd), 'out_w': jax.random.uniform(ks[5], (H, O), jnp.float32, -sh, sh), 'out_b': jax.random.uniform(ks[6], (O,), jnp.float32, -sh, sh)}
    _L1_ffn_all = _L1_ffn_setup()
    _L1_ffn_in = {k: v for k, v in _L1_ffn_all.items() if k in ('gate_w', 'gate_b', 'expert_w', 'expert_b', 'out_w', 'out_b')}
    del _L1_ffn_all
    return {'x': x, 'txt': txt, 'L0_tok_W': _L0_tok_in['W'], 'L0_attn_Wq': _L0_attn_in['Wq'], 'L0_attn_Wk': _L0_attn_in['Wk'], 'L0_attn_Wv': _L0_attn_in['Wv'], 'L0_attn_Wo': _L0_attn_in['Wo'], 'L0_ffn_U1': _L0_ffn_in['U1'], 'L0_ffn_V1': _L0_ffn_in['V1'], 'L0_ffn_b1': _L0_ffn_in['b1'], 'L0_ffn_U2': _L0_ffn_in['U2'], 'L0_ffn_V2': _L0_ffn_in['V2'], 'L0_ffn_b2': _L0_ffn_in['b2'], 'L1_attn_Wq': _L1_attn_in['Wq'], 'L1_attn_Wk': _L1_attn_in['Wk'], 'L1_attn_Wv': _L1_attn_in['Wv'], 'L1_attn_gn_weight': _L1_attn_in['gn_weight'], 'L1_attn_gn_bias': _L1_attn_in['gn_bias'], 'L1_attn_Wout': _L1_attn_in['Wout'], 'L1_ffn_gate_w': _L1_ffn_in['gate_w'], 'L1_ffn_gate_b': _L1_ffn_in['gate_b'], 'L1_ffn_expert_w': _L1_ffn_in['expert_w'], 'L1_ffn_expert_b': _L1_ffn_in['expert_b'], 'L1_ffn_out_w': _L1_ffn_in['out_w'], 'L1_ffn_out_b': _L1_ffn_in['out_b']}

def reference(x, txt, L0_tok_W, L0_attn_Wq, L0_attn_Wk, L0_attn_Wv, L0_attn_Wo, L0_ffn_U1, L0_ffn_V1, L0_ffn_b1, L0_ffn_U2, L0_ffn_V2, L0_ffn_b2, L1_attn_Wq, L1_attn_Wk, L1_attn_Wv, L1_attn_gn_weight, L1_attn_gn_bias, L1_attn_Wout, L1_ffn_gate_w, L1_ffn_gate_b, L1_ffn_expert_w, L1_ffn_expert_b, L1_ffn_out_w, L1_ffn_out_b):
    import jax
    import jax.numpy as jnp

    def _L0_tok_ref(inputs, W):
        import jax, jax.numpy as jnp
        import numpy as np
        from jax import lax
        PATCH = 16
        B, C, H, Wimg = inputs.shape
        patches = lax.conv_general_dilated_patches(inputs, filter_shape=[PATCH, PATCH], window_strides=[PATCH, PATCH], padding='VALID', dimension_numbers=('NCHW', 'HWIO', 'NCHW'))
        patches = patches.reshape(B, -1, C * PATCH * PATCH)
        return jnp.einsum('bnf,fh->bnh', patches, W)

    def _L0_attn_ref(x, Wq, Wk, Wv, Wo):
        import jax, jax.numpy as jnp
        import numpy as np
        B, S, HID = (2, 512, 256)
        NH, NKV, D = (16, 4, 64)
        SCALE = 1.0 / np.sqrt(D).astype(np.float32)
        SOFTCAP = 30.0
        WINDOW = 256
        NEG = -1e+30
        b, s, _ = x.shape
        n_rep = NH // NKV
        q = (x @ Wq.T).reshape(b, s, NH, D)
        k = (x @ Wk.T).reshape(b, s, NKV, D)
        v = (x @ Wv.T).reshape(b, s, NKV, D)
        k = jnp.repeat(k, n_rep, axis=2)
        v = jnp.repeat(v, n_rep, axis=2)
        scores = jnp.einsum('bqhd,bkhd->bhqk', q, k) * SCALE
        scores = SOFTCAP * jnp.tanh(scores / SOFTCAP)
        i = jnp.arange(s)[:, None]
        j = jnp.arange(s)[None, :]
        mask = (j <= i) & (j > i - WINDOW)
        scores = jnp.where(mask, scores, NEG)
        p = jax.nn.softmax(scores, axis=-1)
        o = jnp.einsum('bhqk,bkhd->bqhd', p, v).reshape(b, s, NH * D)
        return o @ Wo.T

    def _L0_ffn_ref(x, U1, V1, b1, U2, V2, b2):
        import jax, jax.numpy as jnp
        import numpy as np
        D_MODEL, D_FF, RANK = (256, 1024, 64)
        B, S = (4, 1024)
        P = jnp.einsum('bsd,dr->bsr', x, U1)
        H = jax.nn.gelu(jnp.einsum('bsr,rf->bsf', P, V1) + b1)
        Q = jnp.einsum('bsf,fr->bsr', H, U2)
        return jnp.einsum('bsr,rd->bsd', Q, V2) + b2

    def _L1_attn_ref(x, Wq, Wk, Wv, gn_weight, gn_bias, Wout):
        import math
        import jax, jax.numpy as jnp
        import numpy as np
        D_MODEL = 256
        N_HEADS = 16
        HEAD_DIM = D_MODEL // N_HEADS
        B, L = (2, 512)
        EPS = 1e-05

        def _gammas():
            return jnp.array([1.0 - 2.0 ** (-5 - math.floor(8 * i / N_HEADS)) for i in range(N_HEADS)], dtype=jnp.float32)

        def _decay_mask(seq_len):
            idx = jnp.arange(seq_len)
            diff = idx[:, None] - idx[None, :]
            g = _gammas()[:, None, None]
            pow_ = g ** jnp.maximum(diff, 0).astype(jnp.float32)
            return jnp.where(diff >= 0, pow_, 0.0)
        Bq, Lq, _ = x.shape
        Q = jnp.einsum('bld,hde->bhle', x, Wq)
        K = jnp.einsum('bld,hde->bhle', x, Wk)
        V = jnp.einsum('bld,hde->bhle', x, Wv)
        Dm = _decay_mask(Lq)
        scores = jnp.einsum('bhle,bhme->bhlm', Q, K) * Dm[None] / math.sqrt(HEAD_DIM)
        out = jnp.einsum('bhlm,bhme->bhle', scores, V)
        combined = out.transpose(0, 2, 1, 3).reshape(Bq, Lq, D_MODEL)
        c = combined.transpose(0, 2, 1).reshape(Bq, N_HEADS, HEAD_DIM, Lq)
        mean = jnp.mean(c, axis=(2, 3), keepdims=True)
        var = jnp.var(c, axis=(2, 3), keepdims=True)
        c = (c - mean) / jnp.sqrt(var + EPS)
        c = c.reshape(Bq, D_MODEL, Lq)
        c = c * gn_weight[None, :, None] + gn_bias[None, :, None]
        combined = c.transpose(0, 2, 1)
        return combined @ Wout

    def _L1_ffn_ref(x, gate_w, gate_b, expert_w, expert_b, out_w, out_b):
        import jax, jax.numpy as jnp
        import numpy as np
        B, S, D, E, H, O = (4, 512, 256, 8, 512, 256)
        Bq, Sq, Dq = x.shape
        xt = x.reshape(-1, Dq)
        logits = xt @ gate_w + gate_b
        idx = jnp.argmax(logits, axis=-1)
        all_out = jnp.einsum('td,edh->teh', xt, expert_w) + expert_b[None]
        onehot = jax.nn.one_hot(idx, expert_w.shape[0], dtype=x.dtype)
        sel = jnp.einsum('te,teh->th', onehot, all_out)
        out = sel @ out_w + out_b
        return out.reshape(Bq, Sq, -1)
    h = _L0_tok_ref(x, L0_tok_W)
    h = jnp.concatenate([h, txt], axis=1)
    h = h + _L0_attn_ref(_layernorm(h, axis=-1), L0_attn_Wq, L0_attn_Wk, L0_attn_Wv, L0_attn_Wo)
    h = h + _L0_ffn_ref(_layernorm(h, axis=-1), L0_ffn_U1, L0_ffn_V1, L0_ffn_b1, L0_ffn_U2, L0_ffn_V2, L0_ffn_b2)
    h = h + _L1_attn_ref(_layernorm(h, axis=-1), L1_attn_Wq, L1_attn_Wk, L1_attn_Wv, L1_attn_gn_weight, L1_attn_gn_bias, L1_attn_Wout)
    h = h + _L1_ffn_ref(_layernorm(h, axis=-1), L1_ffn_gate_w, L1_ffn_gate_b, L1_ffn_expert_w, L1_ffn_expert_b, L1_ffn_out_w, L1_ffn_out_b)
    return h

_drawn_inputs = setup_inputs


def setup_inputs(seed=0):
    import zlib

    import numpy as np

    out = dict(_drawn_inputs(seed))
    spreads = {'L0_ffn_b1': (0.0, 0.295),
     'L0_ffn_b2': (0.0, 0.1),
     'L1_attn_gn_weight': (1.0, 0.2),
     'L1_attn_gn_bias': (0.0, 0.1)}
    factors = {'L0_attn_Wq': 3.107,
     'L0_attn_Wk': 3.008,
     'L0_ffn_U1': 3.608,
     'L0_ffn_V1': 4.07,
     'L1_ffn_expert_b': 3.981,
     'L1_ffn_out_b': 3.209}
    for name, (base, spread) in spreads.items():
        noise = np.random.default_rng([zlib.crc32(name.encode()), seed]).standard_normal(out[name].shape)
        drawn = base * np.exp(spread * noise) if base else spread * noise
        out[name] = jnp.asarray(drawn.astype(out[name].dtype))
    for name, factor in factors.items():
        out[name] = (out[name] * factor).astype(out[name].dtype)
    return out
```

```python
import concourse.bass as bass
from concourse import mybir
from contextlib import ExitStack

F32 = mybir.dt.float32
U32 = mybir.dt.uint32
ALU = mybir.AluOpType
ACT = mybir.ActivationFunctionType

B, IMG_TOK, TXT_TOK, D = 32, 196, 77, 256
S = IMG_TOK + TXT_TOK
SP = S + 1
P = 128
CH = [(0, 128), (128, 128), (256, S - 256)]
PATCH_F = 768
FK = PATCH_F // P
NH, NKV, HD = 16, 4, 64
CAP = 30.0
D_FF, RANK = 1024, 64
MF = D_FF // P
RP = 8
NE, EH = 8, 512
EPS = 1e-5
TOK_BLOCKS = B * IMG_TOK // P
EB = 7
MB = 112
M_BLOCKS = B * S // MB
W0 = 402
TW = S + 1 - 256


def build(nc, xT, txt, consts, w, out):
    ctx = ExitStack()
    with ctx:
        def sb(name, shape, dt=F32):
            return ctx.enter_context(nc.sbuf_tensor(name, shape, dt))

        def sem(name):
            return ctx.enter_context(nc.semaphore(name))

        h_img = nc.dram_tensor("h_img", (B * IMG_TOK, D), F32, kind="Internal").ap()
        h_ret = nc.dram_tensor("h_ret", (B * S, D), F32, kind="Internal").ap()

        wq = sb("wq", [P, 2, NH * HD])
        wk = sb("wk", [P, 2, 2 * NKV * HD])
        wv = sb("wv", [P, 2, NKV * HD])
        wo = sb("wo", [P, 8, D])
        u1 = sb("u1", [P, 2, P])
        v1 = sb("v1", [RANK, D_FF])
        b1 = sb("b1", [P, MF])
        u2 = sb("u2", [P, MF, RANK])
        v2 = sb("v2", [P, D])
        b2 = sb("b2", [P, D])
        rwq = sb("rwq", [P, 2, D])
        rwk = sb("rwk", [P, 2, D])
        rwv = sb("rwv", [P, 2, D])
        gnw = sb("gnw", [P, 2])
        gnb = sb("gnb", [P, 2])
        wout = sb("wout", [P, 2, D])
        gate_w = sb("gate_w", [P, 2, NE])
        gate_b = sb("gate_b", [P, NE])
        iota8 = sb("iota8", [P, NE])
        ident = sb("ident", [P, P])
        ones = sb("ones", [P, HD])
        eps = sb("eps", [P, 3])
        half = sb("half", [P, 3])
        pmask = sb("pmask", [P, W0])
        tmask = sb("tmask", [CH[2][1], TW])
        tri = sb("tri", [P, P])
        blockdiag = sb("blockdiag", [P, P])
        headavg = sb("headavg", [P, P])
        dec_q = sb("dec_q", [P, 2, 2, SP])
        dec_k = sb("dec_k", [P, 2, SP])
        dec_kt = sb("dec_kt", [P, 2, D])
        moe_w = sb("moe_w", [P, 2, NE, D])
        moe_b = sb("moe_b", [NE, D])

        banks = ctx.enter_context(nc.psum_tensor("banks", [P, 8, 512], F32))
        psum = [banks[:, n, :] for n in range(8)]
        S_BANK, O_BANK, D_BANK, Y = psum[0:2], psum[2], psum[3], psum[4:8]
        QKV_BANK = [psum[0], psum[1], psum[2], psum[3]]

        stage1 = ExitStack()
        with stage1:
            def sb1(name, shape, dt=F32):
                return stage1.enter_context(nc.sbuf_tensor(name, shape, dt))

            patch = sb1("patch", [P, EB, FK, P])
            wtok = sb1("wtok", [P, FK, D])
            emb = sb1("emb", [P, EB, D])
            ewT = sb1("ewT", [P, 4, NE, D])
            ebT = sb1("ebT", [P, 4, NE])
            ow = sb1("ow", [P, 4, D])
            ob = sb1("ob", [NE, D])
            tok_w_in, patch_in, const_in = sem("tok_w_in"), [sem(f"patch_in{k}") for k in range(EB)], sem("const_in")
            emb_ps, emb_saved, emb_out = sem("emb_ps"), sem("emb_saved"), [sem(f"emb_out{k}") for k in range(EB)]
            expert_in, fuse_ps, fuse_saved = sem("expert_in"), sem("fuse_ps"), sem("fuse_saved")
            block = stage1.enter_context(nc.Block())
            n_blocks = TOK_BLOCKS // EB

            loads = [(wq, w["wq"]), (wk, w["wk"]), (wv, w["wv"]), (wo, w["wo"]), (u1, w["u1"]), (v1, w["v1"]),
                     (b1, w["b1"]), (u2, w["u2"]), (v2, w["v2"]), (b2, w["b2"]), (rwq, w["rwq"]), (rwk, w["rwk"]),
                     (rwv, w["rwv"]), (gnw, w["gnw"]), (gnb, w["gnb"]), (wout, w["wout"]), (gate_w, w["gate_w"]),
                     (gate_b, w["gate_b"])]
            loads += [(t, consts[n]) for n, t in (
                ("iota8", iota8), ("ident", ident), ("ones", ones), ("half", half), ("eps", eps), ("pmask", pmask), ("tmask", tmask),
                ("tri", tri), ("blockdiag", blockdiag), ("headavg", headavg), ("dec_q", dec_q), ("dec_k", dec_k),
                ("dec_kt", dec_kt))]

            @block.sync
            def _(sp):
                sp.dma_start(wtok[:], w["wtok"]).then_inc(tok_w_in, 16)
                for k in range(EB):
                    sp.dma_start(patch[:, k], xT[k]).then_inc(patch_in[k], 16)
                with sp.Fori(1, n_blocks) as i:
                    for k in range(EB):
                        sp.wait_ge(emb_ps, (i - 1) * EB + k + 1)
                        sp.dma_start(patch[:, k], xT[bass.ds(i * EB + k, 1)].rearrange("o p k t -> (o p) k t"))\
                            .then_inc(patch_in[k], 16)

            @block.gpsimd
            def _(pool):
                for t, src in loads:
                    pool.dma_start(t[:], src).then_inc(const_in, 16)
                pool.wait_ge(const_in, 16 * len(loads))

            @block.tensor
            def _(pe):
                pe.wait_ge(tok_w_in, 16)

                def embed(i, k, reuse):
                    pe.wait_ge(patch_in[k], (i + 1) * 16)
                    if reuse:
                        pe.wait_ge(emb_saved, (i - 1) * EB + k + 1)
                    for f in range(FK):
                        mm = nc.tensor.matmul(psum[k][:, 0:D], patch[:, k, f, :], wtok[:, f, :],
                                              start=(f == 0), stop=(f == FK - 1))
                    mm.then_inc(emb_ps, 1)

                for k in range(EB):
                    embed(0, k, False)
                with pe.Fori(1, n_blocks) as i:
                    for k in range(EB):
                        embed(i, k, True)
                pe.wait_ge(expert_in, 64)
                pe.wait_ge(emb_saved, TOK_BLOCKS)
                for n in range(2 * NE):
                    e, kd = n // 2, n % 2
                    if n >= 4:
                        pe.wait_ge(fuse_saved, n - 3)
                    for t in range(4):
                        mm = nc.tensor.matmul(psum[n % 4][:, 0:D], ewT[:, t, e, kd * P:(kd + 1) * P], ow[:, t, :],
                                              start=(t == 0), stop=(t == 3))
                    mm.then_inc(fuse_ps, 1)
                for t in range(4):
                    mm = nc.tensor.matmul(psum[4][0:NE, 0:D], ebT[:, t, :], ow[:, t, :], start=(t == 0), stop=(t == 3))
                mm.then_inc(fuse_ps, 1)

            @block.vector
            def _(dve):
                def save(i, k, reuse):
                    dve.wait_ge(emb_ps, i * EB + k + 1)
                    if reuse:
                        dve.wait_ge(emb_out[k], i * 16)
                    nc.vector.tensor_copy(emb[:, k, :], psum[k][:, 0:D]).then_inc(emb_saved, 1)

                for k in range(EB):
                    save(0, k, False)
                with dve.Fori(1, n_blocks) as i:
                    for k in range(EB):
                        save(i, k, True)
                for n in range(2 * NE):
                    dve.wait_ge(fuse_ps, n + 1)
                    nc.vector.tensor_copy(moe_w[:, n % 2, n // 2, :], psum[n % 4][:, 0:D]).then_inc(fuse_saved, 1)
                dve.wait_ge(fuse_ps, 2 * NE + 1)
                dve.wait_ge(expert_in, 64)
                nc.vector.tensor_tensor(moe_b[:, :], psum[4][0:NE, 0:D], ob[:, :], ALU.add).then_inc(fuse_saved, 1)

            @block.scalar
            def _(act):
                for t, src in ((ewT, w["ewT"]), (ebT, w["ebT"]), (ow, w["ow"]), (ob, w["ob"])):
                    act.dma_start(t[:], src).then_inc(expert_in, 16)
                with act.Fori(0, n_blocks) as i:
                    for k in range(EB):
                        act.wait_ge(emb_saved, i * EB + k + 1)
                        act.dma_start(h_img[bass.ds((i * EB + k) * P, P), :], emb[:, k, :]).then_inc(emb_out[k], 16)
                for k in range(EB):
                    act.wait_ge(emb_out[k], n_blocks * 16)

        stage2 = ExitStack()
        with stage2:
            def sb2(name, shape, dt=F32):
                return stage2.enter_context(nc.sbuf_tensor(name, shape, dt))

            def sem2(name):
                return stage2.enter_context(nc.semaphore(name))

            h_in = sb2("h_in", [P, 3, D])
            h = sb2("h", [P, 3, D])
            h_out = sb2("h_out", [P, 3, D])
            st = {n: sb2(f"ln_st{n}", [P, 3, 6]) for n in (1, 2, 3)}
            mv = {n: sb2(f"ln_mv{n}", [P, 3, 2]) for n in (1, 2, 3)}
            ve = {n: sb2(f"ln_ve{n}", [P, 3]) for n in (1, 2, 3)}
            rs = {n: sb2(f"ln_rs{n}", [P, 3]) for n in (1, 2, 3)}
            xn = {n: sb2(f"xn{n}", [P, 3, D]) for n in (1, 2, 3)}
            xt = {n: sb2(f"xt{n}", [P, 2, SP]) for n in (1, 2, 3)}
            qt = sb2("qt", [P, 8, SP])
            kt = sb2("kt", [P, NKV, SP])
            v = sb2("v", [P, 3, NKV * HD])
            capped = sb2("capped", [P, 2, 420])
            probs = sb2("probs", [P, 4, 420])
            tail_t = sb2("tail_t", [CH[2][1], 2, NH // 2, TW])
            tail_p = sb2("tail_p", [CH[2][1], 2, NH // 2, TW])
            inv_den = sb2("inv_den", [P, SP])
            ot = sb2("ot", [P, 8, SP])
            pt = sb2("pt", [P, SP])
            gelu = sb2("gelu", [P, MF, SP])
            qf = sb2("qf", [P, SP])
            rq = sb2("rq", [P, 2, 2, SP])
            rk = sb2("rk", [P, 2, SP])
            rkt = sb2("rkt", [P, 2, D])
            rv = sb2("rv", [P, 3, RP, 2, 32])
            state = sb2("state", [P, 4, P])
            rs_sb = sb2("rs_sb", [P, 2, 4, 2, 2, P])
            ct = sb2("ct", [P, 2, SP])
            cn = sb2("cn", [P, 2, SP])
            gst = sb2("gst", [P, 2, 6])
            gmv = sb2("gmv", [P, 2, 2])
            gsq = sb2("gsq", [P, 2])
            gm = sb2("gm", [P, 2, 2])
            gmm = sb2("gmm", [P, 2])
            gvar = sb2("gvar", [P, 2])
            gve = sb2("gve", [P, 2])
            grs = sb2("grs", [P, 2])
            gsc = sb2("gsc", [P, 2])
            gms = sb2("gms", [P, 2])
            gbi = sb2("gbi", [P, 2])

            zeroed = sem2("zeroed")
            hin_in = sem2("hin_in")
            h_in_dma = sem2("h_in_dma")
            hout_dma = sem2("hout_dma")
            ln_mv = {n: sem2(f"ln_mv_done{n}") for n in (1, 2, 3)}
            ln_rs = {n: sem2(f"ln_rs_done{n}") for n in (1, 2, 3)}
            xn_done = {n: sem2(f"xn_done{n}") for n in (1, 2, 3)}
            xt_ps = {n: sem2(f"xt_ps{n}") for n in (1, 2, 3)}
            xt_act = {n: sem2(f"xt_act{n}") for n in (1, 2, 3)}
            xt_dve = {n: sem2(f"xt_dve{n}") for n in (1, 2, 3)}
            oproj_ps, att_added = sem2("oproj_ps"), sem2("att_added")
            qkv_ps, qkv_act, qkv_dve = sem2("qkv_ps"), sem2("qkv_act"), sem2("qkv_dve")
            tail_ps, tail_act, tail_done = sem2("tail_ps"), sem2("tail_act"), sem2("tail_done")
            score_ps, cap_done, exp_done, prob_done = (sem2(n) for n in ("score_ps", "cap_done", "exp_done", "prob_done"))
            pv_ps, inv_done, ot_done = sem2("pv_ps"), sem2("inv_done"), sem2("ot_done")
            p_ps, p_saved = sem2("p_ps"), sem2("p_saved")
            ff_ps, gelu_done = sem2("ff_ps"), sem2("gelu_done")
            qf_ps, qf_saved = sem2("qf_ps"), sem2("qf_saved")
            b2_added, ffo_ps, ffn_added = sem2("b2_added"), sem2("ffo_ps"), sem2("ffn_added")
            rq_ps, rq_saved = sem2("rq_ps"), sem2("rq_saved")
            rk_ps, rk_saved = sem2("rk_ps"), sem2("rk_saved")
            rv_ps, rv_saved = sem2("rv_ps"), sem2("rv_saved")
            rkt_ps, rkt_saved = sem2("rkt_ps"), sem2("rkt_saved")
            state_ps, state_saved = sem2("state_ps"), sem2("state_saved")
            rs_ps, rs_masked = sem2("rs_ps"), sem2("rs_masked")
            rpv_ps, ct_saved = sem2("rpv_ps"), sem2("ct_saved")
            gn_ps, gn_dve, gn_pool, cn_done = sem2("gn_ps"), sem2("gn_dve"), sem2("gn_pool"), sem2("cn_done")
            wo_ps, ret_added = sem2("wo_ps"), sem2("ret_added")

            XT_BANK = {1: (Y[3], Y[0]), 2: (Y[0], Y[1]), 3: (Y[1], Y[2])}
            RV_BANK = (Y[3], Y[0], Y[1])

            def qkv_target(u):
                bank = QKV_BANK[u % 4]
                if u < 8:
                    return qt[:, u, :], bank[:, 0:SP]
                if u < 12:
                    return kt[:, u - 8, :], bank[:, 0:SP]
                n = CH[u - 12][1]
                return v[0:n, u - 12, :], bank[0:n, 0:NKV * HD]

            RQ_BANK, RK_BANK, RKT_BANK = (Y[3], Y[0]), (Y[1], Y[2]), (Y[2], Y[3])
            RS_AT = {9: (0, 1), 10: (2, 3), 11: (4, 5), 12: (6, 7, 8)}

            def RS_BANK(u):
                return Y[1 + u % 3]

            block = stage2.enter_context(nc.Block())

            def turns(eng, turn):
                turn(0, False, True)
                turn(1, True, True)
                with eng.Fori(2, B - 1) as i:
                    turn(i, True, True)
                turn(B - 1, True, False)
                turn(B, True, None)

            @block.sync
            def _(sp):
                def load(dst, n, s):
                    r = n * IMG_TOK
                    t = n * TXT_TOK
                    k = IMG_TOK - P
                    sp.dma_start(dst[:, 0, :], h_img[bass.ds(r, P), :]).then_inc(s, 16)
                    sp.dma_start(dst[0:k, 1, :], h_img[bass.ds(r + P, k), :]).then_inc(s, 16)
                    sp.dma_start(dst[k:P, 1, :], txt[bass.ds(t, P - k), :]).then_inc(s, 16)
                    sp.dma_start(dst[0:CH[2][1], 2, :], txt[bass.ds(t + P - k, CH[2][1]), :]).then_inc(s, 16)

                def turn(i, prev, nxt):
                    if nxt:
                        sp.wait_ge(xn_done[1], 3 * i + 3)
                        load(h_in, i + 1, hin_in)
                    if nxt is not None:
                        if prev:
                            sp.wait_ge(ret_added, 3 * (i - 1) + 3)
                            store(i - 1)
                        load(h, i, h_in_dma)
                    else:
                        sp.wait_ge(ret_added, 3 * (i - 1) + 3)
                        store(i - 1)

                def store(n):
                    sp.dma_start(h_ret[bass.ds(n * S, 2 * P), :].rearrange("(c p) d -> p c d", p=P), h_out[:, 0:2, :])\
                        .then_inc(hout_dma, 16)
                    sp.dma_start(h_ret[bass.ds(n * S + 2 * P, CH[2][1]), :], h_out[0:CH[2][1], 2, :]).then_inc(hout_dma, 16)

                load(h_in, 0, hin_in)
                turns(sp, turn)
                sp.wait_ge(hout_dma, 32 * B)

            @block.gpsimd
            def _(pool):
                def ln_pow(n, e):
                    pool.wait_ge(ln_mv[n], 3 * e + 3)
                    nc.gpsimd.tensor_tensor(ve[n][:, :], mv[n][:, :, 1], eps[:, :], ALU.add).then_inc(ln_rs[n], 1)
                    pool.wait_ge(ln_rs[n], 2 * e + 1)
                    nc.gpsimd.tensor_tensor(rs[n][:, :], ve[n][:, :], half[:, :], ALU.pow).then_inc(ln_rs[n], 1)

                def turn(i, prev, nxt):
                    a = i - 1
                    if prev:
                        ln_pow(2, a)
                    if nxt is not None:
                        pool.wait_ge(tail_act, 2 * i + 2)
                        nc.gpsimd.tensor_tensor(tail_p[:, :, :, :].rearrange("p e h q -> p (e h) q"),
                                                tail_p[:, :, :, :].rearrange("p e h q -> p (e h) q"),
                                                tmask[:, None, :].to_broadcast([CH[2][1], NH, TW]), ALU.mult).then_inc(tail_done, 1)
                    for hh in range(NH):
                        if nxt is not None:
                            pool.wait_ge(exp_done, NH * i + hh + 1)
                            nc.gpsimd.tensor_tensor(probs[:, hh % 4, 0:W0], probs[:, hh % 4, 0:W0], pmask[:, :], ALU.mult)\
                                .then_inc(prob_done, 1)
                        if hh == 0 and prev:
                            pool.wait_ge(xn_done[2], 3 * a + 3)
                            nc.gpsimd.tensor_tensor(h[:, 0:2, :], h[:, 0:2, :], b2[:, None, :].to_broadcast([P, 2, D]), ALU.add)\
                                .then_inc(b2_added, 1)
                            nc.gpsimd.tensor_tensor(h[0:CH[2][1], 2, :], h[0:CH[2][1], 2, :], b2[0:CH[2][1], :], ALU.add)\
                                .then_inc(b2_added, 1)
                        if hh == 3 and nxt:
                            ln_pow(1, i + 1)
                        if hh == 5 and prev:
                            ln_pow(3, a)
                        if hh == 14 and prev:
                            pool.wait_ge(gn_dve, 12 * a + 9)
                            nc.gpsimd.tensor_tensor(gve[:, :], gvar[:, :], eps[:, 0:2], ALU.add).then_inc(gn_pool, 1)
                            pool.wait_ge(gn_pool, 2 * a + 1)
                            nc.gpsimd.tensor_tensor(grs[:, :], gve[:, :], half[:, 0:2], ALU.pow).then_inc(gn_pool, 1)

                pool.wait_ge(zeroed, 8)
                ln_pow(1, 0)
                turns(pool, turn)

            @block.scalar
            def _(act):
                def ln_evac(n, e):
                    act.wait_ge(xt_ps[n], 2 * e + 1)
                    nc.scalar.activation(xt[n][:, 0, 0:S], XT_BANK[n][0][:, 0:S], ACT.Copy).then_inc(xt_act[n], 1)

                def turn(i, prev, nxt):
                    a = i - 1
                    if nxt is not None:
                        for u in range(0, 15, 2):
                            act.wait_ge(qkv_ps, 15 * i + u + 1)
                            dst, src = qkv_target(u)
                            nc.scalar.activation(dst, src, ACT.Copy).then_inc(qkv_act, 1)
                        act.wait_ge(tail_ps, i + 1)
                        nc.scalar.activation(tail_t[:, :, :, :], banks[0:CH[2][1], 2:4, 0:NH // 2 * TW].rearrange("p e (h q) -> p e h q", q=TW),
                                             ACT.Tanh, scale=HD ** -0.5 / CAP).then_inc(tail_act, 1)
                        act.wait_ge(tail_act, 2 * i + 1)
                        nc.scalar.activation(tail_p[:, :, :, :], tail_t[:, :, :, :], ACT.Exp, scale=CAP).then_inc(tail_act, 1)
                    for hh in range(NH):
                        if nxt is not None:
                            act.wait_ge(score_ps, NH * i + hh + 1)
                            nc.scalar.activation(capped[:, hh % 2, :], S_BANK[hh % 2][:, 0:420], ACT.Tanh,
                                                 scale=HD ** -0.5 / CAP).then_inc(cap_done, 1)
                            act.wait_ge(cap_done, NH * i + hh + 1)
                            if hh >= 4:
                                act.wait_ge(pv_ps, NH * i + hh - 3)
                            nc.scalar.activation(probs[:, hh % 4, :], capped[:, hh % 2, :], ACT.Exp, scale=CAP)\
                                .then_inc(exp_done, 1)
                        if prev:
                            rest(hh, a)
                        if hh == 5 and nxt:
                            ln_evac(1, i + 1)

                def rest(hh, a):
                    if hh == 0:
                        ln_evac(2, a)
                        act.wait_ge(p_ps, a + 1)
                        nc.scalar.activation(pt[:, :], Y[2][:, 0:SP], ACT.Copy).then_inc(p_saved, 1)
                    if hh in (1, 2):
                        for m in range(4 * hh - 4, 4 * hh):
                            act.wait_ge(ff_ps, MF * a + m + 1)
                            nc.scalar.activation(gelu[:, m, :], Y[(3 + m) % 4][:, 0:SP], ACT.Gelu_apprx_tanh,
                                                 bias=b1[:, m:m + 1]).then_inc(gelu_done, 1)
                    if hh == 7:
                        ln_evac(3, a)
                    if hh == 8:
                        for c, (_, n) in enumerate(CH):
                            act.wait_ge(rv_ps, 3 * a + c + 1)
                            for e in range(2):
                                cp = nc.scalar.activation(
                                    rv[0:n, c, :, e, 16 * e:16 * e + 16],
                                    RV_BANK[c][0:n, 0:D].rearrange("p (r e d) -> p r e d", e=2, d=16)[:, :, e, :], ACT.Copy)
                            cp.then_inc(rv_saved, 1)
                    if hh in (11, 12, 13):
                        c = hh - 11
                        t, n = CH[c]
                        act.wait_ge(rpv_ps, 3 * a + c + 1)
                        nc.scalar.activation(ct[:, :, t:t + n], Y[0][:, :].rearrange("p (m q) -> p m q", m=2)[:, :, 0:n],
                                             ACT.Copy).then_inc(ct_saved, 1)
                    if hh == 14:
                        act.wait_ge(gn_dve, 12 * a + 12)
                        for m in range(2):
                            nc.scalar.activation(cn[:, m, 0:S], ct[:, m, 0:S], ACT.Identity,
                                                 scale=gsc[:, m:m + 1], bias=gbi[:, m:m + 1]).then_inc(cn_done, 1)

                act.wait_ge(zeroed, 8)
                ln_evac(1, 0)
                turns(act, turn)

            @block.vector
            def _(dve):
                for t in (xt[1][:, :, S:SP], xt[2][:, :, S:SP], xt[3][:, :, S:SP], rv[:, :, :, :, :], mv[1][:, :, :], mv[2][:, :, :],
                          mv[3][:, :, :], ct[:, :, :]):
                    nc.vector.memset(t, 0.0).then_inc(zeroed, 1)

                def ln_stats(n, e, src):
                    for c, (_, r) in enumerate(CH):
                        nc.vector.bn_stats(st[n][0:r, c, :], src[0:r, c, :])
                    dve.drain()
                    for c, (_, r) in enumerate(CH):
                        nc.vector.bn_aggr(mv[n][0:r, c, :], st[n][0:r, c, :]).then_inc(ln_mv[n], 1)

                def ln_apply(n, e, src):
                    dve.wait_ge(ln_rs[n], 2 * e + 2)
                    for c, (_, r) in enumerate(CH):
                        nc.vector.tensor_scalar(xn[n][0:r, c, :], src[0:r, c, :], mv[n][0:r, c, 0:1], rs[n][0:r, c:c + 1],
                                                ALU.subtract, ALU.mult).then_inc(xn_done[n], 1)

                def ln_evac(n, e):
                    dve.wait_ge(xt_ps[n], 2 * e + 2)
                    nc.vector.tensor_copy(xt[n][:, 1, 0:S], XT_BANK[n][1][:, 0:S]).then_inc(xt_dve[n], 1)

                def turn(i, prev, nxt):
                    a = i - 1
                    if prev:
                        dve.wait_ge(h_in_dma, 64 * a + 64)
                        for c, (_, r) in enumerate(CH):
                            dve.wait_ge(oproj_ps, 3 * a + c + 1)
                            nc.vector.tensor_tensor(h[0:r, c, :], Y[c][0:r, 0:D], h[0:r, c, :], ALU.add).then_inc(att_added, 1)
                        dve.wait_ge(att_added, 3 * a + 3)
                        ln_stats(2, a, h)
                    if nxt is not None:
                        for u in range(1, 15, 2):
                            if u == 5 and prev:
                                ln_apply(2, a, h)
                            dve.wait_ge(qkv_ps, 15 * i + u + 1)
                            dst, src = qkv_target(u)
                            nc.vector.tensor_copy(dst, src).then_inc(qkv_dve, 1)
                    elif prev:
                        ln_apply(2, a, h)
                    for hh in range(NH):
                        if prev:
                            rest(hh, a)
                        if nxt:
                            if hh == 3:
                                dve.wait_ge(hin_in, 64 * (i + 1) + 64)
                                ln_stats(1, i + 1, h_in)
                            if hh == 4:
                                ln_apply(1, i + 1, h_in)
                            if hh == 5:
                                ln_evac(1, i + 1)
                        if nxt is not None and hh % 2:
                            j = hh // 2
                            dve.wait_ge(pv_ps, NH * i + hh + 1)
                            nc.vector.reciprocal(inv_den[:, :], D_BANK[:, 0:SP]).then_inc(inv_done, 1)
                            dve.wait_ge(inv_done, 8 * i + j + 1)
                            nc.vector.tensor_tensor(ot[:, j, :], O_BANK[:, 0:SP], inv_den[:, :], ALU.mult).then_inc(ot_done, 1)

                def rest(hh, a):
                    if hh == 0:
                        ln_evac(2, a)
                    if hh == 3:
                        dve.wait_ge(qf_ps, a + 1)
                        nc.vector.tensor_copy(qf[:, :], Y[3][:, 0:SP]).then_inc(qf_saved, 1)
                    if hh == 4:
                        dve.wait_ge(b2_added, 2 * a + 2)
                        for c, (_, r) in enumerate(CH):
                            dve.wait_ge(ffo_ps, 3 * a + c + 1)
                            nc.vector.tensor_tensor(h[0:r, c, :], Y[c][0:r, 0:D], h[0:r, c, :], ALU.add).then_inc(ffn_added, 1)
                    if hh == 5:
                        dve.wait_ge(ffn_added, 3 * a + 3)
                        ln_stats(3, a, h)
                    if hh == 6:
                        ln_apply(3, a, h)
                    if hh == 7:
                        ln_evac(3, a)
                        for m in range(2):
                            dve.wait_ge(rq_ps, 2 * a + m + 1)
                            for e in range(2):
                                nc.vector.tensor_tensor(rq[:, m, e, :], RQ_BANK[m][:, 0:SP], dec_q[:, m, e, :], ALU.mult)\
                                    .then_inc(rq_saved, 1)
                        for m in range(2):
                            dve.wait_ge(rk_ps, 2 * a + m + 1)
                            nc.vector.tensor_tensor(rk[:, m, :], RK_BANK[m][:, 0:SP], dec_k[:, m, :], ALU.mult).then_inc(rk_saved, 1)
                    if hh == 8:
                        for c in range(2):
                            dve.wait_ge(rkt_ps, 2 * a + c + 1)
                            nc.vector.tensor_tensor(rkt[:, c, :], RKT_BANK[c][:, 0:D], dec_kt[:, c, :], ALU.mult).then_inc(rkt_saved, 1)
                    if hh == 9:
                        dve.wait_ge(state_ps, a + 1)
                        nc.vector.tensor_tensor(state[:, :, :], Y[0][:, :].rearrange("p (n q) -> p n q", n=4),
                                                blockdiag[:, None, :].to_broadcast([P, 4, P]), ALU.mult).then_inc(state_saved, 1)
                    for u in RS_AT.get(hh, ()):
                        dve.wait_ge(rs_ps, 9 * a + u + 1)
                        c = u // 4
                        n = CH[c][1]
                        if u == 8:
                            dve.wait_ge(rpv_ps, 3 * a + 1)
                            nc.vector.tensor_tensor(
                                rs_sb[0:n, 0].rearrange("p r m e q -> p (r m e) q")[:, :, 0:n], RS_BANK(u)[0:n, 0:16 * n].rearrange("p (h q) -> p h q", q=n),
                                tri[0:n, None, 0:n].to_broadcast([n, NH, n]), ALU.mult).then_inc(rs_masked, 1)
                        else:
                            nc.vector.tensor_tensor(
                                rs_sb[:, c, u % 4, :, :, :], RS_BANK(u)[:, :].rearrange("p (m e q) -> p m e q", m=2, e=2),
                                tri[:, None, None, :].to_broadcast([P, 2, 2, P]), ALU.mult).then_inc(rs_masked, 1)
                    if hh == 14:
                        g = 12 * a
                        dve.wait_ge(ct_saved, 3 * a + 3)
                        for m in range(2):
                            nc.vector.bn_stats(gst[:, m, :], ct[:, m, 0:S]).then_inc(gn_dve, 1)
                        dve.drain()
                        for m in range(2):
                            nc.vector.bn_aggr(gmv[:, m, :], gst[:, m, :]).then_inc(gn_dve, 1)
                        dve.wait_ge(gn_dve, g + 4)
                        nc.vector.tensor_tensor(gsq[:, :], gmv[:, :, 0], gmv[:, :, 0], ALU.mult).then_inc(gn_dve, 1)
                        dve.wait_ge(gn_dve, g + 5)
                        nc.vector.tensor_tensor(gmv[:, :, 1], gsq[:, :], gmv[:, :, 1], ALU.add).then_inc(gn_dve, 1)
                        dve.wait_ge(gn_ps, a + 1)
                        nc.vector.tensor_copy(gm[:, :, :], Y[0][:, 0:4].rearrange("p (m s) -> p m s", m=2)).then_inc(gn_dve, 1)
                        dve.wait_ge(gn_dve, g + 7)
                        nc.vector.tensor_tensor(gmm[:, :], gm[:, :, 0], gm[:, :, 0], ALU.mult).then_inc(gn_dve, 1)
                        dve.wait_ge(gn_dve, g + 8)
                        nc.vector.tensor_tensor(gvar[:, :], gm[:, :, 1], gmm[:, :], ALU.subtract).then_inc(gn_dve, 1)
                        dve.wait_ge(gn_pool, 2 * a + 2)
                        nc.vector.tensor_tensor(gsc[:, :], grs[:, :], gnw[:, :], ALU.mult).then_inc(gn_dve, 1)
                        dve.wait_ge(gn_dve, g + 10)
                        nc.vector.tensor_tensor(gms[:, :], gm[:, :, 0], gsc[:, :], ALU.mult).then_inc(gn_dve, 1)
                        dve.wait_ge(gn_dve, g + 11)
                        nc.vector.tensor_tensor(gbi[:, :], gnb[:, :], gms[:, :], ALU.subtract).then_inc(gn_dve, 1)
                    if hh == 15:
                        if not isinstance(a, int) or a > 0:
                            dve.wait_ge(hout_dma, 32 * a)
                        for c, (_, r) in enumerate(CH):
                            dve.wait_ge(wo_ps, 3 * a + c + 1)
                            nc.vector.tensor_tensor(h_out[0:r, c, :], Y[1 + c][0:r, 0:D], h[0:r, c, :], ALU.add).then_inc(ret_added, 1)

                dve.wait_ge(zeroed, 8)
                dve.wait_ge(hin_in, 64)
                ln_stats(1, 0, h_in)
                ln_apply(1, 0, h_in)
                ln_evac(1, 0)
                turns(dve, turn)

            @block.tensor
            def _(pe):
                mm = nc.tensor.matmul

                def ln_transpose(n, e):
                    pe.wait_ge(xn_done[n], 3 * e + 3)
                    for k in range(2):
                        for c, (t, r) in enumerate(CH):
                            last = nc.tensor.transpose(XT_BANK[n][k][:, t:t + r], xn[n][0:r, c, k * P:(k + 1) * P], ident[0:r, 0:r])
                        last.then_inc(xt_ps[n], 1)

                def xt_ready(n, e):
                    pe.wait_ge(xt_act[n], e + 1)
                    pe.wait_ge(xt_dve[n], e + 1)

                def scores(i, hh):
                    g, j, s = hh // 4, hh // 2, 64 * (hh % 2)
                    if hh >= 2:
                        pe.wait_ge(cap_done, NH * i + hh - 1)
                    mm(S_BANK[hh % 2][:, 0:SP], kt[s:s + 64, g, 0:P], qt[s:s + 64, j, :], start=True, stop=True)
                    mm(S_BANK[hh % 2][:, SP:420], kt[s:s + 64, g, P:2 * P], qt[s:s + 64, j, P:SP], start=True, stop=True)\
                        .then_inc(score_ps, 1)

                def weighted(i, hh):
                    g, s = hh // 4, 64 * (hh % 2)
                    if hh == 0:
                        pe.wait_ge(tail_done, i + 1)
                    elif hh % 2 == 0:
                        pe.wait_ge(ot_done, 8 * i + hh // 2)
                    pe.wait_ge(prob_done, NH * i + hh + 1)
                    for bank, lhs in ((O_BANK, v), (D_BANK, None)):
                        for c, (t, r) in enumerate(CH):
                            left = ones[0:r, :] if lhs is None else v[0:r, c, 64 * g:64 * g + 64]
                            right = (probs[:, hh % 4, 0:SP], probs[:, hh % 4, SP:420], tail_p[:, hh % 2, hh // 2, :])[c]
                            last = mm(bank[s:s + 64, t:SP], left, right, start=(c == 0), stop=(c == 2))
                    last.then_inc(pv_ps, 1)

                def turn(i, prev, nxt):
                    a = i - 1
                    if prev:
                        pe.wait_ge(ot_done, 8 * a + 8)
                        if not isinstance(i, int) or i > 1:
                            pe.wait_ge(ret_added, 3 * a)
                        for c, (t, r) in enumerate(CH):
                            for j in range(8):
                                last = mm(Y[c][0:r, 0:D], ot[:, j, t:t + r], wo[:, j, :], start=(j == 0), stop=(j == 7))
                            last.then_inc(oproj_ps, 1)
                    if nxt is not None:
                        xt_ready(1, i)
                        for u in range(15):
                            if u >= 4:
                                pe.wait_ge(qkv_dve if u % 2 else qkv_act, (7 if u % 2 else 8) * i + (u - 4) // 2 + 1)
                            dst = qkv_target(u)[1]
                            for k in range(2):
                                if u < 8:
                                    last = mm(dst, wq[:, k, u * P:(u + 1) * P], xt[1][:, k, :], start=(k == 0), stop=(k == 1))
                                elif u < 12:
                                    last = mm(dst, wk[:, k, (u - 8) * P:(u - 7) * P], xt[1][:, k, :], start=(k == 0), stop=(k == 1))
                                else:
                                    t, r = CH[u - 12]
                                    last = mm(dst, xt[1][:, k, t:t + r], wv[:, k, :], start=(k == 0), stop=(k == 1))
                            last.then_inc(qkv_ps, 1)
                        pe.wait_ge(qkv_act, 8 * i + 8)
                        pe.wait_ge(qkv_dve, 7 * i + 7)
                        scores(i, 0)
                        t, r = CH[2]
                        for hh in range(NH):
                            s = 64 * (hh % 2)
                            last = mm(psum[2 + hh % 2][0:r, hh // 2 * TW:(hh // 2 + 1) * TW], kt[s:s + 64, hh // 4, t:t + r],
                                      qt[s:s + 64, hh // 2, t:SP], start=True, stop=True)
                        last.then_inc(tail_ps, 1)
                    for hh in range(NH):
                        if nxt is not None and hh < NH - 1:
                            scores(i, hh + 1)
                        if prev:
                            rest(hh, a)
                        if hh == 5 and nxt:
                            if prev:
                                pe.wait_ge(ffn_added, 3 * a + 1)
                            ln_transpose(1, i + 1)
                        if hh == 7 and prev:
                            if nxt:
                                xt_ready(1, i + 1)
                            retention_in(a)
                        if nxt is not None:
                            weighted(i, hh)

                def rest(hh, a):
                    if hh == 0:
                        ln_transpose(2, a)
                        xt_ready(2, a)
                        for k in range(2):
                            last = mm(Y[2][:, 0:SP], u1[:, k, :], xt[2][:, k, :], start=(k == 0), stop=(k == 1))
                        last.then_inc(p_ps, 1)
                        pe.wait_ge(p_saved, a + 1)
                    if hh in (1, 2):
                        for m in range(4 * hh - 4, 4 * hh):
                            if m >= 4:
                                pe.wait_ge(gelu_done, MF * a + m - 3)
                            mm(Y[(3 + m) % 4][:, 0:SP], v1[:, m * P:(m + 1) * P], pt[0:RANK, :], start=True, stop=True)\
                                .then_inc(ff_ps, 1)
                    if hh == 3:
                        pe.wait_ge(gelu_done, MF * a + MF)
                        for m in range(MF):
                            s = 64 * (m % 2)
                            last = mm(Y[3][s:s + 64, 0:SP], u2[:, m, :], gelu[:, m, :], start=(m < 2), stop=(m >= MF - 2))
                        last.then_inc(qf_ps, 1)
                    if hh == 4:
                        pe.wait_ge(qf_saved, a + 1)
                        for c, (t, r) in enumerate(CH):
                            mm(Y[c][0:r, 0:D], qf[:, t:t + r], v2[:, :], start=True, stop=True).then_inc(ffo_ps, 1)
                    if hh == 8:
                        for c, (t, r) in enumerate(CH):
                            if c < 2:
                                pe.wait_ge(rq_saved, 4 * a + 2 * c + 2)
                            else:
                                pe.wait_ge(rk_saved, 2 * a + 1)
                            for k in range(2):
                                last = mm(RV_BANK[c][0:r, 0:D], xt[3][:, k, t:t + r], rwv[:, k, :], start=(k == 0), stop=(k == 1))
                            last.then_inc(rv_ps, 1)
                        for c in range(2):
                            if c == 0:
                                pe.wait_ge(rk_saved, 2 * a + 2)
                            else:
                                pe.wait_ge(rv_saved, 3 * a + 1)
                            t, r = CH[c]
                            for k in range(2):
                                last = mm(RKT_BANK[c][0:r, 0:D], xt[3][:, k, t:t + r], rwk[:, k, :], start=(k == 0), stop=(k == 1))
                            last.then_inc(rkt_ps, 1)
                    if hh == 9:
                        pe.wait_ge(rkt_saved, 2 * a + 2)
                        pe.wait_ge(rv_saved, 3 * a + 3)
                        for c in range(2):
                            for m in range(2):
                                n = 2 * c + m
                                last = mm(Y[0][:, n * P:(n + 1) * P], rkt[:, c, m * P:(m + 1) * P], heads_of(c, m), start=True, stop=True)
                        last.then_inc(state_ps, 1)
                    for u in RS_AT.get(hh, ()):
                        if 3 <= u < 7:
                            pe.wait_ge(rs_masked, 9 * a + u - 2)
                        if u == 7:
                            pe.wait_ge(rs_masked, 9 * a + 6)
                        c = u // 4
                        t, r = CH[c]
                        pairs = [pr + 4 * m for pr in range(4) for m in range(2)] if u == 8 else (u % 4, u % 4 + 4)
                        for n, pr in enumerate(pairs):
                            m, q = pr // 4, 32 * (pr % 4)
                            if n in (2, 4, 6):
                                pe.drain()
                            last = mm(RS_BANK(u)[0:r, 2 * r * n:2 * r * (n + 1)].rearrange("p (e q) -> p e q", e=2),
                                      rk[q:q + 32, m, t:t + r], rq[q:q + 32, m, :, t:t + r], start=True, stop=True)
                        last.then_inc(rs_ps, 1)
                    if hh in (11, 12, 13):
                        retained(hh - 11, a)
                    if hh == 14:
                        pe.wait_ge(ct_saved, 3 * a + 3)
                        pe.wait_ge(gn_dve, 12 * a + 6)
                        mm(Y[0][:, 0:4], headavg[:, :], gmv[:, :, :].rearrange("p m s -> p (m s)"), start=True, stop=True)\
                            .then_inc(gn_ps, 1)
                    if hh == 15:
                        pe.wait_ge(cn_done, 2 * a + 2)
                        for c, (t, r) in enumerate(CH):
                            for m in range(2):
                                last = mm(Y[1 + c][0:r, 0:D], cn[:, m, t:t + r], wout[:, m, :], start=(m == 0), stop=(m == 1))
                            last.then_inc(wo_ps, 1)

                def heads_of(c, m):
                    full = rv[:, c, 4 * m:4 * m + 4, :, :].rearrange("p r e d -> p r (e d)")
                    return bass.AP(full.tensor, full.offset, [list(full.ap[0]), [64, 4], [48, 2], [1, 16]])

                def retention_in(a):
                    ln_transpose(3, a)
                    xt_ready(3, a)
                    for bank, weight, s in ((RQ_BANK, rwq, rq_ps), (RK_BANK, rwk, rk_ps)):
                        for m in range(2):
                            for k in range(2):
                                last = mm(bank[m][:, 0:SP], weight[:, k, m * P:(m + 1) * P], xt[3][:, k, :],
                                          start=(k == 0), stop=(k == 1))
                            last.then_inc(s, 1)

                def retained(c, a):
                    t, r = CH[c]
                    if c == 0:
                        pe.wait_ge(state_saved, a + 1)
                    else:
                        pe.wait_ge(ct_saved, 3 * a + c)
                    pe.wait_ge(rs_masked, 9 * a + (4, 8, 9)[c])
                    for m in range(2):
                        o = m * D
                        for cc in range(c):
                            for e in range(2):
                                mm(Y[0][:, o:o + r], state[:, 2 * cc + m, :], rq[:, m, e, t:t + r],
                                   start=(cc == 0 and e == 0), stop=False, skip_group_check=True)
                        for q in range(4):
                            pr = 4 * m + q
                            for e in range(2):
                                last = mm(Y[0][32 * q:32 * q + 32, o:o + r], rv[0:r, c, pr, e, :], rs_sb[0:r, c % 2, q, m, e, 0:r],
                                          start=(c == 0 and e == 0), stop=(e == 1), skip_group_check=True)
                    last.then_inc(rpv_ps, 1)

                pe.wait_ge(zeroed, 8)
                ln_transpose(1, 0)
                turns(pe, turn)

        stage3 = ExitStack()
        with stage3:
            def sb3(name, shape, dt=F32):
                return stage3.enter_context(nc.sbuf_tensor(name, shape, dt))

            def sem3(name):
                return stage3.enter_context(nc.semaphore(name))

            eh = sb3("eh", [P, 2, D])
            est = sb3("est", [P, 2, 6])
            emv = sb3("emv", [P, 2, 2])
            eve = sb3("eve", [P, 2])
            ers = sb3("ers", [P, 2])
            exn = sb3("exn", [P, 2, D])
            ext = sb3("ext", [P, 2, 2, MB])
            logit = sb3("logit", [P, 2, NE])
            top = sb3("top", [P, 2, NE])
            topi = sb3("topi", [P, 2, NE], U32)
            topf = sb3("topf", [P, 2])
            hot = sb3("hot", [P, 2, NE])
            hotT = sb3("hotT", [NE, 2, MB])
            acc = sb3("acc", [P, 2, D])
            e_dve, e_pool, e_xn = (sem3(n) for n in ("e_dve", "e_pool", "e_xn"))
            e_in, e_out = ([sem3(f"{n}{k}") for k in range(2)] for n in ("e_in", "e_out"))
            ext_ps, ext_saved, logit_ps, hot_ps, hot_saved = (sem3(n) for n in ("ext_ps", "ext_saved", "logit_ps", "hot_ps", "hot_saved"))
            expert_ps, bias_ps, acc_step = (sem3(n) for n in ("expert_ps", "bias_ps", "acc_step"))
            hot_done = sem3("hot_done")
            block = stage3.enter_context(nc.Block())
            XB, LB, EBK = psum[0], psum[1], psum[4:8]
            NB = M_BLOCKS // 2

            @block.sync
            def _(sp):
                def fetch(n, k, first):
                    if not first:
                        sp.wait_ge(acc_step, 9 * (n - 2) + 9)
                    sp.dma_start(eh[0:MB, k, :], h_ret[bass.ds(n * MB, MB), :]).then_inc(e_in[k], 16)

                fetch(0, 0, True)
                fetch(1, 1, True)
                with sp.Fori(1, NB) as i:
                    for k in range(2):
                        fetch(2 * i + k, k, False)

            @block.gpsimd
            def _(pool):
                with pool.Fori(0, NB) as i:
                    for k in range(2):
                        n = 2 * i + k
                        pool.wait_ge(e_dve, 6 * n + 2)
                        nc.gpsimd.tensor_tensor(eve[0:MB, k:k + 1], emv[0:MB, k, 1:2], eps[0:MB, 0:1], ALU.add).then_inc(e_pool, 1)
                        pool.wait_ge(e_pool, 2 * n + 1)
                        nc.gpsimd.tensor_tensor(ers[0:MB, k:k + 1], eve[0:MB, k:k + 1], half[0:MB, 0:1], ALU.pow).then_inc(e_pool, 1)

            @block.scalar
            def _(act):
                with act.Fori(0, NB) as i:
                    for k in range(2):
                        n = 2 * i + k
                        act.wait_ge(ext_ps, n + 1)
                        nc.scalar.activation(ext[:, k, :, :], XB[:, 0:2 * MB].rearrange("p (k t) -> p k t", k=2), ACT.Copy)\
                            .then_inc(ext_saved, 1)
                        act.wait_ge(hot_ps, n + 1)
                        nc.scalar.activation(hotT[:, k, :], LB[0:NE, 64:64 + MB], ACT.Copy).then_inc(hot_saved, 1)
                        act.wait_ge(acc_step, 9 * n + 9)
                        act.dma_start(out[bass.ds(n * MB, MB), :], acc[0:MB, k, :]).then_inc(e_out[k], 16)
                for k in range(2):
                    act.wait_ge(e_out[k], NB * 16)

            @block.vector
            def _(dve):
                def one(p, k, first):
                    n = 2 * p + k
                    d = 6 * n
                    dve.wait_ge(e_in[k], 16 * p + 16)
                    nc.vector.bn_stats(est[0:MB, k, :], eh[0:MB, k, :]).then_inc(e_dve, 1)
                    dve.drain()
                    nc.vector.bn_aggr(emv[0:MB, k, :], est[0:MB, k, :]).then_inc(e_dve, 1)
                    dve.wait_ge(e_pool, 2 * n + 2)
                    nc.vector.tensor_scalar(exn[0:MB, k, :], eh[0:MB, k, :], emv[0:MB, k, 0:1], ers[0:MB, k:k + 1],
                                            ALU.subtract, ALU.mult).then_inc(e_xn, 1)
                    dve.wait_ge(logit_ps, n + 1)
                    nc.vector.tensor_tensor(logit[0:MB, k, :], LB[0:MB, 0:NE], gate_b[0:MB, :], ALU.add).then_inc(e_dve, 1)
                    dve.drain()
                    nc.vector.max(top[0:MB, k, :], logit[0:MB, k, :]).then_inc(e_dve, 1)
                    dve.drain()
                    nc.vector.max_index(topi[0:MB, k, :], top[0:MB, k, :], logit[0:MB, k, :]).then_inc(e_dve, 1)
                    dve.wait_ge(e_dve, d + 5)
                    nc.vector.tensor_copy(topf[0:MB, k:k + 1], topi[0:MB, k, 0:1]).then_inc(e_dve, 1)
                    dve.wait_ge(e_dve, d + 6)
                    nc.vector.tensor_scalar(hot[0:MB, k, :], iota8[0:MB, :], topf[0:MB, k:k + 1], None, ALU.is_equal).then_inc(hot_done, 1)
                    if not first:
                        dve.wait_ge(e_out[k], 16 * p)
                    dve.wait_ge(bias_ps, n + 1)
                    nc.vector.tensor_tensor(acc[0:MB, k, :], LB[0:MB, 256:512], eh[0:MB, k, :], ALU.add).then_inc(acc_step, 1)
                    for e in range(NE):
                        dve.wait_ge(acc_step, 9 * n + e + 1)
                        dve.wait_ge(expert_ps, 4 * n + e // 2 + 1)
                        nc.vector.scalar_tensor_tensor(out=acc[0:MB, k, :], in0=EBK[e // 2][0:MB, (e % 2) * D:(e % 2 + 1) * D],
                                                       scalar=hot[0:MB, k, e:e + 1], in1=acc[0:MB, k, :],
                                                       op0=ALU.mult, op1=ALU.add).then_inc(acc_step, 1)

                one(0, 0, True)
                one(0, 1, True)
                with dve.Fori(1, NB) as p:
                    for k in range(2):
                        one(p, k, False)

            @block.tensor
            def _(pe):
                mm = nc.tensor.matmul

                def one(n, k, first):
                    pe.wait_ge(e_xn, n + 1)
                    for kk in range(2):
                        last = nc.tensor.transpose(XB[:, kk * MB:(kk + 1) * MB], exn[0:MB, k, kk * P:(kk + 1) * P], ident[0:MB, 0:MB])
                    last.then_inc(ext_ps, 1)
                    pe.wait_ge(ext_saved, n + 1)
                    if not first:
                        pe.wait_ge(acc_step, 9 * (n - 1) + 1)
                    for kk in range(2):
                        last = mm(LB[0:MB, 0:NE], ext[:, k, kk, :], gate_w[:, kk, :], start=(kk == 0), stop=(kk == 1))
                    last.then_inc(logit_ps, 1)
                    for q in range(4):
                        if not first:
                            pe.wait_ge(acc_step, 9 * (n - 1) + 2 * q + 3)
                        for kk in range(2):
                            last = mm(EBK[q][0:MB, :], ext[:, k, kk, :], moe_w[:, kk, 2 * q:2 * q + 2, :],
                                      start=(kk == 0), stop=(kk == 1))
                        last.then_inc(expert_ps, 1)
                    pe.wait_ge(hot_done, n + 1)
                    nc.tensor.transpose(LB[0:NE, 64:64 + MB], hot[0:MB, k, :], ident[0:MB, 0:MB]).then_inc(hot_ps, 1)
                    pe.wait_ge(hot_saved, n + 1)
                    mm(LB[0:MB, 256:512], hotT[:, k, :], moe_b[:, :], start=True, stop=True).then_inc(bias_ps, 1)

                one(0, 0, True)
                one(1, 1, False)
                with pe.Fori(1, NB) as i:
                    for k in range(2):
                        one(2 * i + k, k, False)


def kernel(**inputs):
    import numpy as np
    import concourse.bacc as bacc
    from concourse.bass_utils import run_bass_kernel_spmd

    f32 = np.float32

    def tiles(a):
        return a.reshape(-1, P, a.shape[1]).transpose(1, 0, 2)

    g = {n: np.asarray(a) for n, a in inputs.items()}
    x = g["x"].reshape(B, 3, 14, 16, 14, 16).transpose(0, 1, 3, 5, 2, 4).reshape(TOK_BLOCKS, P, FK, P)
    wkT = g["L0_attn_Wk"].T.reshape(D, NKV, 1, HD)
    heads = lambda a: a.transpose(1, 0, 2).reshape(D, D)
    ew = g["L1_ffn_expert_w"]
    weights = {
        "wtok": tiles(g["L0_tok_W"]),
        "wq": tiles(g["L0_attn_Wq"].T), "wk": tiles(np.concatenate([wkT, wkT], 2).reshape(D, 2 * NKV * HD)),
        "wv": tiles(g["L0_attn_Wv"].T), "wo": tiles(g["L0_attn_Wo"].T),
        "u1": tiles(np.concatenate([g["L0_ffn_U1"]] * 2, 1)), "v1": g["L0_ffn_V1"],
        "b1": g["L0_ffn_b1"].reshape(MF, P).T, "u2": tiles(g["L0_ffn_U2"]),
        "v2": np.concatenate([g["L0_ffn_V2"]] * 2, 0), "b2": np.broadcast_to(g["L0_ffn_b2"], (P, D)),
        "rwq": tiles(heads(g["L1_attn_Wq"])), "rwk": tiles(heads(g["L1_attn_Wk"])), "rwv": tiles(heads(g["L1_attn_Wv"])),
        "gnw": g["L1_attn_gn_weight"].reshape(2, P).T, "gnb": g["L1_attn_gn_bias"].reshape(2, P).T,
        "wout": tiles(g["L1_attn_Wout"]), "gate_w": tiles(g["L1_ffn_gate_w"]),
        "gate_b": np.broadcast_to(g["L1_ffn_gate_b"], (P, NE)),
        "ewT": ew.transpose(2, 0, 1).reshape(4, P, NE, D).transpose(1, 0, 2, 3),
        "ebT": tiles(g["L1_ffn_expert_b"].T), "ow": tiles(g["L1_ffn_out_w"]),
        "ob": np.broadcast_to(g["L1_ffn_out_b"], (NE, D)),
    }

    p, q = np.arange(P)[:, None], np.arange(P)[None, :]
    tri = (q >= p).astype(f32)
    window = (p > np.arange(TW)[None, :]).astype(f32)
    tail = (np.arange(TW)[None, :] >= np.arange(CH[2][1])[:, None]).astype(f32)
    gamma = np.array([1.0 - 2.0 ** (-5 - i // 2) for i in range(NH)])
    chan = np.arange(D)
    power = gamma[chan // 16][:, None] ** np.arange(SP)[None, :]
    parity = (chan // 16 % 2)[:, None, None] == np.arange(2)[None, :, None]
    dec_q = power[:, None, :] * parity / 4.0
    dec_kt = (1.0 / power)[:, 0:2 * P].T.reshape(2, P, D).transpose(1, 0, 2)
    tables = {
        "iota8": np.broadcast_to(np.arange(NE, dtype=f32), (P, NE)), "ident": np.eye(P, dtype=f32),
        "ones": np.ones((P, HD), f32), "half": np.full((P, 3), -0.5, f32), "eps": np.full((P, 3), EPS, f32),
        "pmask": np.concatenate([tri, np.ones((P, P), f32), window, tri], 1), "tmask": tail, "tri": tri,
        "blockdiag": (p // 16 == q // 16).astype(f32), "headavg": (p // 16 == q // 16).astype(f32) / 16,
        "dec_q": dec_q.reshape(2, P, 2, SP).transpose(1, 0, 2, 3), "dec_k": tiles(1.0 / power), "dec_kt": dec_kt,
    }

    nc = bacc.Bacc("TRN2", target_bir_lowering=False, num_devices=1)
    arrays = {}

    def give(name, a):
        a = np.ascontiguousarray(a)
        arrays[name] = a
        return nc.dram_tensor(name, a.shape, mybir.dt.from_np(a.dtype), kind="ExternalInput").ap()

    xT = give("patches", x.transpose(0, 3, 2, 1))
    txt = give("txt_rows", g["txt"].reshape(B * TXT_TOK, D))
    w = {n: give(f"w_{n}", a) for n, a in weights.items()}
    consts = {n: give(f"c_{n}", a.astype(f32)) for n, a in tables.items()}
    out = nc.dram_tensor("out_rows", (B * S, D), F32, kind="ExternalOutput").ap()
    build(nc, xT, txt, consts, w, out)
    r = run_bass_kernel_spmd(nc, [arrays], core_ids=[0])
    return np.asarray(r.results[0]["out_rows"]).reshape(B, S, D)
```

```python
import concourse.bass as bass
from concourse import mybir
from contextlib import ExitStack

F32 = mybir.dt.float32
F32R = mybir.dt.float32r
U32 = mybir.dt.uint32
ALU = mybir.AluOpType
ACT = mybir.ActivationFunctionType

B, IMG_TOK, TXT_TOK, D = 32, 196, 77, 256
S = IMG_TOK + TXT_TOK
SP = S + 1
P = 128
CH = [(0, 128), (128, 128), (256, S - 256)]
PATCH_F = 768
FK = PATCH_F // P
NH, NKV, HD = 16, 4, 64
CAP = 30.0
D_FF, RANK = 1024, 64
MF = D_FF // P
RP = 8
NE, EH = 8, 512
EPS = 1e-5
TOK_BLOCKS = B * IMG_TOK // P
EB = 7
W0 = 402
TW = S + 1 - 256


def build(nc, xT, txt, consts, w, out):
    ctx = ExitStack()
    with ctx:
        def sb(name, shape, dt=F32):
            return ctx.enter_context(nc.sbuf_tensor(name, shape, dt))

        def sem(name):
            return ctx.enter_context(nc.semaphore(name))

        h_img = nc.dram_tensor("h_img", (B * IMG_TOK, D), F32, kind="Internal").ap()
        h_ret = nc.dram_tensor("h_ret", (B * S, D), F32, kind="Internal").ap()

        wq = sb("wq", [P, 2, NH * HD])
        wk = sb("wk", [P, 2, 2 * NKV * HD])
        wv = sb("wv", [P, 2, NKV * HD])
        wo = sb("wo", [P, 8, D])
        u1 = sb("u1", [P, 2, P])
        v1 = sb("v1", [RANK, D_FF])
        b1 = sb("b1", [P, MF])
        u2 = sb("u2", [P, MF, RANK])
        v2 = sb("v2", [P, D])
        b2 = sb("b2", [P, D])
        rwq = sb("rwq", [P, 2, D])
        rwk = sb("rwk", [P, 2, D])
        rwv = sb("rwv", [P, 2, D])
        gnw = sb("gnw", [P, 2])
        gnb = sb("gnb", [P, 2])
        wout = sb("wout", [P, 2, D])
        gate_w = sb("gate_w", [P, 2, NE])
        gate_b = sb("gate_b", [P, NE])
        iota8 = sb("iota8", [P, NE])
        ident = sb("ident", [P, P])
        ones = sb("ones", [P, HD])
        eps = sb("eps", [P, 3])
        half = sb("half", [P, 3])
        pmask = sb("pmask", [P, W0])
        tmask = sb("tmask", [CH[2][1], TW])
        tri = sb("tri", [P, P])
        blockdiag = sb("blockdiag", [P, P])
        headavg = sb("headavg", [P, P])
        dec_q = sb("dec_q", [P, 2, 2, SP])
        dec_k = sb("dec_k", [P, 2, SP])
        dec_kt = sb("dec_kt", [P, 2, D])
        moe_hi = sb("moe_hi", [P, 2, NE, D], F32R)
        moe_lo = sb("moe_lo", [P, 2, NE, D], F32R)
        gate_hi = sb("gate_hi", [P, 2, NE], F32R)
        gate_lo = sb("gate_lo", [P, 2, NE], F32R)
        moe_b = sb("moe_b", [NE, D])

        banks = ctx.enter_context(nc.psum_tensor("banks", [P, 8, 512], F32))
        psum = [banks[:, n, :] for n in range(8)]
        S_BANK, O_BANK, D_BANK, Y = psum[0:2], psum[2], psum[3], psum[4:8]
        QKV_BANK = [psum[0], psum[1], psum[2], psum[3]]

        stage1 = ExitStack()
        with stage1:
            def sb1(name, shape, dt=F32):
                return stage1.enter_context(nc.sbuf_tensor(name, shape, dt))

            patch = sb1("patch", [P, EB, FK, P])
            wtok = sb1("wtok", [P, FK, D])
            emb = sb1("emb", [P, EB, D])
            ewT = sb1("ewT", [P, 4, NE, D])
            ebT = sb1("ebT", [P, 4, NE])
            ow = sb1("ow", [P, 4, D])
            ob = sb1("ob", [NE, D])
            tok_w_in, patch_in, const_in = sem("tok_w_in"), [sem(f"patch_in{k}") for k in range(EB)], sem("const_in")
            emb_ps, emb_saved, emb_out = sem("emb_ps"), sem("emb_saved"), [sem(f"emb_out{k}") for k in range(EB)]
            expert_in, fuse_ps, fuse_hi, fuse_saved = (sem(n) for n in ("expert_in", "fuse_ps", "fuse_hi", "fuse_saved"))
            block = stage1.enter_context(nc.Block())
            n_blocks = TOK_BLOCKS // EB

            loads = [(wq, w["wq"]), (wk, w["wk"]), (wv, w["wv"]), (wo, w["wo"]), (u1, w["u1"]), (v1, w["v1"]),
                     (b1, w["b1"]), (u2, w["u2"]), (v2, w["v2"]), (b2, w["b2"]), (rwq, w["rwq"]), (rwk, w["rwk"]),
                     (rwv, w["rwv"]), (gnw, w["gnw"]), (gnb, w["gnb"]), (wout, w["wout"]), (gate_w, w["gate_w"]),
                     (gate_b, w["gate_b"])]
            loads += [(t, consts[n]) for n, t in (
                ("iota8", iota8), ("ident", ident), ("ones", ones), ("half", half), ("eps", eps), ("pmask", pmask), ("tmask", tmask),
                ("tri", tri), ("blockdiag", blockdiag), ("headavg", headavg), ("dec_q", dec_q), ("dec_k", dec_k),
                ("dec_kt", dec_kt))]

            @block.sync
            def _(sp):
                sp.dma_start(wtok[:], w["wtok"]).then_inc(tok_w_in, 16)
                for k in range(EB):
                    sp.dma_start(patch[:, k], xT[k]).then_inc(patch_in[k], 16)
                with sp.Fori(1, n_blocks) as i:
                    for k in range(EB):
                        sp.wait_ge(emb_ps, (i - 1) * EB + k + 1)
                        sp.dma_start(patch[:, k], xT[bass.ds(i * EB + k, 1)].rearrange("o p k t -> (o p) k t"))\
                            .then_inc(patch_in[k], 16)

            @block.gpsimd
            def _(pool):
                for t, src in loads:
                    pool.dma_start(t[:], src).then_inc(const_in, 16)
                pool.wait_ge(const_in, 16 * len(loads))

            @block.tensor
            def _(pe):
                pe.wait_ge(tok_w_in, 16)

                def embed(i, k, reuse):
                    pe.wait_ge(patch_in[k], (i + 1) * 16)
                    if reuse:
                        pe.wait_ge(emb_saved, (i - 1) * EB + k + 1)
                    for f in range(FK):
                        mm = nc.tensor.matmul(psum[k][:, 0:D], patch[:, k, f, :], wtok[:, f, :],
                                              start=(f == 0), stop=(f == FK - 1))
                    mm.then_inc(emb_ps, 1)

                for k in range(EB):
                    embed(0, k, False)
                with pe.Fori(1, n_blocks) as i:
                    for k in range(EB):
                        embed(i, k, True)
                pe.wait_ge(expert_in, 64)
                pe.wait_ge(emb_saved, TOK_BLOCKS)
                for n in range(2 * NE):
                    e, kd = n // 2, n % 2
                    if n >= 4:
                        pe.wait_ge(fuse_saved, n - 3)
                    for t in range(4):
                        mm = nc.tensor.matmul(psum[n % 4][:, 0:D], ewT[:, t, e, kd * P:(kd + 1) * P], ow[:, t, :],
                                              start=(t == 0), stop=(t == 3))
                    mm.then_inc(fuse_ps, 1)
                for t in range(4):
                    mm = nc.tensor.matmul(psum[4][0:NE, 0:D], ebT[:, t, :], ow[:, t, :], start=(t == 0), stop=(t == 3))
                mm.then_inc(fuse_ps, 1)

            @block.vector
            def _(dve):
                def save(i, k, reuse):
                    dve.wait_ge(emb_ps, i * EB + k + 1)
                    if reuse:
                        dve.wait_ge(emb_out[k], i * 16)
                    nc.vector.tensor_copy(emb[:, k, :], psum[k][:, 0:D]).then_inc(emb_saved, 1)

                for k in range(EB):
                    save(0, k, False)
                with dve.Fori(1, n_blocks) as i:
                    for k in range(EB):
                        save(i, k, True)
                for n in range(2 * NE):
                    dve.wait_ge(fuse_ps, n + 1)
                    nc.vector.tensor_copy(moe_hi[:, n % 2, n // 2, :], psum[n % 4][:, 0:D]).then_inc(fuse_hi, 1)
                    dve.wait_ge(fuse_hi, n + 1)
                    nc.vector.tensor_tensor(moe_lo[:, n % 2, n // 2, :], psum[n % 4][:, 0:D],
                                            moe_hi[:, n % 2, n // 2, :].bitcast(F32), ALU.subtract).then_inc(fuse_saved, 1)
                dve.wait_ge(fuse_ps, 2 * NE + 1)
                dve.wait_ge(expert_in, 64)
                nc.vector.tensor_tensor(moe_b[:, :], psum[4][0:NE, 0:D], ob[:, :], ALU.add).then_inc(fuse_saved, 1)
                dve.wait_ge(const_in, 16 * len(loads))
                nc.vector.tensor_copy(gate_hi[:, :, :], gate_w[:, :, :]).then_inc(fuse_hi, 1)
                dve.wait_ge(fuse_hi, 2 * NE + 1)
                nc.vector.tensor_tensor(gate_lo[:, :, :], gate_w[:, :, :], gate_hi[:, :, :].bitcast(F32), ALU.subtract)\
                    .then_inc(fuse_saved, 1)

            @block.scalar
            def _(act):
                for t, src in ((ewT, w["ewT"]), (ebT, w["ebT"]), (ow, w["ow"]), (ob, w["ob"])):
                    act.dma_start(t[:], src).then_inc(expert_in, 16)
                with act.Fori(0, n_blocks) as i:
                    for k in range(EB):
                        act.wait_ge(emb_saved, i * EB + k + 1)
                        act.dma_start(h_img[bass.ds((i * EB + k) * P, P), :], emb[:, k, :]).then_inc(emb_out[k], 16)
                for k in range(EB):
                    act.wait_ge(emb_out[k], n_blocks * 16)

        stage2 = ExitStack()
        with stage2:
            def sb2(name, shape, dt=F32):
                return stage2.enter_context(nc.sbuf_tensor(name, shape, dt))

            def sem2(name):
                return stage2.enter_context(nc.semaphore(name))

            h_in = sb2("h_in", [P, 3, D])
            h = sb2("h", [P, 3, D])
            h_out = sb2("h_out", [P, 3, D])
            st = {n: sb2(f"ln_st{n}", [P, 3, 6]) for n in (1, 2, 3)}
            mv = {n: sb2(f"ln_mv{n}", [P, 3, 2]) for n in (1, 2, 3)}
            ve = {n: sb2(f"ln_ve{n}", [P, 3]) for n in (1, 2, 3)}
            rs = {n: sb2(f"ln_rs{n}", [P, 3]) for n in (1, 2, 3)}
            xn = {n: sb2(f"xn{n}", [P, 3, D]) for n in (1, 2, 3)}
            xt = {n: sb2(f"xt{n}", [P, 2, SP]) for n in (1, 2, 3)}
            qt = sb2("qt", [P, 8, SP])
            kt = sb2("kt", [P, NKV, SP])
            v = sb2("v", [P, 3, NKV * HD])
            capped = sb2("capped", [P, 2, 420])
            probs = sb2("probs", [P, 4, 420])
            tail_t = sb2("tail_t", [CH[2][1], 2, NH // 2, TW])
            tail_p = sb2("tail_p", [CH[2][1], 2, NH // 2, TW])
            inv_den = sb2("inv_den", [P, SP])
            ot = sb2("ot", [P, 8, SP])
            pt = sb2("pt", [P, SP])
            gelu = sb2("gelu", [P, MF, SP])
            qf = sb2("qf", [P, SP])
            rq = sb2("rq", [P, 2, 2, SP])
            rk = sb2("rk", [P, 2, SP])
            rkt = sb2("rkt", [P, 2, D])
            rv = sb2("rv", [P, 3, RP, 2, 32])
            state = sb2("state", [P, 4, P])
            rs_sb = sb2("rs_sb", [P, 2, 4, 2, 2, P])
            ct = sb2("ct", [P, 2, SP])
            cn = sb2("cn", [P, 2, SP])
            gst = sb2("gst", [P, 2, 6])
            gmv = sb2("gmv", [P, 2, 2])
            gsq = sb2("gsq", [P, 2])
            gm = sb2("gm", [P, 2, 2])
            gmm = sb2("gmm", [P, 2])
            gvar = sb2("gvar", [P, 2])
            gve = sb2("gve", [P, 2])
            grs = sb2("grs", [P, 2])
            gsc = sb2("gsc", [P, 2])
            gms = sb2("gms", [P, 2])
            gbi = sb2("gbi", [P, 2])

            zeroed = sem2("zeroed")
            hin_in = sem2("hin_in")
            h_in_dma = sem2("h_in_dma")
            hout_dma = sem2("hout_dma")
            ln_mv = {n: sem2(f"ln_mv_done{n}") for n in (1, 2, 3)}
            ln_rs = {n: sem2(f"ln_rs_done{n}") for n in (1, 2, 3)}
            xn_done = {n: sem2(f"xn_done{n}") for n in (1, 2, 3)}
            xt_ps = {n: sem2(f"xt_ps{n}") for n in (1, 2, 3)}
            xt_act = {n: sem2(f"xt_act{n}") for n in (1, 2, 3)}
            xt_dve = {n: sem2(f"xt_dve{n}") for n in (1, 2, 3)}
            oproj_ps, att_added = sem2("oproj_ps"), sem2("att_added")
            qkv_ps, qkv_act, qkv_dve = sem2("qkv_ps"), sem2("qkv_act"), sem2("qkv_dve")
            tail_ps, tail_act, tail_done = sem2("tail_ps"), sem2("tail_act"), sem2("tail_done")
            score_ps, cap_done, exp_done, prob_done = (sem2(n) for n in ("score_ps", "cap_done", "exp_done", "prob_done"))
            pv_ps, inv_done, ot_done = sem2("pv_ps"), sem2("inv_done"), sem2("ot_done")
            p_ps, p_saved = sem2("p_ps"), sem2("p_saved")
            ff_ps, gelu_done = sem2("ff_ps"), sem2("gelu_done")
            qf_ps, qf_saved = sem2("qf_ps"), sem2("qf_saved")
            b2_added, ffo_ps, ffn_added = sem2("b2_added"), sem2("ffo_ps"), sem2("ffn_added")
            rq_ps, rq_saved = sem2("rq_ps"), sem2("rq_saved")
            rk_ps, rk_saved = sem2("rk_ps"), sem2("rk_saved")
            rv_ps, rv_saved = sem2("rv_ps"), sem2("rv_saved")
            rkt_ps, rkt_saved = sem2("rkt_ps"), sem2("rkt_saved")
            state_ps, state_saved = sem2("state_ps"), sem2("state_saved")
            rs_ps, rs_masked = sem2("rs_ps"), sem2("rs_masked")
            rpv_ps, ct_saved = sem2("rpv_ps"), sem2("ct_saved")
            gn_ps, gn_dve, gn_pool, cn_done = sem2("gn_ps"), sem2("gn_dve"), sem2("gn_pool"), sem2("cn_done")
            wo_ps, ret_added = sem2("wo_ps"), sem2("ret_added")

            XT_BANK = {1: (Y[3], Y[0]), 2: (Y[0], Y[1]), 3: (Y[1], Y[2])}
            RV_BANK = (Y[3], Y[0], Y[1])

            def qkv_target(u):
                bank = QKV_BANK[u % 4]
                if u < 8:
                    return qt[:, u, :], bank[:, 0:SP]
                if u < 12:
                    return kt[:, u - 8, :], bank[:, 0:SP]
                n = CH[u - 12][1]
                return v[0:n, u - 12, :], bank[0:n, 0:NKV * HD]

            RQ_BANK, RK_BANK, RKT_BANK = (Y[3], Y[0]), (Y[1], Y[2]), (Y[2], Y[3])
            RS_AT = {9: (0, 1), 10: (2, 3), 11: (4, 5), 12: (6, 7, 8)}

            def RS_BANK(u):
                return Y[1 + u % 3]

            block = stage2.enter_context(nc.Block())

            def turns(eng, turn):
                turn(0, False, True)
                turn(1, True, True)
                with eng.Fori(2, B - 1) as i:
                    turn(i, True, True)
                turn(B - 1, True, False)
                turn(B, True, None)

            @block.sync
            def _(sp):
                def load(dst, n, s):
                    r = n * IMG_TOK
                    t = n * TXT_TOK
                    k = IMG_TOK - P
                    sp.dma_start(dst[:, 0, :], h_img[bass.ds(r, P), :]).then_inc(s, 16)
                    sp.dma_start(dst[0:k, 1, :], h_img[bass.ds(r + P, k), :]).then_inc(s, 16)
                    sp.dma_start(dst[k:P, 1, :], txt[bass.ds(t, P - k), :]).then_inc(s, 16)
                    sp.dma_start(dst[0:CH[2][1], 2, :], txt[bass.ds(t + P - k, CH[2][1]), :]).then_inc(s, 16)

                def turn(i, prev, nxt):
                    if nxt:
                        sp.wait_ge(xn_done[1], 3 * i + 3)
                        load(h_in, i + 1, hin_in)
                    if nxt is not None:
                        if prev:
                            sp.wait_ge(ret_added, 3 * (i - 1) + 3)
                            store(i - 1)
                        load(h, i, h_in_dma)
                    else:
                        sp.wait_ge(ret_added, 3 * (i - 1) + 3)
                        store(i - 1)

                def store(n):
                    sp.dma_start(h_ret[bass.ds(n * S, 2 * P), :].rearrange("(c p) d -> p c d", p=P), h_out[:, 0:2, :])\
                        .then_inc(hout_dma, 16)
                    sp.dma_start(h_ret[bass.ds(n * S + 2 * P, CH[2][1]), :], h_out[0:CH[2][1], 2, :]).then_inc(hout_dma, 16)

                load(h_in, 0, hin_in)
                turns(sp, turn)
                sp.wait_ge(hout_dma, 32 * B)

            @block.gpsimd
            def _(pool):
                def ln_pow(n, e):
                    pool.wait_ge(ln_mv[n], 3 * e + 3)
                    nc.gpsimd.tensor_tensor(ve[n][:, :], mv[n][:, :, 1], eps[:, :], ALU.add).then_inc(ln_rs[n], 1)
                    pool.wait_ge(ln_rs[n], 2 * e + 1)
                    nc.gpsimd.tensor_tensor(rs[n][:, :], ve[n][:, :], half[:, :], ALU.pow).then_inc(ln_rs[n], 1)

                def turn(i, prev, nxt):
                    a = i - 1
                    if prev:
                        ln_pow(2, a)
                    if nxt is not None:
                        pool.wait_ge(tail_act, 2 * i + 2)
                        nc.gpsimd.tensor_tensor(tail_p[:, :, :, :].rearrange("p e h q -> p (e h) q"),
                                                tail_p[:, :, :, :].rearrange("p e h q -> p (e h) q"),
                                                tmask[:, None, :].to_broadcast([CH[2][1], NH, TW]), ALU.mult).then_inc(tail_done, 1)
                    for hh in range(NH):
                        if nxt is not None:
                            pool.wait_ge(exp_done, NH * i + hh + 1)
                            nc.gpsimd.tensor_tensor(probs[:, hh % 4, 0:W0], probs[:, hh % 4, 0:W0], pmask[:, :], ALU.mult)\
                                .then_inc(prob_done, 1)
                        if hh == 0 and prev:
                            pool.wait_ge(xn_done[2], 3 * a + 3)
                            nc.gpsimd.tensor_tensor(h[:, 0:2, :], h[:, 0:2, :], b2[:, None, :].to_broadcast([P, 2, D]), ALU.add)\
                                .then_inc(b2_added, 1)
                            nc.gpsimd.tensor_tensor(h[0:CH[2][1], 2, :], h[0:CH[2][1], 2, :], b2[0:CH[2][1], :], ALU.add)\
                                .then_inc(b2_added, 1)
                        if hh == 3 and nxt:
                            ln_pow(1, i + 1)
                        if hh == 5 and prev:
                            ln_pow(3, a)
                        if hh == 14 and prev:
                            pool.wait_ge(gn_dve, 12 * a + 9)
                            nc.gpsimd.tensor_tensor(gve[:, :], gvar[:, :], eps[:, 0:2], ALU.add).then_inc(gn_pool, 1)
                            pool.wait_ge(gn_pool, 2 * a + 1)
                            nc.gpsimd.tensor_tensor(grs[:, :], gve[:, :], half[:, 0:2], ALU.pow).then_inc(gn_pool, 1)

                pool.wait_ge(zeroed, 8)
                ln_pow(1, 0)
                turns(pool, turn)

            @block.scalar
            def _(act):
                def ln_evac(n, e):
                    act.wait_ge(xt_ps[n], 2 * e + 1)
                    nc.scalar.activation(xt[n][:, 0, 0:S], XT_BANK[n][0][:, 0:S], ACT.Copy).then_inc(xt_act[n], 1)

                def turn(i, prev, nxt):
                    a = i - 1
                    if nxt is not None:
                        for u in range(0, 15, 2):
                            act.wait_ge(qkv_ps, 15 * i + u + 1)
                            dst, src = qkv_target(u)
                            nc.scalar.activation(dst, src, ACT.Copy).then_inc(qkv_act, 1)
                        act.wait_ge(tail_ps, i + 1)
                        nc.scalar.activation(tail_t[:, :, :, :], banks[0:CH[2][1], 2:4, 0:NH // 2 * TW].rearrange("p e (h q) -> p e h q", q=TW),
                                             ACT.Tanh, scale=HD ** -0.5 / CAP).then_inc(tail_act, 1)
                        act.wait_ge(tail_act, 2 * i + 1)
                        nc.scalar.activation(tail_p[:, :, :, :], tail_t[:, :, :, :], ACT.Exp, scale=CAP).then_inc(tail_act, 1)
                    for hh in range(NH):
                        if nxt is not None:
                            act.wait_ge(score_ps, NH * i + hh + 1)
                            nc.scalar.activation(capped[:, hh % 2, :], S_BANK[hh % 2][:, 0:420], ACT.Tanh,
                                                 scale=HD ** -0.5 / CAP).then_inc(cap_done, 1)
                            act.wait_ge(cap_done, NH * i + hh + 1)
                            if hh >= 4:
                                act.wait_ge(pv_ps, NH * i + hh - 3)
                            nc.scalar.activation(probs[:, hh % 4, :], capped[:, hh % 2, :], ACT.Exp, scale=CAP)\
                                .then_inc(exp_done, 1)
                        if prev:
                            rest(hh, a)
                        if hh == 5 and nxt:
                            ln_evac(1, i + 1)

                def rest(hh, a):
                    if hh == 0:
                        ln_evac(2, a)
                        act.wait_ge(p_ps, a + 1)
                        nc.scalar.activation(pt[:, :], Y[2][:, 0:SP], ACT.Copy).then_inc(p_saved, 1)
                    if hh in (1, 2):
                        for m in range(4 * hh - 4, 4 * hh):
                            act.wait_ge(ff_ps, MF * a + m + 1)
                            nc.scalar.activation(gelu[:, m, :], Y[(3 + m) % 4][:, 0:SP], ACT.Gelu_apprx_tanh,
                                                 bias=b1[:, m:m + 1]).then_inc(gelu_done, 1)
                    if hh == 7:
                        ln_evac(3, a)
                    if hh == 8:
                        for c, (_, n) in enumerate(CH):
                            act.wait_ge(rv_ps, 3 * a + c + 1)
                            for e in range(2):
                                cp = nc.scalar.activation(
                                    rv[0:n, c, :, e, 16 * e:16 * e + 16],
                                    RV_BANK[c][0:n, 0:D].rearrange("p (r e d) -> p r e d", e=2, d=16)[:, :, e, :], ACT.Copy)
                            cp.then_inc(rv_saved, 1)
                    if hh in (11, 12, 13):
                        c = hh - 11
                        t, n = CH[c]
                        act.wait_ge(rpv_ps, 3 * a + c + 1)
                        nc.scalar.activation(ct[:, :, t:t + n], Y[0][:, :].rearrange("p (m q) -> p m q", m=2)[:, :, 0:n],
                                             ACT.Copy).then_inc(ct_saved, 1)
                    if hh == 14:
                        act.wait_ge(gn_dve, 12 * a + 12)
                        for m in range(2):
                            nc.scalar.activation(cn[:, m, 0:S], ct[:, m, 0:S], ACT.Identity,
                                                 scale=gsc[:, m:m + 1], bias=gbi[:, m:m + 1]).then_inc(cn_done, 1)

                act.wait_ge(zeroed, 8)
                ln_evac(1, 0)
                turns(act, turn)

            @block.vector
            def _(dve):
                for t in (xt[1][:, :, S:SP], xt[2][:, :, S:SP], xt[3][:, :, S:SP], rv[:, :, :, :, :], mv[1][:, :, :], mv[2][:, :, :],
                          mv[3][:, :, :], ct[:, :, :]):
                    nc.vector.memset(t, 0.0).then_inc(zeroed, 1)

                def ln_stats(n, e, src):
                    for c, (_, r) in enumerate(CH):
                        nc.vector.bn_stats(st[n][0:r, c, :], src[0:r, c, :])
                    dve.drain()
                    for c, (_, r) in enumerate(CH):
                        nc.vector.bn_aggr(mv[n][0:r, c, :], st[n][0:r, c, :]).then_inc(ln_mv[n], 1)

                def ln_apply(n, e, src):
                    dve.wait_ge(ln_rs[n], 2 * e + 2)
                    for c, (_, r) in enumerate(CH):
                        nc.vector.tensor_scalar(xn[n][0:r, c, :], src[0:r, c, :], mv[n][0:r, c, 0:1], rs[n][0:r, c:c + 1],
                                                ALU.subtract, ALU.mult).then_inc(xn_done[n], 1)

                def ln_evac(n, e):
                    dve.wait_ge(xt_ps[n], 2 * e + 2)
                    nc.vector.tensor_copy(xt[n][:, 1, 0:S], XT_BANK[n][1][:, 0:S]).then_inc(xt_dve[n], 1)

                def turn(i, prev, nxt):
                    a = i - 1
                    if prev:
                        dve.wait_ge(h_in_dma, 64 * a + 64)
                        for c, (_, r) in enumerate(CH):
                            dve.wait_ge(oproj_ps, 3 * a + c + 1)
                            nc.vector.tensor_tensor(h[0:r, c, :], Y[c][0:r, 0:D], h[0:r, c, :], ALU.add).then_inc(att_added, 1)
                        dve.wait_ge(att_added, 3 * a + 3)
                        ln_stats(2, a, h)
                    if nxt is not None:
                        for u in range(1, 15, 2):
                            if u == 5 and prev:
                                ln_apply(2, a, h)
                            dve.wait_ge(qkv_ps, 15 * i + u + 1)
                            dst, src = qkv_target(u)
                            nc.vector.tensor_copy(dst, src).then_inc(qkv_dve, 1)
                    elif prev:
                        ln_apply(2, a, h)
                    for hh in range(NH):
                        if prev:
                            rest(hh, a)
                        if nxt:
                            if hh == 3:
                                dve.wait_ge(hin_in, 64 * (i + 1) + 64)
                                ln_stats(1, i + 1, h_in)
                            if hh == 4:
                                ln_apply(1, i + 1, h_in)
                            if hh == 5:
                                ln_evac(1, i + 1)
                        if nxt is not None and hh % 2:
                            j = hh // 2
                            dve.wait_ge(pv_ps, NH * i + hh + 1)
                            nc.vector.reciprocal(inv_den[:, :], D_BANK[:, 0:SP]).then_inc(inv_done, 1)
                            dve.wait_ge(inv_done, 8 * i + j + 1)
                            nc.vector.tensor_tensor(ot[:, j, :], O_BANK[:, 0:SP], inv_den[:, :], ALU.mult).then_inc(ot_done, 1)

                def rest(hh, a):
                    if hh == 0:
                        ln_evac(2, a)
                    if hh == 3:
                        dve.wait_ge(qf_ps, a + 1)
                        nc.vector.tensor_copy(qf[:, :], Y[3][:, 0:SP]).then_inc(qf_saved, 1)
                    if hh == 4:
                        dve.wait_ge(b2_added, 2 * a + 2)
                        for c, (_, r) in enumerate(CH):
                            dve.wait_ge(ffo_ps, 3 * a + c + 1)
                            nc.vector.tensor_tensor(h[0:r, c, :], Y[c][0:r, 0:D], h[0:r, c, :], ALU.add).then_inc(ffn_added, 1)
                    if hh == 5:
                        dve.wait_ge(ffn_added, 3 * a + 3)
                        ln_stats(3, a, h)
                    if hh == 6:
                        ln_apply(3, a, h)
                    if hh == 7:
                        ln_evac(3, a)
                        for m in range(2):
                            dve.wait_ge(rq_ps, 2 * a + m + 1)
                            for e in range(2):
                                nc.vector.tensor_tensor(rq[:, m, e, :], RQ_BANK[m][:, 0:SP], dec_q[:, m, e, :], ALU.mult)\
                                    .then_inc(rq_saved, 1)
                        for m in range(2):
                            dve.wait_ge(rk_ps, 2 * a + m + 1)
                            nc.vector.tensor_tensor(rk[:, m, :], RK_BANK[m][:, 0:SP], dec_k[:, m, :], ALU.mult).then_inc(rk_saved, 1)
                    if hh == 8:
                        for c in range(2):
                            dve.wait_ge(rkt_ps, 2 * a + c + 1)
                            nc.vector.tensor_tensor(rkt[:, c, :], RKT_BANK[c][:, 0:D], dec_kt[:, c, :], ALU.mult).then_inc(rkt_saved, 1)
                    if hh == 9:
                        dve.wait_ge(state_ps, a + 1)
                        nc.vector.tensor_tensor(state[:, :, :], Y[0][:, :].rearrange("p (n q) -> p n q", n=4),
                                                blockdiag[:, None, :].to_broadcast([P, 4, P]), ALU.mult).then_inc(state_saved, 1)
                    for u in RS_AT.get(hh, ()):
                        dve.wait_ge(rs_ps, 9 * a + u + 1)
                        c = u // 4
                        n = CH[c][1]
                        if u == 8:
                            dve.wait_ge(rpv_ps, 3 * a + 1)
                            nc.vector.tensor_tensor(
                                rs_sb[0:n, 0].rearrange("p r m e q -> p (r m e) q")[:, :, 0:n], RS_BANK(u)[0:n, 0:16 * n].rearrange("p (h q) -> p h q", q=n),
                                tri[0:n, None, 0:n].to_broadcast([n, NH, n]), ALU.mult).then_inc(rs_masked, 1)
                        else:
                            nc.vector.tensor_tensor(
                                rs_sb[:, c, u % 4, :, :, :], RS_BANK(u)[:, :].rearrange("p (m e q) -> p m e q", m=2, e=2),
                                tri[:, None, None, :].to_broadcast([P, 2, 2, P]), ALU.mult).then_inc(rs_masked, 1)
                    if hh == 14:
                        g = 12 * a
                        dve.wait_ge(ct_saved, 3 * a + 3)
                        for m in range(2):
                            nc.vector.bn_stats(gst[:, m, :], ct[:, m, 0:S]).then_inc(gn_dve, 1)
                        dve.drain()
                        for m in range(2):
                            nc.vector.bn_aggr(gmv[:, m, :], gst[:, m, :]).then_inc(gn_dve, 1)
                        dve.wait_ge(gn_dve, g + 4)
                        nc.vector.tensor_tensor(gsq[:, :], gmv[:, :, 0], gmv[:, :, 0], ALU.mult).then_inc(gn_dve, 1)
                        dve.wait_ge(gn_dve, g + 5)
                        nc.vector.tensor_tensor(gmv[:, :, 1], gsq[:, :], gmv[:, :, 1], ALU.add).then_inc(gn_dve, 1)
                        dve.wait_ge(gn_ps, a + 1)
                        nc.vector.tensor_copy(gm[:, :, :], Y[0][:, 0:4].rearrange("p (m s) -> p m s", m=2)).then_inc(gn_dve, 1)
                        dve.wait_ge(gn_dve, g + 7)
                        nc.vector.tensor_tensor(gmm[:, :], gm[:, :, 0], gm[:, :, 0], ALU.mult).then_inc(gn_dve, 1)
                        dve.wait_ge(gn_dve, g + 8)
                        nc.vector.tensor_tensor(gvar[:, :], gm[:, :, 1], gmm[:, :], ALU.subtract).then_inc(gn_dve, 1)
                        dve.wait_ge(gn_pool, 2 * a + 2)
                        nc.vector.tensor_tensor(gsc[:, :], grs[:, :], gnw[:, :], ALU.mult).then_inc(gn_dve, 1)
                        dve.wait_ge(gn_dve, g + 10)
                        nc.vector.tensor_tensor(gms[:, :], gm[:, :, 0], gsc[:, :], ALU.mult).then_inc(gn_dve, 1)
                        dve.wait_ge(gn_dve, g + 11)
                        nc.vector.tensor_tensor(gbi[:, :], gnb[:, :], gms[:, :], ALU.subtract).then_inc(gn_dve, 1)
                    if hh == 15:
                        if not isinstance(a, int) or a > 0:
                            dve.wait_ge(hout_dma, 32 * a)
                        for c, (_, r) in enumerate(CH):
                            dve.wait_ge(wo_ps, 3 * a + c + 1)
                            nc.vector.tensor_tensor(h_out[0:r, c, :], Y[1 + c][0:r, 0:D], h[0:r, c, :], ALU.add).then_inc(ret_added, 1)

                dve.wait_ge(zeroed, 8)
                dve.wait_ge(hin_in, 64)
                ln_stats(1, 0, h_in)
                ln_apply(1, 0, h_in)
                ln_evac(1, 0)
                turns(dve, turn)

            @block.tensor
            def _(pe):
                mm = nc.tensor.matmul

                def ln_transpose(n, e):
                    pe.wait_ge(xn_done[n], 3 * e + 3)
                    for k in range(2):
                        for c, (t, r) in enumerate(CH):
                            last = nc.tensor.transpose(XT_BANK[n][k][:, t:t + r], xn[n][0:r, c, k * P:(k + 1) * P], ident[0:r, 0:r])
                        last.then_inc(xt_ps[n], 1)

                def xt_ready(n, e):
                    pe.wait_ge(xt_act[n], e + 1)
                    pe.wait_ge(xt_dve[n], e + 1)

                def scores(i, hh):
                    g, j, s = hh // 4, hh // 2, 64 * (hh % 2)
                    if hh >= 2:
                        pe.wait_ge(cap_done, NH * i + hh - 1)
                    mm(S_BANK[hh % 2][:, 0:SP], kt[s:s + 64, g, 0:P], qt[s:s + 64, j, :], start=True, stop=True)
                    mm(S_BANK[hh % 2][:, SP:420], kt[s:s + 64, g, P:2 * P], qt[s:s + 64, j, P:SP], start=True, stop=True)\
                        .then_inc(score_ps, 1)

                def weighted(i, hh):
                    g, s = hh // 4, 64 * (hh % 2)
                    if hh == 0:
                        pe.wait_ge(tail_done, i + 1)
                    elif hh % 2 == 0:
                        pe.wait_ge(ot_done, 8 * i + hh // 2)
                    pe.wait_ge(prob_done, NH * i + hh + 1)
                    for bank, lhs in ((O_BANK, v), (D_BANK, None)):
                        for c, (t, r) in enumerate(CH):
                            left = ones[0:r, :] if lhs is None else v[0:r, c, 64 * g:64 * g + 64]
                            right = (probs[:, hh % 4, 0:SP], probs[:, hh % 4, SP:420], tail_p[:, hh % 2, hh // 2, :])[c]
                            last = mm(bank[s:s + 64, t:SP], left, right, start=(c == 0), stop=(c == 2))
                    last.then_inc(pv_ps, 1)

                def turn(i, prev, nxt):
                    a = i - 1
                    if prev:
                        pe.wait_ge(ot_done, 8 * a + 8)
                        if not isinstance(i, int) or i > 1:
                            pe.wait_ge(ret_added, 3 * a)
                        for c, (t, r) in enumerate(CH):
                            for j in range(8):
                                last = mm(Y[c][0:r, 0:D], ot[:, j, t:t + r], wo[:, j, :], start=(j == 0), stop=(j == 7))
                            last.then_inc(oproj_ps, 1)
                    if nxt is not None:
                        xt_ready(1, i)
                        for u in range(15):
                            if u >= 4:
                                pe.wait_ge(qkv_dve if u % 2 else qkv_act, (7 if u % 2 else 8) * i + (u - 4) // 2 + 1)
                            dst = qkv_target(u)[1]
                            for k in range(2):
                                if u < 8:
                                    last = mm(dst, wq[:, k, u * P:(u + 1) * P], xt[1][:, k, :], start=(k == 0), stop=(k == 1))
                                elif u < 12:
                                    last = mm(dst, wk[:, k, (u - 8) * P:(u - 7) * P], xt[1][:, k, :], start=(k == 0), stop=(k == 1))
                                else:
                                    t, r = CH[u - 12]
                                    last = mm(dst, xt[1][:, k, t:t + r], wv[:, k, :], start=(k == 0), stop=(k == 1))
                            last.then_inc(qkv_ps, 1)
                        pe.wait_ge(qkv_act, 8 * i + 8)
                        pe.wait_ge(qkv_dve, 7 * i + 7)
                        scores(i, 0)
                        t, r = CH[2]
                        for hh in range(NH):
                            s = 64 * (hh % 2)
                            last = mm(psum[2 + hh % 2][0:r, hh // 2 * TW:(hh // 2 + 1) * TW], kt[s:s + 64, hh // 4, t:t + r],
                                      qt[s:s + 64, hh // 2, t:SP], start=True, stop=True)
                        last.then_inc(tail_ps, 1)
                    for hh in range(NH):
                        if nxt is not None and hh < NH - 1:
                            scores(i, hh + 1)
                        if prev:
                            rest(hh, a)
                        if hh == 5 and nxt:
                            if prev:
                                pe.wait_ge(ffn_added, 3 * a + 1)
                            ln_transpose(1, i + 1)
                        if hh == 7 and prev:
                            if nxt:
                                xt_ready(1, i + 1)
                            retention_in(a)
                        if nxt is not None:
                            weighted(i, hh)

                def rest(hh, a):
                    if hh == 0:
                        ln_transpose(2, a)
                        xt_ready(2, a)
                        for k in range(2):
                            last = mm(Y[2][:, 0:SP], u1[:, k, :], xt[2][:, k, :], start=(k == 0), stop=(k == 1))
                        last.then_inc(p_ps, 1)
                        pe.wait_ge(p_saved, a + 1)
                    if hh in (1, 2):
                        for m in range(4 * hh - 4, 4 * hh):
                            if m >= 4:
                                pe.wait_ge(gelu_done, MF * a + m - 3)
                            mm(Y[(3 + m) % 4][:, 0:SP], v1[:, m * P:(m + 1) * P], pt[0:RANK, :], start=True, stop=True)\
                                .then_inc(ff_ps, 1)
                    if hh == 3:
                        pe.wait_ge(gelu_done, MF * a + MF)
                        for m in range(MF):
                            s = 64 * (m % 2)
                            last = mm(Y[3][s:s + 64, 0:SP], u2[:, m, :], gelu[:, m, :], start=(m < 2), stop=(m >= MF - 2))
                        last.then_inc(qf_ps, 1)
                    if hh == 4:
                        pe.wait_ge(qf_saved, a + 1)
                        for c, (t, r) in enumerate(CH):
                            mm(Y[c][0:r, 0:D], qf[:, t:t + r], v2[:, :], start=True, stop=True).then_inc(ffo_ps, 1)
                    if hh == 8:
                        for c, (t, r) in enumerate(CH):
                            if c < 2:
                                pe.wait_ge(rq_saved, 4 * a + 2 * c + 2)
                            else:
                                pe.wait_ge(rk_saved, 2 * a + 1)
                            for k in range(2):
                                last = mm(RV_BANK[c][0:r, 0:D], xt[3][:, k, t:t + r], rwv[:, k, :], start=(k == 0), stop=(k == 1))
                            last.then_inc(rv_ps, 1)
                        for c in range(2):
                            if c == 0:
                                pe.wait_ge(rk_saved, 2 * a + 2)
                            else:
                                pe.wait_ge(rv_saved, 3 * a + 1)
                            t, r = CH[c]
                            for k in range(2):
                                last = mm(RKT_BANK[c][0:r, 0:D], xt[3][:, k, t:t + r], rwk[:, k, :], start=(k == 0), stop=(k == 1))
                            last.then_inc(rkt_ps, 1)
                    if hh == 9:
                        pe.wait_ge(rkt_saved, 2 * a + 2)
                        pe.wait_ge(rv_saved, 3 * a + 3)
                        for c in range(2):
                            for m in range(2):
                                n = 2 * c + m
                                last = mm(Y[0][:, n * P:(n + 1) * P], rkt[:, c, m * P:(m + 1) * P], heads_of(c, m), start=True, stop=True)
                        last.then_inc(state_ps, 1)
                    for u in RS_AT.get(hh, ()):
                        if 3 <= u < 7:
                            pe.wait_ge(rs_masked, 9 * a + u - 2)
                        if u == 7:
                            pe.wait_ge(rs_masked, 9 * a + 6)
                        c = u // 4
                        t, r = CH[c]
                        pairs = [pr + 4 * m for pr in range(4) for m in range(2)] if u == 8 else (u % 4, u % 4 + 4)
                        for n, pr in enumerate(pairs):
                            m, q = pr // 4, 32 * (pr % 4)
                            if n in (2, 4, 6):
                                pe.drain()
                            last = mm(RS_BANK(u)[0:r, 2 * r * n:2 * r * (n + 1)].rearrange("p (e q) -> p e q", e=2),
                                      rk[q:q + 32, m, t:t + r], rq[q:q + 32, m, :, t:t + r], start=True, stop=True)
                        last.then_inc(rs_ps, 1)
                    if hh in (11, 12, 13):
                        retained(hh - 11, a)
                    if hh == 14:
                        pe.wait_ge(ct_saved, 3 * a + 3)
                        pe.wait_ge(gn_dve, 12 * a + 6)
                        mm(Y[0][:, 0:4], headavg[:, :], gmv[:, :, :].rearrange("p m s -> p (m s)"), start=True, stop=True)\
                            .then_inc(gn_ps, 1)
                    if hh == 15:
                        pe.wait_ge(cn_done, 2 * a + 2)
                        for c, (t, r) in enumerate(CH):
                            for m in range(2):
                                last = mm(Y[1 + c][0:r, 0:D], cn[:, m, t:t + r], wout[:, m, :], start=(m == 0), stop=(m == 1))
                            last.then_inc(wo_ps, 1)

                def heads_of(c, m):
                    full = rv[:, c, 4 * m:4 * m + 4, :, :].rearrange("p r e d -> p r (e d)")
                    return bass.AP(full.tensor, full.offset, [list(full.ap[0]), [64, 4], [48, 2], [1, 16]])

                def retention_in(a):
                    ln_transpose(3, a)
                    xt_ready(3, a)
                    for bank, weight, s in ((RQ_BANK, rwq, rq_ps), (RK_BANK, rwk, rk_ps)):
                        for m in range(2):
                            for k in range(2):
                                last = mm(bank[m][:, 0:SP], weight[:, k, m * P:(m + 1) * P], xt[3][:, k, :],
                                          start=(k == 0), stop=(k == 1))
                            last.then_inc(s, 1)

                def retained(c, a):
                    t, r = CH[c]
                    if c == 0:
                        pe.wait_ge(state_saved, a + 1)
                    else:
                        pe.wait_ge(ct_saved, 3 * a + c)
                    pe.wait_ge(rs_masked, 9 * a + (4, 8, 9)[c])
                    for m in range(2):
                        o = m * D
                        for cc in range(c):
                            for e in range(2):
                                mm(Y[0][:, o:o + r], state[:, 2 * cc + m, :], rq[:, m, e, t:t + r],
                                   start=(cc == 0 and e == 0), stop=False, skip_group_check=True)
                        for q in range(4):
                            pr = 4 * m + q
                            for e in range(2):
                                last = mm(Y[0][32 * q:32 * q + 32, o:o + r], rv[0:r, c, pr, e, :], rs_sb[0:r, c % 2, q, m, e, 0:r],
                                          start=(c == 0 and e == 0), stop=(e == 1), skip_group_check=True)
                    last.then_inc(rpv_ps, 1)

                pe.wait_ge(zeroed, 8)
                ln_transpose(1, 0)
                turns(pe, turn)

        stage3 = ExitStack()
        with stage3:
            def sb3(name, shape, dt=F32):
                return stage3.enter_context(nc.sbuf_tensor(name, shape, dt))

            def sem3(name):
                return stage3.enter_context(nc.semaphore(name))

            eh = sb3("eh", [P, 2, D])
            est = sb3("est", [P, 2, 6])
            emv = sb3("emv", [P, 2, 2])
            eve = sb3("eve", [P, 2])
            ers = sb3("ers", [P, 2])
            exn = sb3("exn", [P, 2, D])
            ext_hi = sb3("ext_hi", [P, 2, 2, P], F32R)
            ext_lo = sb3("ext_lo", [P, 2, 2, P], F32R)
            logit = sb3("logit", [P, 2, NE])
            top = sb3("top", [P, 2, NE])
            topi = sb3("topi", [P, 2, NE], U32)
            topf = sb3("topf", [P, 2])
            hot = sb3("hot", [P, 2, NE])
            hotT = sb3("hotT", [NE, 2, P])
            acc = sb3("acc", [P, 2, D])
            e_in, e_out = ([sem3(f"{n}{k}") for k in range(2)] for n in ("e_in", "e_out"))
            e_mv, e_rs, e_xn = sem3("e_mv"), sem3("e_rs"), sem3("e_xn")
            ext_ps, hi_saved, lo_saved = sem3("ext_ps"), sem3("hi_saved"), sem3("lo_saved")
            logit_ps, gated, hot_done = sem3("logit_ps"), sem3("gated"), sem3("hot_done")
            hot_ps, hot_saved, bias_ps = sem3("hot_ps"), sem3("hot_saved"), sem3("bias_ps")
            expert_ps, acc_step = sem3("expert_ps"), sem3("acc_step")
            block = stage3.enter_context(nc.Block())
            XB, LB, HB, BB, EBK = psum[0], psum[1], psum[2], psum[3], psum[4:8]
            NB = B * S // (2 * P)
            LAST = B * S - 2 * P * NB

            @block.sync
            def _(sp):
                def fetch(n, k, r, reuse):
                    if reuse:
                        sp.wait_ge(acc_step, 9 * (n - 2) + 1)
                    sp.dma_start(eh[0:r, k, :], h_ret[bass.ds(n * P, r), :]).then_inc(e_in[k], 16)

                fetch(0, 0, P, False)
                fetch(1, 1, P, False)
                with sp.Fori(1, NB) as i:
                    for k in range(2):
                        fetch(2 * i + k, k, P, True)
                fetch(2 * NB, 0, LAST, True)

            @block.gpsimd
            def _(pool):
                def rstd(n, k, r):
                    pool.wait_ge(e_mv, n + 1)
                    nc.gpsimd.tensor_tensor(eve[0:r, k:k + 1], emv[0:r, k, 1:2], eps[0:r, 0:1], ALU.add).then_inc(e_rs, 1)
                    pool.wait_ge(e_rs, 2 * n + 1)
                    nc.gpsimd.tensor_tensor(ers[0:r, k:k + 1], eve[0:r, k:k + 1], half[0:r, 0:1], ALU.pow).then_inc(e_rs, 1)

                with pool.Fori(0, NB) as i:
                    for k in range(2):
                        rstd(2 * i + k, k, P)
                rstd(2 * NB, 0, LAST)

            @block.scalar
            def _(act):
                def front(n, k, r):
                    act.wait_ge(ext_ps, n + 1)
                    nc.scalar.activation(ext_hi[:, k, :, 0:r], XB[:, 0:2 * P].rearrange("p (k t) -> p k t", k=2)[:, :, 0:r], ACT.Copy)\
                        .then_inc(hi_saved, 1)
                    act.wait_ge(hot_ps, n + 1)
                    nc.scalar.activation(hotT[:, k, 0:r], HB[0:NE, 0:r], ACT.Copy).then_inc(hot_saved, 1)

                def store(n, k, r):
                    act.wait_ge(acc_step, 9 * n + 9)
                    act.dma_start(out[bass.ds(n * P, r), :], acc[0:r, k, :]).then_inc(e_out[k], 16)

                front(0, 0, P)
                with act.Fori(0, NB - 1) as i:
                    for k in range(2):
                        front(2 * i + k + 1, 1 - k, P)
                        store(2 * i + k, k, P)
                front(2 * NB - 1, 1, P)
                store(2 * NB - 2, 0, P)
                front(2 * NB, 0, LAST)
                store(2 * NB - 1, 1, P)
                store(2 * NB, 0, LAST)
                act.wait_ge(e_out[0], (NB + 1) * 16)
                act.wait_ge(e_out[1], NB * 16)

            @block.vector
            def _(dve):
                def stats(p, k, r):
                    dve.wait_ge(e_in[k], 16 * p + 16)
                    nc.vector.bn_stats(est[0:r, k, :], eh[0:r, k, :])
                    dve.drain()
                    nc.vector.bn_aggr(emv[0:r, k, :], est[0:r, k, :]).then_inc(e_mv, 1)

                def normalise(n, k, r):
                    dve.wait_ge(e_rs, 2 * n + 2)
                    nc.vector.tensor_scalar(exn[0:r, k, :], eh[0:r, k, :], emv[0:r, k, 0:1], ers[0:r, k:k + 1],
                                            ALU.subtract, ALU.mult).then_inc(e_xn, 1)

                def split(n, k, r):
                    dve.wait_ge(hi_saved, n + 1)
                    nc.vector.tensor_tensor(ext_lo[:, k, :, 0:r], XB[:, 0:2 * P].rearrange("p (k t) -> p k t", k=2)[:, :, 0:r],
                                            ext_hi[:, k, :, 0:r].bitcast(F32), ALU.subtract).then_inc(lo_saved, 1)

                def gate(n, k, r):
                    dve.wait_ge(logit_ps, n + 1)
                    nc.vector.tensor_tensor(logit[0:r, k, :], LB[0:r, 0:NE], gate_b[0:r, :], ALU.add)
                    dve.drain()
                    nc.vector.max(top[0:r, k, :], logit[0:r, k, :])
                    dve.drain()
                    nc.vector.max_index(topi[0:r, k, :], top[0:r, k, :], logit[0:r, k, :])
                    dve.drain()
                    nc.vector.tensor_copy(topf[0:r, k:k + 1], topi[0:r, k, 0:1])
                    dve.drain()
                    nc.vector.tensor_scalar(hot[0:r, k, :], iota8[0:r, :], topf[0:r, k:k + 1], None, ALU.is_equal).then_inc(hot_done, 1)

                def begin(p, n, k, r):
                    if not isinstance(p, int) or p > 0:
                        dve.wait_ge(e_out[k], 16 * p)
                    dve.wait_ge(bias_ps, n + 1)
                    nc.vector.tensor_tensor(acc[0:r, k, :], BB[0:r, 0:D], eh[0:r, k, :], ALU.add).then_inc(acc_step, 1)

                def pick(n, k, r, e):
                    dve.wait_ge(acc_step, 9 * n + e + 1)
                    dve.wait_ge(expert_ps, 4 * n + e // 2 + 1)
                    nc.vector.scalar_tensor_tensor(out=acc[0:r, k, :], in0=EBK[e // 2][0:r, (e % 2) * D:(e % 2 + 1) * D],
                                                   scalar=hot[0:r, k, e:e + 1], in1=acc[0:r, k, :],
                                                   op0=ALU.mult, op1=ALU.add).then_inc(acc_step, 1)

                def step(p, n, k, r, nxt):
                    begin(p, n, k, r)
                    if nxt:
                        stats(nxt[0], 1 - k, nxt[1])
                    pick(n, k, r, 0)
                    pick(n, k, r, 1)
                    if nxt:
                        normalise(n + 1, 1 - k, nxt[1])
                    pick(n, k, r, 2)
                    pick(n, k, r, 3)
                    if nxt:
                        split(n + 1, 1 - k, nxt[1])
                    pick(n, k, r, 4)
                    pick(n, k, r, 5)
                    if nxt:
                        gate(n + 1, 1 - k, nxt[1])
                    pick(n, k, r, 6)
                    pick(n, k, r, 7)

                stats(0, 0, P)
                normalise(0, 0, P)
                split(0, 0, P)
                gate(0, 0, P)
                step(0, 0, 0, P, (0, P))
                with dve.Fori(1, NB) as p:
                    step(p - 1, 2 * p - 1, 1, P, (p, P))
                    step(p, 2 * p, 0, P, (p, P))
                step(NB - 1, 2 * NB - 1, 1, P, (NB, LAST))
                step(NB, 2 * NB, 0, LAST, None)

            @block.tensor
            def _(pe):
                mm = nc.tensor.matmul

                def turn_x(n, k, r):
                    pe.wait_ge(e_xn, n + 1)
                    for kk in range(2):
                        last = nc.tensor.transpose(XB[:, kk * P:kk * P + r], exn[0:r, k, kk * P:(kk + 1) * P], ident[0:r, 0:r])
                    last.then_inc(ext_ps, 1)

                def logits(n, k, r):
                    pe.wait_ge(hi_saved, n + 1)
                    pe.wait_ge(lo_saved, n + 1)
                    terms = [(x, g, kk) for x in (ext_hi, ext_lo) for g in (gate_hi, gate_lo) for kk in range(2)]
                    for t, (x, g, kk) in enumerate(terms):
                        last = mm(LB[0:r, 0:NE], x[:, k, kk, 0:r], g[:, kk, :], start=(t == 0), stop=(t == 7))
                    last.then_inc(logit_ps, 1)

                def bias(n, k, r):
                    pe.wait_ge(hot_done, n + 1)
                    nc.tensor.transpose(HB[0:NE, 0:r], hot[0:r, k, :], ident[0:r, 0:r]).then_inc(hot_ps, 1)
                    pe.wait_ge(hot_saved, n + 1)
                    mm(BB[0:r, 0:D], hotT[:, k, 0:r], moe_b[:, :], start=True, stop=True).then_inc(bias_ps, 1)

                def experts(n, k, r, q):
                    if not isinstance(n, int) or n > 0:
                        pe.wait_ge(acc_step, 9 * (n - 1) + 2 * q + 3)
                    terms = [(x, g, kk) for x, g in ((ext_hi, moe_hi), (ext_hi, moe_lo), (ext_lo, moe_hi)) for kk in range(2)]
                    for t, (x, g, kk) in enumerate(terms):
                        last = mm(EBK[q][0:r, :], x[:, k, kk, 0:r], g[:, kk, 2 * q:2 * q + 2, :], start=(t == 0), stop=(t == 5))
                    last.then_inc(expert_ps, 1)

                def step(n, k, r, nxt):
                    experts(n, k, r, 0)
                    experts(n, k, r, 1)
                    if nxt:
                        turn_x(n + 1, 1 - k, nxt)
                    experts(n, k, r, 2)
                    if nxt:
                        logits(n + 1, 1 - k, nxt)
                    experts(n, k, r, 3)
                    if nxt:
                        bias(n + 1, 1 - k, nxt)

                turn_x(0, 0, P)
                logits(0, 0, P)
                bias(0, 0, P)
                step(0, 0, P, P)
                with pe.Fori(1, NB) as i:
                    step(2 * i - 1, 1, P, P)
                    step(2 * i, 0, P, P)
                step(2 * NB - 1, 1, P, LAST)
                step(2 * NB, 0, LAST, None)


def kernel(**inputs):
    import numpy as np
    import concourse.bacc as bacc
    from concourse.bass_utils import run_bass_kernel_spmd

    f32 = np.float32

    def tiles(a):
        return a.reshape(-1, P, a.shape[1]).transpose(1, 0, 2)

    g = {n: np.asarray(a) for n, a in inputs.items()}
    x = g["x"].reshape(B, 3, 14, 16, 14, 16).transpose(0, 1, 3, 5, 2, 4).reshape(TOK_BLOCKS, P, FK, P)
    wkT = g["L0_attn_Wk"].T.reshape(D, NKV, 1, HD)
    heads = lambda a: a.transpose(1, 0, 2).reshape(D, D)
    ew = g["L1_ffn_expert_w"]
    weights = {
        "wtok": tiles(g["L0_tok_W"]),
        "wq": tiles(g["L0_attn_Wq"].T), "wk": tiles(np.concatenate([wkT, wkT], 2).reshape(D, 2 * NKV * HD)),
        "wv": tiles(g["L0_attn_Wv"].T), "wo": tiles(g["L0_attn_Wo"].T),
        "u1": tiles(np.concatenate([g["L0_ffn_U1"]] * 2, 1)), "v1": g["L0_ffn_V1"],
        "b1": g["L0_ffn_b1"].reshape(MF, P).T, "u2": tiles(g["L0_ffn_U2"]),
        "v2": np.concatenate([g["L0_ffn_V2"]] * 2, 0), "b2": np.broadcast_to(g["L0_ffn_b2"], (P, D)),
        "rwq": tiles(heads(g["L1_attn_Wq"])), "rwk": tiles(heads(g["L1_attn_Wk"])), "rwv": tiles(heads(g["L1_attn_Wv"])),
        "gnw": g["L1_attn_gn_weight"].reshape(2, P).T, "gnb": g["L1_attn_gn_bias"].reshape(2, P).T,
        "wout": tiles(g["L1_attn_Wout"]), "gate_w": tiles(g["L1_ffn_gate_w"]),
        "gate_b": np.broadcast_to(g["L1_ffn_gate_b"], (P, NE)),
        "ewT": ew.transpose(2, 0, 1).reshape(4, P, NE, D).transpose(1, 0, 2, 3),
        "ebT": tiles(g["L1_ffn_expert_b"].T), "ow": tiles(g["L1_ffn_out_w"]),
        "ob": np.broadcast_to(g["L1_ffn_out_b"], (NE, D)),
    }

    p, q = np.arange(P)[:, None], np.arange(P)[None, :]
    tri = (q >= p).astype(f32)
    window = (p > np.arange(TW)[None, :]).astype(f32)
    tail = (np.arange(TW)[None, :] >= np.arange(CH[2][1])[:, None]).astype(f32)
    gamma = np.array([1.0 - 2.0 ** (-5 - i // 2) for i in range(NH)])
    chan = np.arange(D)
    power = gamma[chan // 16][:, None] ** np.arange(SP)[None, :]
    parity = (chan // 16 % 2)[:, None, None] == np.arange(2)[None, :, None]
    dec_q = power[:, None, :] * parity / 4.0
    dec_kt = (1.0 / power)[:, 0:2 * P].T.reshape(2, P, D).transpose(1, 0, 2)
    tables = {
        "iota8": np.broadcast_to(np.arange(NE, dtype=f32), (P, NE)), "ident": np.eye(P, dtype=f32),
        "ones": np.ones((P, HD), f32), "half": np.full((P, 3), -0.5, f32), "eps": np.full((P, 3), EPS, f32),
        "pmask": np.concatenate([tri, np.ones((P, P), f32), window, tri], 1), "tmask": tail, "tri": tri,
        "blockdiag": (p // 16 == q // 16).astype(f32), "headavg": (p // 16 == q // 16).astype(f32) / 16,
        "dec_q": dec_q.reshape(2, P, 2, SP).transpose(1, 0, 2, 3), "dec_k": tiles(1.0 / power), "dec_kt": dec_kt,
    }

    nc = bacc.Bacc("TRN2", target_bir_lowering=False, num_devices=1)
    arrays = {}

    def give(name, a):
        a = np.ascontiguousarray(a)
        arrays[name] = a
        return nc.dram_tensor(name, a.shape, mybir.dt.from_np(a.dtype), kind="ExternalInput").ap()

    xT = give("patches", x.transpose(0, 3, 2, 1))
    txt = give("txt_rows", g["txt"].reshape(B * TXT_TOK, D))
    w = {n: give(f"w_{n}", a) for n, a in weights.items()}
    consts = {n: give(f"c_{n}", a.astype(f32)) for n, a in tables.items()}
    out = nc.dram_tensor("out_rows", (B * S, D), F32, kind="ExternalOutput").ap()
    build(nc, xT, txt, consts, w, out)
    r = run_bass_kernel_spmd(nc, [arrays], core_ids=[0])
    return np.asarray(r.results[0]["out_rows"]).reshape(B, S, D)
```

```python
import concourse.bass as bass
import numpy as np
from concourse import mybir
from contextlib import ExitStack

F32 = mybir.dt.float32
F32R = mybir.dt.float32r
U32 = mybir.dt.uint32
ALU = mybir.AluOpType
ACT = mybir.ActivationFunctionType

B, IMG_TOK, TXT_TOK, D = 32, 196, 77, 256
S = IMG_TOK + TXT_TOK
SP = S + 1
P = 128
CH = [(0, 128), (128, 128), (256, S - 256)]
PATCH_F = 768
FK = PATCH_F // P
NH, NKV, HD = 16, 4, 64
CAP = 30.0
D_FF, RANK = 1024, 64
MF = D_FF // P
RP = 8
NE, EH = 8, 512
EPS = 1e-5
TOK_BLOCKS = B * IMG_TOK // P
EB = 7
W0 = 402
TW = S + 1 - 256


def build(nc, xT, txt, consts, w, out):
    ctx = ExitStack()
    with ctx:
        def sb(name, shape, dt=F32):
            return ctx.enter_context(nc.sbuf_tensor(name, shape, dt))

        def sem(name):
            return ctx.enter_context(nc.semaphore(name))

        h_img = nc.dram_tensor("h_img", (B * IMG_TOK, D), F32, kind="Internal").ap()
        moe_dram = nc.dram_tensor("moe_dram", (2, P, 2, NE, D), F32, kind="Internal").ap()
        h_ret = nc.dram_tensor("h_ret", (B * S, D), F32, kind="Internal").ap()

        split = {}

        def halves(name, shape):
            split[name] = (sb(f"{name}_hi", shape, F32R), sb(f"{name}_lo", shape, F32R))
            return split[name]

        wq = halves("wq", [P, 2, NH * HD])
        wk = halves("wk", [P, 2, 2 * NKV * HD])
        wv = halves("wv", [P, 2, NKV * HD])
        wo = halves("wo", [P, 8, D])
        u1 = halves("u1", [P, 2, P])
        v1 = halves("v1", [P, D_FF])
        rwq = halves("rwq", [P, 2, D])
        rwk = halves("rwk", [P, 2, D])
        rwv = halves("rwv", [P, 2, D])
        gate = halves("gate_w", [P, 2, NE])
        b1 = sb("b1", [P, MF])
        u2 = sb("u2", [P, MF, RANK])
        v2 = sb("v2", [P, D])
        b2 = sb("b2", [P, D])
        gnw = sb("gnw", [P, 2])
        gnb = sb("gnb", [P, 2])
        wout = sb("wout", [P, 2, D])
        gate_b = sb("gate_b", [P, NE])
        iota8 = sb("iota8", [P, NE])
        ident = sb("ident", [P, P])
        lower = sb("lower", [P, 1])
        eps = sb("eps", [P, 3])
        half = sb("half", [P, 3])
        pmask = sb("pmask", [P, W0])
        tmask = sb("tmask", [CH[2][1], TW])
        tri = sb("tri", [P, P])
        blockdiag = sb("blockdiag", [P, P])
        headavg = sb("headavg", [P, P])
        dec_q = sb("dec_q", [P, 2, 2, SP])
        dec_k = sb("dec_k", [P, 2, SP])
        dec_kt = sb("dec_kt", [P, 2, D])
        moe_b = sb("moe_b", [NE, D])

        banks = ctx.enter_context(nc.psum_tensor("banks", [P, 8, 512], F32))
        psum = [banks[:, n, :] for n in range(8)]
        S_BANK, O_BANK, D_BANK, Y = psum[0:2], psum[2], psum[3], psum[4:8]
        QKV_BANK = [psum[0], psum[1], Y[0], Y[3]]

        def three(x, w):
            return ((x[0], w[0]), (x[0], w[1]), (x[1], w[0]))

        stage1 = ExitStack()
        with stage1:
            def sb1(name, shape, dt=F32):
                return stage1.enter_context(nc.sbuf_tensor(name, shape, dt))

            wtok = (sb1("wtok_hi", [P, FK, D], F32R), sb1("wtok_lo", [P, FK, D], F32R))
            split["wtok"] = wtok
            patch = sb1("patch", [P, EB, FK, P])
            patch_hi = sb1("patch_hi", [P, 2, FK, P], F32R)
            patch_lo = sb1("patch_lo", [P, 2, FK, P], F32R)
            FIRST = ("wtok", "wq", "wk", "wv", "u1", "rwv", "gate_w")
            SECOND = {"wo": "wq", "v1": "wtok", "rwq": "wk", "rwk": "wv"}

            def elements(name):
                return int(np.prod(split[name][0].shape[1:]))

            place = {n: sb1(f"{n}_f32", [P, elements(n)]) for n in FIRST}
            raw = {n: place[SECOND.get(n, n)][:, 0:elements(n)] for n in (*FIRST, *SECOND)}

            def flat(t):
                return t[:] if len(t.shape) == 2 else t[:].rearrange("p a b -> p (a b)")

            emb = sb1("emb", [P, EB, D])
            ewT = sb1("ewT", [P, 2, 4, D])
            moe = [sb1(f"fused_{n}", [P, 2, 2, D], F32R) for n in ("hi", "lo")]
            ebT = sb1("ebT", [P, 4, NE])
            ow = sb1("ow", [P, 4, D])
            ob = sb1("ob", [NE, D])
            tok_w_in, patch_in, const_in = sem("tok_w_in"), [sem(f"patch_in{k}") for k in range(EB)], sem("const_in")
            second_in, moe_out = sem("second_in"), [sem(f"moe_out{k}") for k in range(2)]
            w_hi, w_lo, patch_hi_done, patch_lo_done = (sem(n) for n in ("w_hi", "w_lo", "patch_hi_done", "patch_lo_done"))
            emb_ps, emb_saved, emb_out = sem("emb_ps"), sem("emb_saved"), [sem(f"emb_out{k}") for k in range(EB)]
            expert_in, ew_in = sem("expert_in"), [sem(f"ew_in{k}") for k in range(2)]
            fuse_ps, fuse_hi, fuse_saved = (sem(n) for n in ("fuse_ps", "fuse_hi", "fuse_saved"))
            block = stage1.enter_context(nc.Block())
            n_blocks = TOK_BLOCKS // EB

            loads = [(raw[n], w[n]) for n in FIRST[1:]]
            loads += [(t[:], w[n]) for n, t in (
                ("b1", b1), ("u2", u2), ("v2", v2), ("b2", b2), ("gnw", gnw), ("gnb", gnb), ("wout", wout), ("gate_b", gate_b))]
            loads += [(t[:], consts[n]) for n, t in (
                ("iota8", iota8), ("ident", ident), ("lower", lower), ("half", half), ("eps", eps), ("pmask", pmask),
                ("tmask", tmask), ("tri", tri), ("blockdiag", blockdiag), ("headavg", headavg), ("dec_q", dec_q),
                ("dec_k", dec_k), ("dec_kt", dec_kt))]
            names = (*FIRST, *SECOND)

            @block.sync
            def _(sp):
                sp.dma_start(raw["wtok"], w["wtok"]).then_inc(tok_w_in, 16)
                for k in range(EB):
                    sp.dma_start(patch[:, k], xT[k]).then_inc(patch_in[k], 16)
                with sp.Fori(1, n_blocks) as i:
                    for k in range(EB):
                        sp.wait_ge(patch_lo_done, (i - 1) * EB + k + 1)
                        sp.dma_start(patch[:, k], xT[bass.ds(i * EB + k, 1)].rearrange("o p k t -> (o p) k t"))\
                            .then_inc(patch_in[k], 16)
                for e in range(NE):
                    if e >= 2:
                        sp.wait_ge(fuse_ps, 2 * e - 2)
                    sp.dma_start(ewT[:, e % 2], w["ewT"][e]).then_inc(ew_in[e % 2], 16)

            @block.gpsimd
            def _(pool):
                def split_lo(n, name):
                    pool.wait_ge(w_hi, n + 1)
                    nc.gpsimd.tensor_tensor(flat(split[name][1]), raw[name], flat(split[name][0]).bitcast(F32), ALU.subtract)\
                        .then_inc(w_lo, 1)

                split_lo(0, FIRST[0])
                for t, src in loads:
                    pool.dma_start(t, src).then_inc(const_in, 16)
                for n, name in enumerate(FIRST[1:]):
                    split_lo(n + 1, name)
                pool.wait_ge(w_lo, len(FIRST))
                for name in SECOND:
                    pool.dma_start(raw[name], w[name]).then_inc(second_in, 16)
                for n, name in enumerate(SECOND):
                    split_lo(len(FIRST) + n, name)

            @block.tensor
            def _(pe):
                pe.wait_ge(w_lo, 1)

                def embed(i, k, reuse):
                    n = i * EB + k
                    pe.wait_ge(patch_lo_done, n + 1)
                    if reuse:
                        pe.wait_ge(emb_saved, n - EB + 1)
                    pairs = [(x, y, f) for f in range(FK) for x, y in three((patch_hi, patch_lo), wtok)]
                    for t, (x, y, f) in enumerate(pairs):
                        mm = nc.tensor.matmul(psum[k][:, 0:D], x[:, k % 2, f, :], y[:, f, :], start=(t == 0), stop=(t == len(pairs) - 1))
                    mm.then_inc(emb_ps, 1)

                for k in range(EB):
                    embed(0, k, False)
                with pe.Fori(1, n_blocks) as i:
                    for k in range(EB):
                        embed(i, k, True)
                pe.wait_ge(expert_in, 48)
                pe.wait_ge(emb_saved, TOK_BLOCKS)
                for n in range(2 * NE):
                    e, kd = n // 2, n % 2
                    pe.wait_ge(ew_in[e % 2], 16 * (e // 2) + 16)
                    if n >= 4:
                        pe.wait_ge(fuse_saved, n - 3)
                    for t in range(4):
                        mm = nc.tensor.matmul(psum[n % 4][:, 0:D], ewT[:, e % 2, t, kd * P:(kd + 1) * P], ow[:, t, :],
                                              start=(t == 0), stop=(t == 3))
                    mm.then_inc(fuse_ps, 1)
                for t in range(4):
                    mm = nc.tensor.matmul(psum[4][0:NE, 0:D], ebT[:, t, :], ow[:, t, :], start=(t == 0), stop=(t == 3))
                mm.then_inc(fuse_ps, 1)

            @block.vector
            def _(dve):
                def split_lo(i, k, first):
                    n = i * EB + k
                    dve.wait_ge(patch_hi_done, n + 1)
                    nc.vector.tensor_tensor(patch_lo[:, k % 2], patch[:, k], patch_hi[:, k % 2].bitcast(F32), ALU.subtract)\
                        .then_inc(patch_lo_done, 1)

                def save(i, k, reuse):
                    n = i * EB + k
                    dve.wait_ge(emb_ps, n + 1)
                    if reuse:
                        dve.wait_ge(emb_out[k], i * 16)
                    nc.vector.tensor_copy(emb[:, k, :], psum[k][:, 0:D]).then_inc(emb_saved, 1)

                split_lo(0, 0, True)
                for k in range(EB - 1):
                    split_lo(0, k + 1, True)
                    save(0, k, False)
                with dve.Fori(1, n_blocks) as i:
                    split_lo(i, 0, False)
                    save(i - 1, EB - 1, True)
                    for k in range(EB - 1):
                        split_lo(i, k + 1, False)
                        save(i, k, True)
                save(n_blocks - 1, EB - 1, True)
                for n in range(2 * NE):
                    dve.wait_ge(fuse_ps, n + 1)
                    e, kd = n // 2, n % 2
                    if e >= 2 and kd == 0:
                        dve.wait_ge(moe_out[e % 2], 32 * (e // 2))
                    nc.vector.tensor_copy(moe[0][:, e % 2, kd, :], psum[n % 4][:, 0:D]).then_inc(fuse_hi, 1)
                    dve.wait_ge(fuse_hi, n + 1)
                    nc.vector.tensor_tensor(moe[1][:, e % 2, kd, :], psum[n % 4][:, 0:D],
                                            moe[0][:, e % 2, kd, :].bitcast(F32), ALU.subtract).then_inc(fuse_saved, 1)
                dve.wait_ge(fuse_ps, 2 * NE + 1)
                dve.wait_ge(expert_in, 48)
                nc.vector.tensor_tensor(moe_b[:, :], psum[4][0:NE, 0:D], ob[:, :], ALU.add).then_inc(fuse_saved, 1)

            @block.scalar
            def _(act):
                def split_hi(n, name):
                    nc.scalar.activation(flat(split[name][0]), raw[name], ACT.Copy).then_inc(w_hi, 1)

                def patch_split(i, k, reuse):
                    n = i * EB + k
                    act.wait_ge(patch_in[k], (i + 1) * 16)
                    if reuse or k >= 2:
                        act.wait_ge(emb_ps, n if k == 0 else n - 1)
                    nc.scalar.activation(patch_hi[:, k % 2], patch[:, k], ACT.Copy).then_inc(patch_hi_done, 1)

                def store(i, k):
                    act.wait_ge(emb_saved, i * EB + k + 1)
                    act.dma_start(h_img[bass.ds((i * EB + k) * P, P), :], emb[:, k, :]).then_inc(emb_out[k], 16)

                act.wait_ge(tok_w_in, 16)
                split_hi(0, names[0])
                for t, src in ((ebT, w["ebT"]), (ow, w["ow"]), (ob, w["ob"])):
                    act.dma_start(t[:], src).then_inc(expert_in, 16)
                patch_split(0, 0, False)
                patch_split(0, 1, False)
                for k in range(EB - 2):
                    patch_split(0, k + 2, False)
                    store(0, k)
                with act.Fori(1, n_blocks) as i:
                    for k in range(EB):
                        patch_split(i, k, True)
                        if k < 2:
                            store(i - 1, EB - 2 + k)
                        else:
                            store(i, k - 2)
                store(n_blocks - 1, EB - 2)
                store(n_blocks - 1, EB - 1)
                act.wait_ge(const_in, 16 * len(loads))
                for n, name in enumerate(names[1:]):
                    if n + 1 == len(FIRST):
                        act.wait_ge(second_in, 16 * len(SECOND))
                    split_hi(n + 1, name)
                for e in range(NE):
                    act.wait_ge(fuse_saved, 2 * e + 2)
                    for half_, m in enumerate(moe):
                        act.dma_start(moe_dram[half_, :, :, e, :], m[:, e % 2].bitcast(F32)).then_inc(moe_out[e % 2], 16)
                for k in range(EB):
                    act.wait_ge(emb_out[k], n_blocks * 16)
                for k in range(2):
                    act.wait_ge(moe_out[k], NE // 2 * 32)

        stage2 = ExitStack()
        with stage2:
            def sb2(name, shape, dt=F32):
                return stage2.enter_context(nc.sbuf_tensor(name, shape, dt))

            def sem2(name):
                return stage2.enter_context(nc.semaphore(name))

            h_in = sb2("h_in", [P, 3, D])
            h = sb2("h", [P, 3, D])
            h_out = sb2("h_out", [P, 3, D])
            st = {n: sb2(f"ln_st{n}", [P, 3, 6]) for n in (1, 2, 3)}
            mv = {n: sb2(f"ln_mv{n}", [P, 3, 2]) for n in (1, 2, 3)}
            ve = {n: sb2(f"ln_ve{n}", [P, 3]) for n in (1, 2, 3)}
            rs = {n: sb2(f"ln_rs{n}", [P, 3]) for n in (1, 2, 3)}
            xn = {n: sb2(f"xn{n}", [P, 3, D]) if n == 2 else h_in for n in (1, 2)}
            xt = {n: (sb2(f"xt_hi{n}", [P, 2, SP], F32R), sb2(f"xt_lo{n}", [P, 2, SP], F32R)) for n in (1, 2)}
            xn[3], xt[3] = xn[2], xt[2]
            qt = (sb2("qt_hi", [P, 8, SP], F32R), sb2("qt_lo", [P, 8, SP], F32R))
            kt = (sb2("kt_hi", [P, NKV, SP], F32R), sb2("kt_lo", [P, NKV, SP], F32R))
            v = sb2("v", [P, 3, 2 * NKV + 1, HD])
            probs = sb2("probs", [P, 4, 420])
            tail_p = sb2("tail_p", [CH[2][1], 2, NH // 2, TW])
            den = sb2("den", [P, 2, SP])
            ot_f = sb2("ot_f", [P, 2, SP])
            ot = (sb2("ot_hi", [P, 8, SP], F32R), sb2("ot_lo", [P, 8, SP], F32R))
            pt_hi = sb2("pt_hi", [P, SP], F32R)
            pt = sb2("pt", [P, SP], F32R)
            gelu = sb2("gelu", [P, MF, SP])
            qf = sb2("qf", [P, SP])
            rq = sb2("rq", [P, 2, 2, SP])
            rk = sb2("rk", [P, 2, SP])
            rkt = sb2("rkt", [P, 2, D])
            rv = sb2("rv", [P, 3, RP, 2, 32])
            state = sb2("state", [P, 4, P])
            rs_sb = [sb2("rs_sb", [P, 4, 2, 2, P]),
                     gelu[:, :, :].rearrange("p m t -> p (m t)")[:, 0:16 * P].rearrange("p (r m e q) -> p r m e q", r=4, m=2, e=2)]
            ct = sb2("ct", [P, 2, SP])
            gst = sb2("gst", [P, 2, 6])
            gmv = sb2("gmv", [P, 2, 2])
            gsq = sb2("gsq", [P, 2])
            gm = sb2("gm", [P, 2, 2])
            gmm = sb2("gmm", [P, 2])
            gvar = sb2("gvar", [P, 2])
            gve = sb2("gve", [P, 2])
            grs = sb2("grs", [P, 2])
            gsc = sb2("gsc", [P, 2])
            gms = sb2("gms", [P, 2])
            gbi = sb2("gbi", [P, 2])

            zeroed = sem2("zeroed")
            hin_in = sem2("hin_in")
            h_in_dma = sem2("h_in_dma")
            hout_dma = sem2("hout_dma")
            ln_mv = {n: sem2(f"ln_mv_done{n}") for n in (1, 2, 3)}
            ln_rs = {n: sem2(f"ln_rs_done{n}") for n in (1, 2, 3)}
            xn_done = {n: sem2(f"xn_done{n}") for n in (1, 2, 3)}
            xt_ps = {n: sem2(f"xt_ps{n}") for n in (1, 2, 3)}
            xt_act = {n: sem2(f"xt_act{n}") for n in (1, 2, 3)}
            xt_dve = {n: sem2(f"xt_dve{n}") for n in (1, 2, 3)}
            oproj_ps, att_added = sem2("oproj_ps"), sem2("att_added")
            qkv_ps, qk_hi, qk_lo, v_saved = (sem2(n) for n in ("qkv_ps", "qk_hi", "qk_lo", "v_saved"))
            tail_ps, tail_act, tail_done = sem2("tail_ps"), sem2("tail_act"), sem2("tail_done")
            score_ps, cap_done, exp_done, prob_done = (sem2(n) for n in ("score_ps", "cap_done", "exp_done", "prob_done"))
            pv_ps, den_saved, inv_done = sem2("pv_ps"), sem2("den_saved"), sem2("inv_done")
            pv_saved = sem2("pv_saved")
            ot_done, ot_hi, ot_lo = sem2("ot_done"), sem2("ot_hi_done"), sem2("ot_lo_done")
            p_ps, p_hi, p_saved = sem2("p_ps"), sem2("p_hi"), sem2("p_saved")
            ff_ps, gelu_done = sem2("ff_ps"), sem2("gelu_done")
            qf_ps, qf_saved = sem2("qf_ps"), sem2("qf_saved")
            b2_added, ffo_ps, ffn_added = sem2("b2_added"), sem2("ffo_ps"), sem2("ffn_added")
            rq_ps, rq_saved = sem2("rq_ps"), sem2("rq_saved")
            rk_ps, rk_saved = sem2("rk_ps"), sem2("rk_saved")
            rv_ps, rv_saved = sem2("rv_ps"), sem2("rv_saved")
            rkt_ps, rkt_saved = sem2("rkt_ps"), sem2("rkt_saved")
            state_ps, state_saved = sem2("state_ps"), sem2("state_saved")
            rs_ps, rs_masked = sem2("rs_ps"), sem2("rs_masked")
            rpv_ps, ct_saved = sem2("rpv_ps"), sem2("ct_saved")
            gn_ps, gn_dve, gn_pool, cn_done = sem2("gn_ps"), sem2("gn_dve"), sem2("gn_pool"), sem2("cn_done")
            wo_ps, ret_added = sem2("wo_ps"), sem2("ret_added")

            XT_BANK = {1: 6, 2: 4, 3: 5}
            RV_BANK = (Y[3], Y[0], Y[1])

            def qkv_bank(u):
                return QKV_BANK[u % 4]

            OP_BANK = (Y[1][:, 0:D], Y[2][:, 0:D], psum[2][:, 0:D])
            ZEROED = 10
            RQ_BANK, RK_BANK, RKT_BANK = (Y[3], Y[0]), (Y[1], Y[2]), (Y[2], Y[3])
            RS_AT = {8: (0, 1), 9: (2, 3), 10: (4, 5), 11: (6, 7, 8)}

            def RS_BANK(u):
                return Y[1 + u % 3]

            block = stage2.enter_context(nc.Block())

            def turns(eng, turn):
                turn(0, False, True)
                turn(1, True, True)
                with eng.Fori(2, B - 1) as i:
                    turn(i, True, True)
                turn(B - 1, True, False)
                turn(B, True, None)

            @block.sync
            def _(sp):
                def load(dst, n, s):
                    r = n * IMG_TOK
                    t = n * TXT_TOK
                    k = IMG_TOK - P
                    sp.dma_start(dst[:, 0, :], h_img[bass.ds(r, P), :]).then_inc(s, 16)
                    sp.dma_start(dst[0:k, 1, :], h_img[bass.ds(r + P, k), :]).then_inc(s, 16)
                    sp.dma_start(dst[k:P, 1, :], txt[bass.ds(t, P - k), :]).then_inc(s, 16)
                    sp.dma_start(dst[0:CH[2][1], 2, :], txt[bass.ds(t + P - k, CH[2][1]), :]).then_inc(s, 16)

                def turn(i, prev, nxt):
                    if nxt:
                        sp.wait_ge(xt_ps[1], i + 1)
                        load(h_in, i + 1, hin_in)
                    if nxt is not None:
                        if prev:
                            sp.wait_ge(ret_added, 3 * (i - 1) + 3)
                            store(i - 1)
                        load(h, i, h_in_dma)
                    else:
                        sp.wait_ge(ret_added, 3 * (i - 1) + 3)
                        store(i - 1)

                def store(n):
                    sp.dma_start(h_ret[bass.ds(n * S, 2 * P), :].rearrange("(c p) d -> p c d", p=P), h_out[:, 0:2, :])\
                        .then_inc(hout_dma, 16)
                    sp.dma_start(h_ret[bass.ds(n * S + 2 * P, CH[2][1]), :], h_out[0:CH[2][1], 2, :]).then_inc(hout_dma, 16)

                load(h_in, 0, hin_in)
                turns(sp, turn)
                sp.wait_ge(hout_dma, 32 * B)

            @block.gpsimd
            def _(pool):
                def ln_pow(n, e):
                    pool.wait_ge(ln_mv[n], 3 * e + 3)
                    nc.gpsimd.tensor_tensor(ve[n][:, :], mv[n][:, :, 1], eps[:, :], ALU.add).then_inc(ln_rs[n], 1)
                    pool.wait_ge(ln_rs[n], 2 * e + 1)
                    nc.gpsimd.tensor_tensor(rs[n][:, :], ve[n][:, :], half[:, :], ALU.pow).then_inc(ln_rs[n], 1)

                def turn(i, prev, nxt):
                    a = i - 1
                    if prev:
                        attention_lo(a, 7)
                        ln_pow(2, a)
                    for hh in range(NH):
                        if nxt is not None:
                            pool.wait_ge(exp_done, NH * i + hh + 1)
                            nc.gpsimd.tensor_tensor(probs[:, hh % 4, 0:W0], probs[:, hh % 4, 0:W0], pmask[:, :], ALU.mult)\
                                .then_inc(prob_done, 1)
                            if hh == 0:
                                pool.wait_ge(tail_act, 2 * i + 2)
                                nc.gpsimd.tensor_tensor(tail_p[:, :, :, :].rearrange("p e h q -> p (e h) q"),
                                                        tail_p[:, :, :, :].rearrange("p e h q -> p (e h) q"),
                                                        tmask[:, None, :].to_broadcast([CH[2][1], NH, TW]), ALU.mult)\
                                    .then_inc(tail_done, 1)
                            if hh % 2 and hh >= 3:
                                attention_lo(i, hh // 2 - 1)
                        if hh == 1 and prev:
                            pool.wait_ge(xn_done[2], 3 * a + 3)
                            nc.gpsimd.tensor_tensor(h[:, 0:2, :], h[:, 0:2, :], b2[:, None, :].to_broadcast([P, 2, D]), ALU.add)\
                                .then_inc(b2_added, 1)
                            nc.gpsimd.tensor_tensor(h[0:CH[2][1], 2, :], h[0:CH[2][1], 2, :], b2[0:CH[2][1], :], ALU.add)\
                                .then_inc(b2_added, 1)
                        if hh == 3 and nxt:
                            ln_pow(1, i + 1)
                        if hh == 5 and prev:
                            ln_pow(3, a)
                        if hh == 13 and prev:
                            pool.wait_ge(gn_dve, 12 * a + 9)
                            nc.gpsimd.tensor_tensor(gve[:, :], gvar[:, :], eps[:, 0:2], ALU.add).then_inc(gn_pool, 1)
                            pool.wait_ge(gn_pool, 2 * a + 1)
                            nc.gpsimd.tensor_tensor(grs[:, :], gve[:, :], half[:, 0:2], ALU.pow).then_inc(gn_pool, 1)

                def attention_lo(i, j):
                    pool.wait_ge(ot_hi, 8 * i + j + 1)
                    nc.gpsimd.tensor_tensor(ot[1][:, j, :], ot_f[:, j % 2, :], ot[0][:, j, :].bitcast(F32), ALU.subtract)\
                        .then_inc(ot_lo, 1)

                pool.wait_ge(zeroed, ZEROED)
                ln_pow(1, 0)
                turns(pool, turn)

            @block.scalar
            def _(act):
                def ln_evac(n, e):
                    act.wait_ge(xt_ps[n], e + 1)
                    nc.scalar.activation(xt[n][0][:, :, 0:S], banks[:, XT_BANK[n]:XT_BANK[n] + 2, 0:S], ACT.Copy).then_inc(xt_act[n], 1)

                def turn(i, prev, nxt):
                    a = i - 1
                    if nxt is not None:
                        for u in range(15):
                            act.wait_ge(qkv_ps, 15 * i + u + 1)
                            if u >= 12:
                                r = CH[u - 12][1]
                                nc.scalar.activation(v[0:r, u - 12, 1::2, :], qkv_bank(u)[0:r, 0:NKV * HD].rearrange("p (g d) -> p g d", g=NKV),
                                                     ACT.Copy).then_inc(v_saved, 1)
                            else:
                                dst = qt[0][:, u, :] if u < 8 else kt[0][:, u - 8, :]
                                nc.scalar.activation(dst, qkv_bank(u)[:, 0:SP], ACT.Copy).then_inc(qk_hi, 1)
                            if u == 3 and prev:
                                attention_hi(a, 7)
                    else:
                        attention_hi(a, 7)
                    for hh in range(NH):
                        if nxt is not None:
                            act.wait_ge(score_ps, NH * i + hh + 1)
                            if hh >= 4:
                                act.wait_ge(pv_ps, NH * i + hh - 3)
                            nc.scalar.activation(probs[:, hh % 4, :], S_BANK[hh % 2][:, 0:420], ACT.Tanh,
                                                 scale=HD ** -0.5 / CAP).then_inc(cap_done, 1)
                            act.wait_ge(cap_done, NH * i + hh + 1)
                            nc.scalar.activation(probs[:, hh % 4, :], probs[:, hh % 4, :], ACT.Exp, scale=CAP).then_inc(exp_done, 1)
                            if hh == 0:
                                act.wait_ge(tail_ps, i + 1)
                                nc.scalar.activation(tail_p[:, :, :, :], banks[0:CH[2][1], 2:4, 0:NH // 2 * TW].rearrange("p e (h q) -> p e h q", q=TW),
                                                     ACT.Tanh, scale=HD ** -0.5 / CAP).then_inc(tail_act, 1)
                                act.wait_ge(tail_act, 2 * i + 1)
                                nc.scalar.activation(tail_p[:, :, :, :], tail_p[:, :, :, :], ACT.Exp, scale=CAP).then_inc(tail_act, 1)
                            elif hh % 2 == 0:
                                if hh == 2 and prev:
                                    hidden_out(a, 0)
                                pair_out(i, hh // 2 - 1)
                            if hh % 2 and hh >= 3:
                                attention_hi(i, hh // 2 - 1)
                        if prev:
                            rest(hh, a, nxt is None)
                        if hh == 12 and nxt:
                            ln_evac(1, i + 1)
                    if nxt is not None:
                        pair_out(i, 7)

                def pair_out(i, j):
                    act.wait_ge(pv_ps, NH * i + 2 * j + 2)
                    if j >= 2 or not isinstance(i, int) or i > 0:
                        act.wait_ge(ot_lo, 8 * i + j - 1)
                    nc.scalar.activation(den[0:64, j % 2, :], O_BANK[64:128, 0:SP], ACT.Copy)
                    nc.scalar.activation(den[64:128, j % 2, :], D_BANK[0:64, 0:SP], ACT.Copy).then_inc(den_saved, 1)
                    nc.scalar.activation(ot_f[0:64, j % 2, :], O_BANK[0:64, 0:SP], ACT.Copy)
                    nc.scalar.activation(ot_f[64:128, j % 2, :], D_BANK[64:128, 0:SP], ACT.Copy).then_inc(pv_saved, 1)

                def hidden_out(a, first):
                    for m in range(first, first + 4):
                        act.wait_ge(ff_ps, MF * a + m + 1)
                        nc.scalar.activation(gelu[:, m, :], Y[(3 + m) % 4][:, 0:SP], ACT.Gelu_apprx_tanh,
                                             bias=b1[:, m:m + 1]).then_inc(gelu_done, 1)

                def attention_hi(i, j):
                    act.wait_ge(ot_done, 8 * i + j + 1)
                    nc.scalar.activation(ot[0][:, j, :], ot_f[:, j % 2, :], ACT.Copy).then_inc(ot_hi, 1)

                def rest(hh, a, last):
                    if hh == 0:
                        ln_evac(2, a)
                    if hh == 1:
                        act.wait_ge(p_ps, a + 1)
                        nc.scalar.activation(pt_hi[:, :], Y[2][:, 0:SP], ACT.Copy).then_inc(p_hi, 1)
                    if hh == 2 and last:
                        hidden_out(a, 0)
                    if hh == 3:
                        hidden_out(a, 4)
                    if hh == 6:
                        ln_evac(3, a)
                    if hh == 7:
                        for c, (_, n) in enumerate(CH):
                            act.wait_ge(rv_ps, 3 * a + c + 1)
                            for e in range(2):
                                cp = nc.scalar.activation(
                                    rv[0:n, c, :, e, 16 * e:16 * e + 16],
                                    RV_BANK[c][0:n, 0:D].rearrange("p (r e d) -> p r e d", e=2, d=16)[:, :, e, :], ACT.Copy)
                            cp.then_inc(rv_saved, 1)
                    if hh in (10, 11, 12):
                        c = hh - 10
                        t, n = CH[c]
                        act.wait_ge(rpv_ps, 3 * a + c + 1)
                        nc.scalar.activation(ct[:, :, t:t + n], Y[0][:, :].rearrange("p (m q) -> p m q", m=2)[:, :, 0:n],
                                             ACT.Copy).then_inc(ct_saved, 1)
                    if hh == 14:
                        act.wait_ge(gn_dve, 12 * a + 12)
                        for m in range(2):
                            nc.scalar.activation(ct[:, m, 0:S], ct[:, m, 0:S], ACT.Identity,
                                                 scale=gsc[:, m:m + 1], bias=gbi[:, m:m + 1]).then_inc(cn_done, 1)

                act.wait_ge(zeroed, ZEROED)
                ln_evac(1, 0)
                turns(act, turn)

            @block.vector
            def _(dve):
                for t in [x[:, :, S:SP].bitcast(F32) for n in (1, 2) for x in xt[n]] + [
                          rv[:, :, :, :, :], mv[1][:, :, :], mv[2][:, :, :], mv[3][:, :, :], ct[:, :, :]]:
                    nc.vector.memset(t, 0.0).then_inc(zeroed, 1)
                nc.vector.memset(v[:, :, :, :], 1.0).then_inc(zeroed, 1)

                def chunk_stats(n, c, src):
                    r = CH[c][1]
                    nc.vector.bn_stats(st[n][0:r, c, :], src[0:r, c, :])

                def ln_stats(n, e, src, chunks=(0, 1, 2)):
                    for c in chunks:
                        chunk_stats(n, c, src)
                    dve.drain()
                    for c, (_, r) in enumerate(CH):
                        nc.vector.bn_aggr(mv[n][0:r, c, :], st[n][0:r, c, :]).then_inc(ln_mv[n], 1)

                def ln_apply(n, e, src):
                    dve.wait_ge(ln_rs[n], 2 * e + 2)
                    for c, (_, r) in enumerate(CH):
                        nc.vector.tensor_scalar(xn[n][0:r, c, :], src[0:r, c, :], mv[n][0:r, c, 0:1], rs[n][0:r, c:c + 1],
                                                ALU.subtract, ALU.mult).then_inc(xn_done[n], 1)

                def ln_evac(n, e):
                    dve.wait_ge(xt_act[n], e + 1)
                    nc.vector.tensor_tensor(xt[n][1][:, :, 0:S], banks[:, XT_BANK[n]:XT_BANK[n] + 2, 0:S],
                                            xt[n][0][:, :, 0:S].bitcast(F32), ALU.subtract).then_inc(xt_dve[n], 1)

                def turn(i, prev, nxt):
                    a = i - 1
                    if nxt is not None:
                        for u in range(8):
                            dve.wait_ge(qk_hi, 12 * i + u + 1)
                            nc.vector.tensor_tensor(qt[1][:, u, :], qkv_bank(u)[:, 0:SP], qt[0][:, u, :].bitcast(F32), ALU.subtract)\
                                .then_inc(qk_lo, 1)
                    if prev:
                        dve.wait_ge(h_in_dma, 64 * a + 64)
                        for c, (_, r) in enumerate(CH):
                            dve.wait_ge(oproj_ps, 3 * a + c + 1)
                            nc.vector.tensor_tensor(h[0:r, c, :], OP_BANK[c][0:r, :], h[0:r, c, :], ALU.add).then_inc(att_added, 1)
                            if c:
                                dve.wait_ge(att_added, 3 * a + c)
                                chunk_stats(2, c - 1, h)
                        dve.wait_ge(att_added, 3 * a + 3)
                        ln_stats(2, a, h, (2,))
                    if nxt is not None:
                        for u in range(4):
                            dve.wait_ge(qk_hi, 12 * i + u + 9)
                            nc.vector.tensor_tensor(kt[1][:, u, :], qkv_bank(8 + u)[:, 0:SP], kt[0][:, u, :].bitcast(F32), ALU.subtract)\
                                .then_inc(qk_lo, 1)
                    if prev:
                        ln_apply(2, a, h)
                    for hh in range(NH):
                        if prev:
                            rest_first(hh, a)
                        if nxt is not None and hh % 2 == 0 and hh:
                            normalise(i, hh // 2 - 1)
                        if nxt:
                            if hh == 3:
                                dve.wait_ge(hin_in, 64 * (i + 1) + 64)
                                ln_stats(1, i + 1, h_in)
                            if hh == 4:
                                ln_apply(1, i + 1, h_in)
                            if hh == 12:
                                ln_evac(1, i + 1)
                        if prev:
                            rest(hh, a)
                    if nxt is not None:
                        normalise(i, 7)

                def normalise(i, j):
                    dve.wait_ge(den_saved, 8 * i + j + 1)
                    nc.vector.reciprocal(den[:, j % 2, :], den[:, j % 2, :]).then_inc(inv_done, 1)
                    dve.wait_ge(pv_saved, 8 * i + j + 1)
                    dve.wait_ge(inv_done, 8 * i + j + 1)
                    nc.vector.tensor_tensor(ot_f[:, j % 2, :], ot_f[:, j % 2, :], den[:, j % 2, :], ALU.mult).then_inc(ot_done, 1)

                def rest_first(hh, a):
                    if hh == 0:
                        ln_evac(2, a)
                    if hh == 4:
                        dve.wait_ge(qf_ps, a + 1)
                        nc.vector.tensor_copy(qf[:, :], Y[3][:, 0:SP]).then_inc(qf_saved, 1)
                    if hh == 6:
                        ln_evac(3, a)

                def rest(hh, a):
                    if hh == 1:
                        dve.wait_ge(p_hi, a + 1)
                        nc.vector.scalar_tensor_tensor(out=pt[:, :], in0=pt_hi[:, :].bitcast(F32), scalar=lower[:, 0:1],
                                                       in1=Y[2][:, 0:SP], op0=ALU.mult, op1=ALU.add).then_inc(p_saved, 1)
                    if hh == 4:
                        dve.wait_ge(b2_added, 2 * a + 2)
                        for c, (_, r) in enumerate(CH):
                            dve.wait_ge(ffo_ps, 3 * a + c + 1)
                            nc.vector.tensor_tensor(h[0:r, c, :], Y[c][0:r, 0:D], h[0:r, c, :], ALU.add).then_inc(ffn_added, 1)
                            if c:
                                dve.wait_ge(ffn_added, 3 * a + c)
                                chunk_stats(3, c - 1, h)
                        dve.wait_ge(ffn_added, 3 * a + 3)
                        ln_stats(3, a, h, (2,))
                    if hh == 5:
                        ln_apply(3, a, h)
                    if hh == 7:
                        for m in range(2):
                            dve.wait_ge(rq_ps, 2 * a + m + 1)
                            for e in range(2):
                                nc.vector.tensor_tensor(rq[:, m, e, :], RQ_BANK[m][:, 0:SP], dec_q[:, m, e, :], ALU.mult)\
                                    .then_inc(rq_saved, 1)
                        for m in range(2):
                            dve.wait_ge(rk_ps, 2 * a + m + 1)
                            nc.vector.tensor_tensor(rk[:, m, :], RK_BANK[m][:, 0:SP], dec_k[:, m, :], ALU.mult).then_inc(rk_saved, 1)
                        for c in range(2):
                            dve.wait_ge(rkt_ps, 2 * a + c + 1)
                            nc.vector.tensor_tensor(rkt[:, c, :], RKT_BANK[c][:, 0:D], dec_kt[:, c, :], ALU.mult).then_inc(rkt_saved, 1)
                    if hh == 8:
                        dve.wait_ge(state_ps, a + 1)
                        nc.vector.tensor_tensor(state[:, :, :], Y[0][:, :].rearrange("p (n q) -> p n q", n=4),
                                                blockdiag[:, None, :].to_broadcast([P, 4, P]), ALU.mult).then_inc(state_saved, 1)
                    for u in RS_AT.get(hh, ()):
                        dve.wait_ge(rs_ps, 9 * a + u + 1)
                        c = u // 4
                        n = CH[c][1]
                        if u == 8:
                            dve.wait_ge(rpv_ps, 3 * a + 1)
                            nc.vector.tensor_tensor(
                                rs_sb[0][0:n].rearrange("p r m e q -> p (r m e) q")[:, :, 0:n], RS_BANK(u)[0:n, 0:16 * n].rearrange("p (h q) -> p h q", q=n),
                                tri[0:n, None, 0:n].to_broadcast([n, NH, n]), ALU.mult).then_inc(rs_masked, 1)
                        else:
                            nc.vector.tensor_tensor(
                                rs_sb[c][:, u % 4, :, :, :], RS_BANK(u)[:, :].rearrange("p (m e q) -> p m e q", m=2, e=2),
                                tri[:, None, None, :].to_broadcast([P, 2, 2, P]), ALU.mult).then_inc(rs_masked, 1)
                    if hh == 12:
                        g = 12 * a
                        dve.wait_ge(ct_saved, 3 * a + 3)
                        for m in range(2):
                            nc.vector.bn_stats(gst[:, m, :], ct[:, m, 0:S]).then_inc(gn_dve, 1)
                        dve.drain()
                        for m in range(2):
                            nc.vector.bn_aggr(gmv[:, m, :], gst[:, m, :]).then_inc(gn_dve, 1)
                        dve.wait_ge(gn_dve, g + 4)
                        nc.vector.tensor_tensor(gsq[:, :], gmv[:, :, 0], gmv[:, :, 0], ALU.mult).then_inc(gn_dve, 1)
                        dve.wait_ge(gn_dve, g + 5)
                        nc.vector.tensor_tensor(gmv[:, :, 1], gsq[:, :], gmv[:, :, 1], ALU.add).then_inc(gn_dve, 1)
                    if hh == 13:
                        g = 12 * a
                        dve.wait_ge(gn_ps, a + 1)
                        nc.vector.tensor_copy(gm[:, :, :], Y[0][:, 0:4].rearrange("p (m s) -> p m s", m=2)).then_inc(gn_dve, 1)
                        dve.wait_ge(gn_dve, g + 7)
                        nc.vector.tensor_tensor(gmm[:, :], gm[:, :, 0], gm[:, :, 0], ALU.mult).then_inc(gn_dve, 1)
                        dve.wait_ge(gn_dve, g + 8)
                        nc.vector.tensor_tensor(gvar[:, :], gm[:, :, 1], gmm[:, :], ALU.subtract).then_inc(gn_dve, 1)
                        dve.wait_ge(gn_pool, 2 * a + 2)
                        nc.vector.tensor_tensor(gsc[:, :], grs[:, :], gnw[:, :], ALU.mult).then_inc(gn_dve, 1)
                        dve.wait_ge(gn_dve, g + 10)
                        nc.vector.tensor_tensor(gms[:, :], gm[:, :, 0], gsc[:, :], ALU.mult).then_inc(gn_dve, 1)
                        dve.wait_ge(gn_dve, g + 11)
                        nc.vector.tensor_tensor(gbi[:, :], gnb[:, :], gms[:, :], ALU.subtract).then_inc(gn_dve, 1)
                    if hh == 15:
                        if not isinstance(a, int) or a > 0:
                            dve.wait_ge(hout_dma, 32 * a)
                        for c, (_, r) in enumerate(CH):
                            dve.wait_ge(wo_ps, 3 * a + c + 1)
                            nc.vector.tensor_tensor(h_out[0:r, c, :], Y[1 + c][0:r, 0:D], h[0:r, c, :], ALU.add).then_inc(ret_added, 1)

                dve.wait_ge(zeroed, ZEROED)
                dve.wait_ge(hin_in, 64)
                ln_stats(1, 0, h_in)
                ln_apply(1, 0, h_in)
                ln_evac(1, 0)
                turns(dve, turn)

            @block.tensor
            def _(pe):
                mm = nc.tensor.matmul

                def ln_transpose(n, e):
                    pe.wait_ge(xn_done[n], 3 * e + 3)
                    for k in range(2):
                        for c, (t, r) in enumerate(CH):
                            last = nc.tensor.transpose(psum[XT_BANK[n] + k][:, t:t + r], xn[n][0:r, c, k * P:(k + 1) * P], ident[0:r, 0:r])
                    last.then_inc(xt_ps[n], 1)

                def xt_ready(n, e):
                    pe.wait_ge(xt_dve[n], e + 1)

                def project(dst, pairs):
                    for t, (x, y) in enumerate(pairs):
                        last = mm(dst, x, y, start=(t == 0), stop=(t == len(pairs) - 1))
                    return last

                def features(dst, weight, cols, x):
                    return project(dst, [(w[:, k, cols[0]:cols[1]], y[:, k, :]) for k in range(2) for w, y in three(weight, x)])

                def tokens(dst, x, t, r, weight):
                    return project(dst, [(y[:, k, t:t + r], w[:, k, :]) for k in range(2) for y, w in three(x, weight)])

                def scores(i, hh):
                    g, j, s = hh // 4, hh // 2, 64 * (hh % 2)
                    if hh >= 2:
                        pe.wait_ge(cap_done, NH * i + hh - 1)
                    project(S_BANK[hh % 2][:, 0:SP], [(k[s:s + 64, g, 0:P], q[s:s + 64, j, :]) for k, q in three(kt, qt)])
                    if hh == 0:
                        pe.wait_ge(v_saved, 3 * i + 3)
                    project(S_BANK[hh % 2][:, SP:420], [(k[s:s + 64, g, P:2 * P], q[s:s + 64, j, P:SP]) for k, q in three(kt, qt)])\
                        .then_inc(score_ps, 1)

                def weighted(i, hh):
                    g, odd = hh // 4, hh % 2
                    if hh == 0:
                        pe.wait_ge(tail_done, i + 1)
                    elif not odd:
                        pe.wait_ge(pv_saved, 8 * i + hh // 2)
                    pe.wait_ge(prob_done, NH * i + hh + 1)
                    for c, (t, r) in enumerate(CH):
                        left = v[0:r, c, 2 * g + 1 - odd:2 * g + 3 - odd, :]
                        right = (probs[:, hh % 4, 0:SP], probs[:, hh % 4, SP:420], tail_p[:, hh % 2, hh // 2, :])[c]
                        last = mm(psum[2 + odd][:, t:SP], left, right, start=(c == 0), stop=(c == 2))
                    last.then_inc(pv_ps, 1)

                def turn(i, prev, nxt):
                    a = i - 1
                    if nxt is not None:
                        xt_ready(1, i)
                        for u in range(8):
                            unit(i, u, a)
                    if prev:
                        pe.wait_ge(ot_lo, 8 * a + 8)
                        if nxt is None:
                            pe.wait_ge(ret_added, 3 * a)
                        for c, (t, r) in enumerate(CH):
                            project(OP_BANK[c][0:r, :], [(o[:, j, t:t + r], w[:, j, :]) for j in range(8) for o, w in three(ot, wo)])\
                                .then_inc(oproj_ps, 1)
                    if nxt is not None:
                        for u in range(8, 15):
                            unit(i, u, a)
                        pe.wait_ge(qk_lo, 12 * i + 12)
                        pe.wait_ge(v_saved, 3 * i + 1)
                        scores(i, 0)
                        t, r = CH[2]
                        for hh in range(NH):
                            s = 64 * (hh % 2)
                            last = project(psum[2 + hh % 2][0:r, hh // 2 * TW:(hh // 2 + 1) * TW],
                                           [(k[s:s + 64, hh // 4, t:t + r], q[s:s + 64, hh // 2, t:SP]) for k, q in three(kt, qt)])
                        last.then_inc(tail_ps, 1)
                    for hh in range(NH):
                        if prev:
                            before(hh, a)
                        if nxt is not None and hh < NH - 1:
                            scores(i, hh + 1)
                        if hh == 12 and nxt:
                            if prev:
                                pe.wait_ge(rs_masked, 9 * a + 9)
                            ln_transpose(1, i + 1)
                        if hh == 6 and prev:
                            ln_transpose(3, a)
                        if prev:
                            rest(hh, a)
                        if nxt is not None:
                            weighted(i, hh)
                        if prev:
                            after(hh, a, nxt)

                def unit(i, u, a):
                    if u >= 4:
                        pe.wait_ge(qk_lo, 12 * i + u - 3)
                    if u == 2 and (not isinstance(i, int) or i > 1):
                        pe.wait_ge(ret_added, 3 * a)
                    if u < 8:
                        last = features(qkv_bank(u)[:, 0:SP], wq, (u * P, (u + 1) * P), xt[1])
                    elif u < 12:
                        last = features(qkv_bank(u)[:, 0:SP], wk, ((u - 8) * P, (u - 7) * P), xt[1])
                    else:
                        t, r = CH[u - 12]
                        last = tokens(qkv_bank(u)[0:r, 0:NKV * HD], xt[1], t, r, wv)
                    last.then_inc(qkv_ps, 1)

                def before(hh, a):
                    if hh == 0:
                        ln_transpose(2, a)

                def after(hh, a, nxt):
                    if hh == 0:
                        xt_ready(2, a)
                        features(Y[2][:, 0:SP], u1, (0, P), xt[2]).then_inc(p_ps, 1)
                    if hh == 3:
                        pe.wait_ge(gelu_done, MF * a + MF)
                        for m in range(MF):
                            s = 64 * (m % 2)
                            last = mm(Y[3][s:s + 64, 0:SP], u2[:, m, :], gelu[:, m, :], start=(m < 2), stop=(m >= MF - 2))
                        last.then_inc(qf_ps, 1)
                    if hh == 6:
                        xt_ready(3, a)
                        for bank, weight, s in ((RQ_BANK, rwq, rq_ps), (RK_BANK, rwk, rk_ps)):
                            for m in range(2):
                                features(bank[m][:, 0:SP], weight, (m * P, (m + 1) * P), xt[3]).then_inc(s, 1)
                    if hh == 14:
                        if nxt:
                            xt_ready(1, a + 2)
                        pe.wait_ge(cn_done, 2 * a + 2)
                        for c, (t, r) in enumerate(CH):
                            for m in range(2):
                                last = mm(Y[1 + c][0:r, 0:D], ct[:, m, t:t + r], wout[:, m, :], start=(m == 0), stop=(m == 1))
                            last.then_inc(wo_ps, 1)

                def rest(hh, a):
                    if hh in (1, 2):
                        if hh == 1:
                            pe.wait_ge(p_saved, a + 1)
                        for m in range(4 * hh - 4, 4 * hh):
                            if m >= 4:
                                pe.wait_ge(gelu_done, MF * a + m - 3)
                            project(Y[(3 + m) % 4][:, 0:SP], [(w[:, m * P:(m + 1) * P], pt[:, :]) for w in v1]).then_inc(ff_ps, 1)
                    if hh == 4:
                        pe.wait_ge(qf_saved, a + 1)
                        for c, (t, r) in enumerate(CH):
                            mm(Y[c][0:r, 0:D], qf[:, t:t + r], v2[:, :], start=True, stop=True).then_inc(ffo_ps, 1)
                    if hh == 7:
                        for c, (t, r) in enumerate(CH):
                            if c < 2:
                                pe.wait_ge(rq_saved, 4 * a + 2 * c + 2)
                            else:
                                pe.wait_ge(rk_saved, 2 * a + 1)
                            tokens(RV_BANK[c][0:r, 0:D], xt[3], t, r, rwv).then_inc(rv_ps, 1)
                        for c in range(2):
                            if c == 0:
                                pe.wait_ge(rk_saved, 2 * a + 2)
                            else:
                                pe.wait_ge(rv_saved, 3 * a + 1)
                            t, r = CH[c]
                            tokens(RKT_BANK[c][0:r, 0:D], xt[3], t, r, rwk).then_inc(rkt_ps, 1)
                    if hh == 8:
                        pe.wait_ge(rkt_saved, 2 * a + 2)
                        pe.wait_ge(rv_saved, 3 * a + 3)
                        for c in range(2):
                            for m in range(2):
                                n = 2 * c + m
                                last = mm(Y[0][:, n * P:(n + 1) * P], rkt[:, c, m * P:(m + 1) * P], heads_of(c, m), start=True, stop=True)
                        last.then_inc(state_ps, 1)
                    for u in RS_AT.get(hh, ()):
                        if 3 <= u < 7:
                            pe.wait_ge(rs_masked, 9 * a + u - 2)
                        if u == 7:
                            pe.wait_ge(rs_masked, 9 * a + 6)
                        c = u // 4
                        t, r = CH[c]
                        pairs = [pr + 4 * m for pr in range(4) for m in range(2)] if u == 8 else (u % 4, u % 4 + 4)
                        for n, pr in enumerate(pairs):
                            m, q = pr // 4, 32 * (pr % 4)
                            if n in (2, 4, 6):
                                pe.drain()
                            last = mm(RS_BANK(u)[0:r, 2 * r * n:2 * r * (n + 1)].rearrange("p (e q) -> p e q", e=2),
                                      rk[q:q + 32, m, t:t + r], rq[q:q + 32, m, :, t:t + r], start=True, stop=True)
                        last.then_inc(rs_ps, 1)
                    if hh in (10, 11, 12):
                        retained(hh - 10, a)
                    if hh == 13:
                        pe.wait_ge(ct_saved, 3 * a + 3)
                        pe.wait_ge(gn_dve, 12 * a + 6)
                        mm(Y[0][:, 0:4], headavg[:, :], gmv[:, :, :].rearrange("p m s -> p (m s)"), start=True, stop=True)\
                            .then_inc(gn_ps, 1)

                def heads_of(c, m):
                    full = rv[:, c, 4 * m:4 * m + 4, :, :].rearrange("p r e d -> p r (e d)")
                    return bass.AP(full.tensor, full.offset, [list(full.ap[0]), [64, 4], [48, 2], [1, 16]])

                def retained(c, a):
                    t, r = CH[c]
                    if c == 0:
                        pe.wait_ge(state_saved, a + 1)
                    else:
                        pe.wait_ge(ct_saved, 3 * a + c)
                    pe.wait_ge(rs_masked, 9 * a + (4, 8, 9)[c])
                    for m in range(2):
                        o = m * D
                        for cc in range(c):
                            for e in range(2):
                                mm(Y[0][:, o:o + r], state[:, 2 * cc + m, :], rq[:, m, e, t:t + r],
                                   start=(cc == 0 and e == 0), stop=False, skip_group_check=True)
                        for q in range(4):
                            pr = 4 * m + q
                            for e in range(2):
                                last = mm(Y[0][32 * q:32 * q + 32, o:o + r], rv[0:r, c, pr, e, :], rs_sb[c % 2][0:r, q, m, e, 0:r],
                                          start=(c == 0 and e == 0), stop=(e == 1), skip_group_check=True)
                    last.then_inc(rpv_ps, 1)

                pe.wait_ge(zeroed, ZEROED)
                ln_transpose(1, 0)
                turns(pe, turn)

        stage3 = ExitStack()
        with stage3:
            def sb3(name, shape, dt=F32):
                return stage3.enter_context(nc.sbuf_tensor(name, shape, dt))

            def sem3(name):
                return stage3.enter_context(nc.semaphore(name))

            moe_hi = sb3("moe_hi", [P, 2, NE, D], F32R)
            moe_lo = sb3("moe_lo", [P, 2, NE, D], F32R)
            moe_in = sem3("moe_in")
            bias_split = sem3("bias_split")
            eh = sb3("eh", [P, 2, D])
            est = sb3("est", [P, 2, 6])
            emv = sb3("emv", [P, 2, 2])
            eve = sb3("eve", [P, 2])
            ers = sb3("ers", [P, 2])
            exn = sb3("exn", [P, 2, D])
            ext_hi = sb3("ext_hi", [P, 2, 2, P], F32R)
            ext_lo = sb3("ext_lo", [P, 2, 2, P], F32R)
            logit = sb3("logit", [P, 2, NE])
            top = sb3("top", [P, 2, NE])
            topi = sb3("topi", [P, 2, NE], U32)
            topf = sb3("topf", [P, 2])
            hot = sb3("hot", [P, 2, NE])
            hotT = sb3("hotT", [NE, 2, P], F32R)
            bias_hi = sb3("bias_hi", [NE, D], F32R)
            bias_lo = sb3("bias_lo", [NE, D], F32R)
            acc = sb3("acc", [P, 2, D])
            e_in, e_out = ([sem3(f"{n}{k}") for k in range(2)] for n in ("e_in", "e_out"))
            e_mv, e_rs, e_xn = sem3("e_mv"), sem3("e_rs"), sem3("e_xn")
            ext_ps, hi_saved, lo_saved = sem3("ext_ps"), sem3("hi_saved"), sem3("lo_saved")
            logit_ps, gated, hot_done = sem3("logit_ps"), sem3("gated"), sem3("hot_done")
            hot_ps, hot_saved, bias_ps = sem3("hot_ps"), sem3("hot_saved"), sem3("bias_ps")
            expert_ps, acc_step = sem3("expert_ps"), sem3("acc_step")
            block = stage3.enter_context(nc.Block())
            XB, LB, HB, BB, EBK = psum[0], psum[1], psum[2], psum[3], psum[4:8]
            NB = B * S // (2 * P)
            LAST = B * S - 2 * P * NB

            @block.sync
            def _(sp):
                def fetch(n, k, r, reuse):
                    if reuse:
                        sp.wait_ge(acc_step, 9 * (n - 2) + 1)
                    sp.dma_start(eh[0:r, k, :], h_ret[bass.ds(n * P, r), :]).then_inc(e_in[k], 16)

                fetch(0, 0, P, False)
                fetch(1, 1, P, False)
                sp.dma_start(moe_hi[:].bitcast(F32), moe_dram[0]).then_inc(moe_in, 16)
                sp.dma_start(moe_lo[:].bitcast(F32), moe_dram[1]).then_inc(moe_in, 16)
                with sp.Fori(1, NB) as i:
                    for k in range(2):
                        fetch(2 * i + k, k, P, True)
                fetch(2 * NB, 0, LAST, True)

            @block.gpsimd
            def _(pool):
                def rstd(n, k, r):
                    pool.wait_ge(e_mv, n + 1)
                    nc.gpsimd.tensor_tensor(eve[0:r, k:k + 1], emv[0:r, k, 1:2], eps[0:r, 0:1], ALU.add).then_inc(e_rs, 1)
                    pool.wait_ge(e_rs, 2 * n + 1)
                    nc.gpsimd.tensor_tensor(ers[0:r, k:k + 1], eve[0:r, k:k + 1], half[0:r, 0:1], ALU.pow).then_inc(e_rs, 1)

                with pool.Fori(0, NB) as i:
                    for k in range(2):
                        rstd(2 * i + k, k, P)
                rstd(2 * NB, 0, LAST)

            @block.scalar
            def _(act):
                def front(n, k, r):
                    act.wait_ge(ext_ps, n + 1)
                    nc.scalar.activation(ext_hi[:, k, :, 0:r], XB[:, 0:2 * P].rearrange("p (k t) -> p k t", k=2)[:, :, 0:r], ACT.Copy)\
                        .then_inc(hi_saved, 1)

                def mask_out(n, k, r):
                    act.wait_ge(hot_ps, n + 1)
                    nc.scalar.activation(hotT[:, k, 0:r], HB[0:NE, 0:r], ACT.Copy).then_inc(hot_saved, 1)

                def store(n, k, r):
                    act.wait_ge(acc_step, 9 * n + 9)
                    act.dma_start(out[bass.ds(n * P, r), :], acc[0:r, k, :]).then_inc(e_out[k], 16)

                front(0, 0, P)
                with act.Fori(0, NB - 1) as i:
                    for k in range(2):
                        mask_out(2 * i + k, k, P)
                        front(2 * i + k + 1, 1 - k, P)
                        store(2 * i + k, k, P)
                mask_out(2 * NB - 2, 0, P)
                front(2 * NB - 1, 1, P)
                store(2 * NB - 2, 0, P)
                mask_out(2 * NB - 1, 1, P)
                front(2 * NB, 0, LAST)
                store(2 * NB - 1, 1, P)
                mask_out(2 * NB, 0, LAST)
                store(2 * NB, 0, LAST)
                act.wait_ge(e_out[0], (NB + 1) * 16)
                act.wait_ge(e_out[1], NB * 16)

            @block.vector
            def _(dve):
                def stats(p, k, r):
                    dve.wait_ge(e_in[k], 16 * p + 16)
                    nc.vector.bn_stats(est[0:r, k, :], eh[0:r, k, :])
                    dve.drain()
                    nc.vector.bn_aggr(emv[0:r, k, :], est[0:r, k, :]).then_inc(e_mv, 1)

                def normalise(n, k, r):
                    dve.wait_ge(e_rs, 2 * n + 2)
                    nc.vector.tensor_scalar(exn[0:r, k, :], eh[0:r, k, :], emv[0:r, k, 0:1], ers[0:r, k:k + 1],
                                            ALU.subtract, ALU.mult).then_inc(e_xn, 1)

                def split(n, k, r):
                    dve.wait_ge(hi_saved, n + 1)
                    nc.vector.tensor_tensor(ext_lo[:, k, :, 0:r], XB[:, 0:2 * P].rearrange("p (k t) -> p k t", k=2)[:, :, 0:r],
                                            ext_hi[:, k, :, 0:r].bitcast(F32), ALU.subtract).then_inc(lo_saved, 1)

                def gate(n, k, r):
                    dve.wait_ge(logit_ps, n + 1)
                    nc.vector.tensor_tensor(logit[0:r, k, :], LB[0:r, 0:NE], gate_b[0:r, :], ALU.add)
                    dve.drain()
                    nc.vector.max(top[0:r, k, :], logit[0:r, k, :])
                    dve.drain()
                    nc.vector.max_index(topi[0:r, k, :], top[0:r, k, :], logit[0:r, k, :])
                    dve.drain()
                    nc.vector.tensor_copy(topf[0:r, k:k + 1], topi[0:r, k, 0:1])
                    dve.drain()
                    nc.vector.tensor_scalar(hot[0:r, k, :], iota8[0:r, :], topf[0:r, k:k + 1], None, ALU.is_equal).then_inc(hot_done, 1)

                def pick(p, n, k, r, e):
                    if e == 0:
                        if not isinstance(p, int) or p > 0:
                            dve.wait_ge(e_out[k], 16 * p)
                    else:
                        dve.wait_ge(acc_step, 9 * n + e + (e >= 4))
                    dve.wait_ge(expert_ps, 4 * n + e // 2 + 1)
                    nc.vector.scalar_tensor_tensor(out=acc[0:r, k, :], in0=EBK[e // 2][0:r, (e % 2) * D:(e % 2 + 1) * D],
                                                   scalar=hot[0:r, k, e:e + 1], in1=(acc if e else eh)[0:r, k, :],
                                                   op0=ALU.mult, op1=ALU.add).then_inc(acc_step, 1)

                def add_bias(n, k, r):
                    dve.wait_ge(acc_step, 9 * n + 4)
                    dve.wait_ge(bias_ps, n + 1)
                    nc.vector.tensor_tensor(acc[0:r, k, :], BB[0:r, 0:D], acc[0:r, k, :], ALU.add).then_inc(acc_step, 1)

                def step(p, n, k, r, nxt):
                    if nxt:
                        stats(nxt[0], 1 - k, nxt[1])
                    pick(p, n, k, r, 0)
                    pick(p, n, k, r, 1)
                    if nxt:
                        normalise(n + 1, 1 - k, nxt[1])
                    pick(p, n, k, r, 2)
                    pick(p, n, k, r, 3)
                    if nxt:
                        split(n + 1, 1 - k, nxt[1])
                    add_bias(n, k, r)
                    pick(p, n, k, r, 4)
                    pick(p, n, k, r, 5)
                    if nxt:
                        gate(n + 1, 1 - k, nxt[1])
                    pick(p, n, k, r, 6)
                    pick(p, n, k, r, 7)

                nc.vector.tensor_copy(bias_hi[:, :], moe_b[:, :]).then_inc(bias_split, 1)
                dve.wait_ge(bias_split, 1)
                nc.vector.tensor_tensor(bias_lo[:, :], moe_b[:, :], bias_hi[:, :].bitcast(F32), ALU.subtract).then_inc(bias_split, 1)
                stats(0, 0, P)
                normalise(0, 0, P)
                split(0, 0, P)
                gate(0, 0, P)
                step(0, 0, 0, P, (0, P))
                with dve.Fori(1, NB) as p:
                    step(p - 1, 2 * p - 1, 1, P, (p, P))
                    step(p, 2 * p, 0, P, (p, P))
                step(NB - 1, 2 * NB - 1, 1, P, (NB, LAST))
                step(NB, 2 * NB, 0, LAST, None)

            @block.tensor
            def _(pe):
                mm = nc.tensor.matmul

                def turn_x(n, k, r):
                    pe.wait_ge(e_xn, n + 1)
                    for kk in range(2):
                        last = nc.tensor.transpose(XB[:, kk * P:kk * P + r], exn[0:r, k, kk * P:(kk + 1) * P], ident[0:r, 0:r])
                    last.then_inc(ext_ps, 1)

                def logits(n, k, r):
                    pe.wait_ge(hi_saved, n + 1)
                    pe.wait_ge(lo_saved, n + 1)
                    terms = [(x, g, kk) for x in (ext_hi, ext_lo) for g in gate for kk in range(2)]
                    for t, (x, g, kk) in enumerate(terms):
                        last = mm(LB[0:r, 0:NE], x[:, k, kk, 0:r], g[:, kk, :], start=(t == 0), stop=(t == 7))
                    last.then_inc(logit_ps, 1)

                def turn_hot(n, k, r):
                    pe.wait_ge(hot_done, n + 1)
                    nc.tensor.transpose(HB[0:NE, 0:r], hot[0:r, k, :], ident[0:r, 0:r]).then_inc(hot_ps, 1)

                def bias(n, k, r):
                    pe.wait_ge(hot_saved, n + 1)
                    if not isinstance(n, int) or n > 0:
                        pe.wait_ge(acc_step, 9 * (n - 1) + 5)
                    mm(BB[0:r, 0:D], hotT[:, k, 0:r], bias_hi[:, :], start=True, stop=False)
                    mm(BB[0:r, 0:D], hotT[:, k, 0:r], bias_lo[:, :], start=False, stop=True).then_inc(bias_ps, 1)

                def experts(n, k, r, q):
                    if not isinstance(n, int) or n > 0:
                        pe.wait_ge(acc_step, 9 * (n - 1) + (2, 4, 7, 9)[q])
                    terms = [(x, g, kk) for x, g in ((ext_hi, moe_hi), (ext_hi, moe_lo), (ext_lo, moe_hi)) for kk in range(2)]
                    for t, (x, g, kk) in enumerate(terms):
                        last = mm(EBK[q][0:r, :], x[:, k, kk, 0:r], g[:, kk, 2 * q:2 * q + 2, :], start=(t == 0), stop=(t == 5))
                    last.then_inc(expert_ps, 1)

                def step(n, k, r, nxt):
                    experts(n, k, r, 0)
                    turn_hot(n, k, r)
                    experts(n, k, r, 1)
                    bias(n, k, r)
                    if nxt:
                        turn_x(n + 1, 1 - k, nxt)
                    experts(n, k, r, 2)
                    if nxt:
                        logits(n + 1, 1 - k, nxt)
                    experts(n, k, r, 3)

                turn_x(0, 0, P)
                logits(0, 0, P)
                pe.wait_ge(moe_in, 32)
                pe.wait_ge(bias_split, 2)
                step(0, 0, P, P)
                with pe.Fori(1, NB) as i:
                    step(2 * i - 1, 1, P, P)
                    step(2 * i, 0, P, P)
                step(2 * NB - 1, 1, P, LAST)
                step(2 * NB, 0, LAST, None)


def kernel(**inputs):
    import numpy as np
    import concourse.bacc as bacc
    from concourse.bass_utils import run_bass_kernel_spmd

    f32 = np.float32

    def tiles(a):
        return a.reshape(-1, P, a.shape[1]).transpose(1, 0, 2)

    g = {n: np.asarray(a) for n, a in inputs.items()}
    x = g["x"].reshape(B, 3, 14, 16, 14, 16).transpose(0, 1, 3, 5, 2, 4).reshape(TOK_BLOCKS, P, FK, P)
    wkT = g["L0_attn_Wk"].T.reshape(D, NKV, 1, HD)
    heads = lambda a: a.transpose(1, 0, 2).reshape(D, D)
    ew = g["L1_ffn_expert_w"]
    weights = {
        "wtok": tiles(g["L0_tok_W"]),
        "wq": tiles(g["L0_attn_Wq"].T), "wk": tiles(np.concatenate([wkT, wkT], 2).reshape(D, 2 * NKV * HD)),
        "wv": tiles(g["L0_attn_Wv"].T), "wo": tiles(g["L0_attn_Wo"].T),
        "u1": tiles(np.concatenate([g["L0_ffn_U1"]] * 2, 1)), "v1": np.concatenate([g["L0_ffn_V1"]] * 2, 0),
        "b1": g["L0_ffn_b1"].reshape(MF, P).T, "u2": tiles(g["L0_ffn_U2"]),
        "v2": np.concatenate([g["L0_ffn_V2"]] * 2, 0), "b2": np.broadcast_to(g["L0_ffn_b2"], (P, D)),
        "rwq": tiles(heads(g["L1_attn_Wq"])), "rwk": tiles(heads(g["L1_attn_Wk"])), "rwv": tiles(heads(g["L1_attn_Wv"])),
        "gnw": g["L1_attn_gn_weight"].reshape(2, P).T, "gnb": g["L1_attn_gn_bias"].reshape(2, P).T,
        "wout": tiles(g["L1_attn_Wout"]), "gate_w": tiles(g["L1_ffn_gate_w"]),
        "gate_b": np.broadcast_to(g["L1_ffn_gate_b"], (P, NE)),
        "ewT": ew.transpose(0, 2, 1).reshape(NE, 4, P, D).transpose(0, 2, 1, 3),
        "ebT": tiles(g["L1_ffn_expert_b"].T), "ow": tiles(g["L1_ffn_out_w"]),
        "ob": np.broadcast_to(g["L1_ffn_out_b"], (NE, D)),
    }

    p, q = np.arange(P)[:, None], np.arange(P)[None, :]
    tri = (q >= p).astype(f32)
    window = (p > np.arange(TW)[None, :]).astype(f32)
    tail = (np.arange(TW)[None, :] >= np.arange(CH[2][1])[:, None]).astype(f32)
    gamma = np.array([1.0 - 2.0 ** (-5 - i // 2) for i in range(NH)])
    chan = np.arange(D)
    power = gamma[chan // 16][:, None] ** np.arange(SP)[None, :]
    parity = (chan // 16 % 2)[:, None, None] == np.arange(2)[None, :, None]
    dec_q = power[:, None, :] * parity / 4.0
    dec_kt = (1.0 / power)[:, 0:2 * P].T.reshape(2, P, D).transpose(1, 0, 2)
    tables = {
        "iota8": np.broadcast_to(np.arange(NE, dtype=f32), (P, NE)), "ident": np.eye(P, dtype=f32),
        "lower": -(p >= 64).astype(f32), "half": np.full((P, 3), -0.5, f32), "eps": np.full((P, 3), EPS, f32),
        "pmask": np.concatenate([tri, np.ones((P, P), f32), window, tri], 1), "tmask": tail, "tri": tri,
        "blockdiag": (p // 16 == q // 16).astype(f32), "headavg": (p // 16 == q // 16).astype(f32) / 16,
        "dec_q": dec_q.reshape(2, P, 2, SP).transpose(1, 0, 2, 3), "dec_k": tiles(1.0 / power), "dec_kt": dec_kt,
    }

    nc = bacc.Bacc("TRN2", target_bir_lowering=False, num_devices=1)
    arrays = {}

    def give(name, a):
        a = np.ascontiguousarray(a)
        arrays[name] = a
        return nc.dram_tensor(name, a.shape, mybir.dt.from_np(a.dtype), kind="ExternalInput").ap()

    xT = give("patches", x.transpose(0, 3, 2, 1))
    txt = give("txt_rows", g["txt"].reshape(B * TXT_TOK, D))
    flat = ("wtok", "wq", "wk", "wv", "wo", "u1", "v1", "rwq", "rwk", "rwv", "gate_w")
    w = {n: give(f"w_{n}", a.reshape(P, -1) if n in flat else a) for n, a in weights.items()}
    consts = {n: give(f"c_{n}", a.astype(f32)) for n, a in tables.items()}
    out = nc.dram_tensor("out_rows", (B * S, D), F32, kind="ExternalOutput").ap()
    build(nc, xT, txt, consts, w, out)
    r = run_bass_kernel_spmd(nc, [arrays], core_ids=[0])
    return np.asarray(r.results[0]["out_rows"]).reshape(B, S, D)
```
